# Optimizing a Trainium2 kernel written in Bass

```python
import numpy as np
import jax
import jax.numpy as jnp

def _softmax(x, axis=-1):
    return jax.nn.softmax(x, axis=axis)

def _gelu(x):
    return jax.nn.gelu(x, approximate=True)

def _silu(x):
    return jax.nn.silu(x)

def _sigmoid(x):
    return jax.nn.sigmoid(x)

def _layernorm(x, axis=-1, eps=1e-05):
    m = jnp.mean(x, axis=axis, keepdims=True)
    v = jnp.var(x, axis=axis, keepdims=True)
    return (x - m) / jnp.sqrt(v + eps)

def _scatter_add(tgt, idx, src, axis=0):
    return tgt.at[idx].add(src)

def _segment_sum(src, seg, n):
    return jax.ops.segment_sum(src, seg, n)
kernel_name = 'mk_gnn_ffn_d1_gnn_r8_75477e'

def setup_inputs(seed: int=0):
    np.random.seed(seed)
    _w = jnp.asarray

    def _rec_inputs():
        import jax
        import jax.numpy as jnp
        _gk = jax.random.key(seed)
        x = -0.0002117 + 1 * jax.random.normal(jax.random.fold_in(_gk, 1), (12500, 256), jnp.float32)
        _s = jax.random.randint(jax.random.fold_in(_gk, 2), (100000,), 0, 12500, jnp.int32)
        _d = jax.random.randint(jax.random.fold_in(_gk, 3), (100000,), 0, 12500, jnp.int32)
        _loop = jnp.arange(12500, dtype=jnp.int32)
        src = jnp.concatenate([_s, _d, _loop])
        dst = jnp.concatenate([_d, _s, _loop])
        _o = jnp.argsort(dst, stable=True)
        src = src[_o]
        dst = dst[_o]
        return (x, src, dst)
    x, src, dst = _rec_inputs()

    def _L0_gnn_setup():
        import jax, jax.numpy as jnp
        import numpy as np
        N = 12500
        E = 100000
        F_IN = 256
        HID = 64
        H = 4
        NEG_SLOPE = 0.2
        BN_EPS = 1e-05

        def _add_self_loops(edge_index, n):
            loop = jnp.arange(n, dtype=edge_index.dtype)
            src = jnp.concatenate([edge_index[0], loop])
            dst = jnp.concatenate([edge_index[1], loop])
            return (src, dst)

        def _batch_norm(x, g, b):
            m = x.mean(0)
            v = x.var(0)
            return g * (x - m) * jax.lax.rsqrt(v + BN_EPS) + b

        def _gcn_conv(x, src, dst, W, b, n):
            deg = jax.ops.segment_sum(jnp.ones_like(dst, jnp.float32), dst, n)
            dinv = jax.lax.rsqrt(jnp.maximum(deg, 1.0))
            norm = dinv[src] * dinv[dst]
            h = x @ W
            out = jax.ops.segment_sum(h[src] * norm[:, None], dst, n)
            return out + b

        def _gat_conv(x, src, dst, W, a_src, a_dst, b, n):
            h = (x @ W).reshape(n, H, HID)
            alpha_s = jnp.einsum('nhc,hc->nh', h, a_src)
            alpha_d = jnp.einsum('nhc,hc->nh', h, a_dst)
            e = alpha_s[src] + alpha_d[dst]
            e = jnp.where(e > 0, e, NEG_SLOPE * e)
            emax = jax.ops.segment_max(e, dst, n)
            w = jnp.exp(e - emax[dst])
            wsum = jax.ops.segment_sum(w, dst, n)
            att = w / wsum[dst]
            out = jax.ops.segment_sum(att[:, :, None] * h[src], dst, n)
            return out.reshape(n, H * HID) + b
        key = jax.random.key(seed)
        ks = jax.random.split(key, 20)
        s = 0.05
        return {'x': jax.random.normal(ks[0], (N, F_IN), jnp.float32), 'edge_index': jax.random.randint(ks[1], (2, E), 0, N, jnp.int64), 'W_gcn': jax.random.normal(ks[2], (F_IN, HID), jnp.float32) * s, 'b_gcn': jnp.zeros((HID,), jnp.float32), 'g0': jnp.ones((HID,), jnp.float32), 'beta0': jnp.zeros((HID,), jnp.float32), 'W1': jax.random.normal(ks[3], (HID, H * HID), jnp.float32) * s, 'a_src1': jax.random.normal(ks[4], (H, HID), jnp.float32) * s, 'a_dst1': jax.random.normal(ks[5], (H, HID), jnp.float32) * s, 'b1': jnp.zeros((H * HID,), jnp.float32), 'g1': jnp.ones((H * HID,), jnp.float32), 'beta1': jnp.zeros((H * HID,), jnp.float32), 'W2': jax.random.normal(ks[6], (H * HID, H * HID), jnp.float32) * s, 'a_src2': jax.random.normal(ks[7], (H, HID), jnp.float32) * s, 'a_dst2': jax.random.normal(ks[8], (H, HID), jnp.float32) * s, 'b2': jnp.zeros((H * HID,), jnp.float32), 'g2': jnp.ones((H * HID,), jnp.float32), 'beta2': jnp.zeros((H * HID,), jnp.float32)}
    _L0_gnn_all = _L0_gnn_setup()
    _L0_gnn_in = {k: v for k, v in _L0_gnn_all.items() if k in ('W_gcn', 'b_gcn', 'g0', 'beta0', 'W1', 'a_src1', 'a_dst1', 'b1', 'g1', 'beta1', 'W2', 'a_src2', 'a_dst2', 'b2', 'g2', 'beta2')}
    del _L0_gnn_all

    def _L0_ffn_setup():
        import jax, jax.numpy as jnp
        import numpy as np
        E = 8
        K = 2
        D = 256
        H = 512
        DOUT = 256
        EPS = 1e-05
        key = jax.random.key(seed)
        ks = jax.random.split(key, 9)
        s = 0.02
        return {'x': jax.random.normal(ks[0], (4, 1024, D), jnp.float32), 'gamma': 1.0 + 0.05 * jax.random.normal(ks[1], (D,), jnp.float32), 'beta': 0.05 * jax.random.normal(ks[2], (D,), jnp.float32), 'Wr': 0.01 * jax.random.normal(ks[3], (D, E), jnp.float32), 'br': jnp.zeros((E,), jnp.float32), 'W1': s * jax.random.normal(ks[4], (E, D, H), jnp.float32), 'b1': s * jax.random.normal(ks[5], (E, H), jnp.float32), 'W2': s * jax.random.normal(ks[6], (E, H, DOUT), jnp.float32), 'b2': s * jax.random.normal(ks[7], (E, DOUT), jnp.float32)}
    _L0_ffn_all = _L0_ffn_setup()
    _L0_ffn_in = {k: v for k, v in _L0_ffn_all.items() if k in ('gamma', 'beta', 'Wr', 'br', 'W1', 'b1', 'W2', 'b2')}
    del _L0_ffn_all
    return {'x': x, 'src': src, 'dst': dst, 'L0_gnn_W_gcn': _L0_gnn_in['W_gcn'], 'L0_gnn_b_gcn': _L0_gnn_in['b_gcn'], 'L0_gnn_g0': _L0_gnn_in['g0'], 'L0_gnn_beta0': _L0_gnn_in['beta0'], 'L0_gnn_W1': _L0_gnn_in['W1'], 'L0_gnn_a_src1': _L0_gnn_in['a_src1'], 'L0_gnn_a_dst1': _L0_gnn_in['a_dst1'], 'L0_gnn_b1': _L0_gnn_in['b1'], 'L0_gnn_g1': _L0_gnn_in['g1'], 'L0_gnn_beta1': _L0_gnn_in['beta1'], 'L0_gnn_W2': _L0_gnn_in['W2'], 'L0_gnn_a_src2': _L0_gnn_in['a_src2'], 'L0_gnn_a_dst2': _L0_gnn_in['a_dst2'], 'L0_gnn_b2': _L0_gnn_in['b2'], 'L0_gnn_g2': _L0_gnn_in['g2'], 'L0_gnn_beta2': _L0_gnn_in['beta2'], 'L0_ffn_gamma': _L0_ffn_in['gamma'], 'L0_ffn_beta': _L0_ffn_in['beta'], 'L0_ffn_Wr': _L0_ffn_in['Wr'], 'L0_ffn_br': _L0_ffn_in['br'], 'L0_ffn_W1': _L0_ffn_in['W1'], 'L0_ffn_b1': _L0_ffn_in['b1'], 'L0_ffn_W2': _L0_ffn_in['W2'], 'L0_ffn_b2': _L0_ffn_in['b2']}

def reference(x, src, dst, L0_gnn_W_gcn, L0_gnn_b_gcn, L0_gnn_g0, L0_gnn_beta0, L0_gnn_W1, L0_gnn_a_src1, L0_gnn_a_dst1, L0_gnn_b1, L0_gnn_g1, L0_gnn_beta1, L0_gnn_W2, L0_gnn_a_src2, L0_gnn_a_dst2, L0_gnn_b2, L0_gnn_g2, L0_gnn_beta2, L0_ffn_gamma, L0_ffn_beta, L0_ffn_Wr, L0_ffn_br, L0_ffn_W1, L0_ffn_b1, L0_ffn_W2, L0_ffn_b2):
    import jax
    import jax.numpy as jnp

    def _L0_gnn_ref(x, edge_index, W_gcn, b_gcn, g0, beta0, W1, a_src1, a_dst1, b1, g1, beta1, W2, a_src2, a_dst2, b2, g2, beta2):
        import jax, jax.numpy as jnp
        import numpy as np
        N = 12500
        E = 100000
        F_IN = 256
        HID = 64
        H = 4
        NEG_SLOPE = 0.2
        BN_EPS = 1e-05

        def _add_self_loops(edge_index, n):
            loop = jnp.arange(n, dtype=edge_index.dtype)
            src = jnp.concatenate([edge_index[0], loop])
            dst = jnp.concatenate([edge_index[1], loop])
            return (src, dst)

        def _batch_norm(x, g, b):
            m = x.mean(0)
            v = x.var(0)
            return g * (x - m) * jax.lax.rsqrt(v + BN_EPS) + b

        def _gcn_conv(x, src, dst, W, b, n):
            deg = jax.ops.segment_sum(jnp.ones_like(dst, jnp.float32), dst, n)
            dinv = jax.lax.rsqrt(jnp.maximum(deg, 1.0))
            norm = dinv[src] * dinv[dst]
            h = x @ W
            out = jax.ops.segment_sum(h[src] * norm[:, None], dst, n)
            return out + b

        def _gat_conv(x, src, dst, W, a_src, a_dst, b, n):
            h = (x @ W).reshape(n, H, HID)
            alpha_s = jnp.einsum('nhc,hc->nh', h, a_src)
            alpha_d = jnp.einsum('nhc,hc->nh', h, a_dst)
            e = alpha_s[src] + alpha_d[dst]
            e = jnp.where(e > 0, e, NEG_SLOPE * e)
            emax = jax.ops.segment_max(e, dst, n)
            w = jnp.exp(e - emax[dst])
            wsum = jax.ops.segment_sum(w, dst, n)
            att = w / wsum[dst]
            out = jax.ops.segment_sum(att[:, :, None] * h[src], dst, n)
            return out.reshape(n, H * HID) + b
        n = x.shape[0]
        src, dst = _add_self_loops(edge_index, n)
        h = jax.nn.relu(_gcn_conv(x, src, dst, W_gcn, b_gcn, n))
        h = _batch_norm(h, g0, beta0)
        h = _gat_conv(h, src, dst, W1, a_src1, a_dst1, b1, n)
        h = jax.nn.elu(_batch_norm(h, g1, beta1))
        h = _gat_conv(h, src, dst, W2, a_src2, a_dst2, b2, n)
        h = jax.nn.elu(_batch_norm(h, g2, beta2))
        return h

    def _L0_ffn_ref(x, gamma, beta, Wr, br, W1, b1, W2, b2):
        import jax, jax.numpy as jnp
        import numpy as np
        E = 8
        K = 2
        D = 256
        H = 512
        DOUT = 256
        EPS = 1e-05
        mu = jnp.mean(x, axis=-1, keepdims=True)
        var = jnp.mean(jnp.square(x - mu), axis=-1, keepdims=True)
        xn = (x - mu) * jax.lax.rsqrt(var + EPS) * gamma + beta
        logits = jnp.einsum('bsd,de->bse', xn, Wr) + br
        top_vals, top_idx = jax.lax.top_k(logits, K)
        w = jax.nn.softmax(top_vals, axis=-1)
        w_full = jnp.einsum('bsk,bske->bse', w, jax.nn.one_hot(top_idx, E, dtype=w.dtype))
        y = jnp.zeros(x.shape[:-1] + (DOUT,), x.dtype)
        for e in range(E):
            h = jax.nn.gelu(jnp.einsum('bsd,dh->bsh', xn, W1[e]) + b1[e], approximate=False)
            y_e = jnp.einsum('bsh,hd->bsd', h, W2[e]) + b2[e]
            y = y + y_e * w_full[..., e, None]
        return y
    edge_index = jnp.stack([src, dst])
    x = x + _L0_gnn_ref(_layernorm(x, axis=-1), edge_index, L0_gnn_W_gcn, L0_gnn_b_gcn, L0_gnn_g0, L0_gnn_beta0, L0_gnn_W1, L0_gnn_a_src1, L0_gnn_a_dst1, L0_gnn_b1, L0_gnn_g1, L0_gnn_beta1, L0_gnn_W2, L0_gnn_a_src2, L0_gnn_a_dst2, L0_gnn_b2, L0_gnn_g2, L0_gnn_beta2)
    x = x + _L0_ffn_ref(_layernorm(x, axis=-1)[None], L0_ffn_gamma, L0_ffn_beta, L0_ffn_Wr, L0_ffn_br, L0_ffn_W1, L0_ffn_b1, L0_ffn_W2, L0_ffn_b2)[0]
    return x

_drawn_inputs = setup_inputs


def setup_inputs(seed=0):
    import zlib

    import numpy as np

    out = dict(_drawn_inputs(seed))
    spreads = {'L0_gnn_b_gcn': (0.0, 0.1),
     'L0_gnn_g0': (1.0, 0.2),
     'L0_gnn_beta0': (0.0, 0.8),
     'L0_gnn_b1': (0.0, 0.8),
     'L0_gnn_g1': (1.0, 0.2),
     'L0_gnn_beta1': (0.0, 0.34),
     'L0_gnn_b2': (0.0, 0.8),
     'L0_gnn_g2': (1.0, 0.2),
     'L0_gnn_beta2': (0.0, 0.1),
     'L0_ffn_br': (0.0, 0.1)}
    factors = {'L0_gnn_a_dst1': 3.574,
     'L0_ffn_gamma': 7.572,
     'L0_ffn_beta': 6.531,
     'L0_ffn_b1': 8.0,
     'L0_ffn_b2': 5.432}
    for name, (base, spread) in spreads.items():
        noise = np.random.default_rng([zlib.crc32(name.encode()), seed]).standard_normal(out[name].shape)
        drawn = base * np.exp(spread * noise) if base else spread * noise
        out[name] = jnp.asarray(drawn.astype(out[name].dtype))
    for name, factor in factors.items():
        out[name] = (out[name] * factor).astype(out[name].dtype)
    return out
```

```python
from contextlib import ExitStack

import concourse.bass as bass
from concourse import mybir

P = 128
F32 = mybir.dt.float32
BF16 = mybir.dt.bfloat16
I32 = mybir.dt.int32
U32 = mybir.dt.uint32
ALU = mybir.AluOpType
ACT = mybir.ActivationFunctionType
AX = mybir.AxisListType.X
MAX = bass.bass_isa.ReduceOp.max

HEADS, HID = 4, 64
FEAT = HEADS * HID
ROW = FEAT + HEADS
WIDE = FEAT + 2 * HEADS
CH = 4
GE = CH * P
RING = 4
SLOPE = 0.2
EPS = 1e-5
SAFE = 60.0
NOWHERE = -1.0e6


class Chain:

    def __init__(self, eng, sem, start=0):
        self.eng, self.sem, self.start, self.n = eng, sem, start, 0

    def __call__(self, ins):
        ins.then_inc(self.sem, 1)
        self.n += 1
        self.eng.wait_ge(self.sem, self.start + self.n)


def pace(eng, n, steps, ring=2):
    leads = [lead for _, lead in steps]
    low, high = -max(leads), n - min(leads)
    first = -(-(ring + max(0, -min(leads))) // ring)
    last = (n - max(leads)) // ring

    def turn(i, c, known):
        for fn, lead in steps:
            if not known or 0 <= ring * i + c + lead < n:
                fn(i, c + lead)

    first, last = (first, last) if last - first >= 2 else (n, n)
    for t in range(low, min(first * ring, high)):
        turn(t // ring, t % ring, True)
    if first < n:
        with eng.Fori(first, last) as i:
            for c in range(ring):
                turn(i, c, False)
        for t in range(last * ring, high):
            turn(t // ring, t % ring, True)


class Mem:

    taken = []

    def __init__(self, nc, ctx, stage=""):
        self.nc, self.ctx, self.stage = nc, ctx, stage

    def sb(self, name, shape, dt=F32):
        return self.ctx.enter_context(self.nc.sbuf_tensor(self.stage + name, shape, dt))

    def ps(self, name, shape=(P, 512), dt=F32):
        return self.ctx.enter_context(self.nc.psum_tensor(self.stage + name, list(shape), dt))

    def sem(self, name):
        handle = self.nc.alloc_semaphore(name=name)
        Mem.taken.append(handle)
        return handle

    @staticmethod
    def clear_signals(nc):
        nc.clear_and_free_semaphores(Mem.taken)
        nc.all_engine_barrier()
        Mem.taken = []


class Shapes:
    def __init__(self, n, e, experts, hidden):
        self.N, self.E = n, e
        self.NW = -(-n // P)
        self.TAIL = n - (self.NW - 1) * P
        self.NWP = -(-(self.NW + 1) // 4) * 4
        self.NG = -(-e // GE)
        self.LAST = e - (self.NG - 1) * GE
        self.NT = -(-self.NG // P)
        self.GT = self.NG // self.NT
        self.WB = next(b for b in (14, 7, 4, 2) if self.NW % b == 0)
        self.NB = self.NW // self.WB
        self.EX, self.HD = experts, hidden
        assert self.NG % 4 == 0 and self.GT * self.NT == self.NG and self.NW % 2 == 0


def wait(eng, sem, count):
    if not isinstance(count, int) or count > 0:
        eng.wait_ge(sem, count)


def spread_of(dve, link, st, mean, var):
    link(dve.tensor_tensor(var, st[:, :, 1], st[:, :, 4], ALU.subtract))
    link(dve.tensor_tensor(mean, st[:, :, 1], st[:, :, 4], ALU.add))
    link(dve.tensor_scalar(mean, mean, 0.5, None, ALU.mult))
    link(dve.scalar_tensor_tensor(out=var, in0=var, scalar=0.25, in1=var, op0=ALU.mult, op1=ALU.mult))
    link(dve.scalar_tensor_tensor(out=var, in0=st[:, :, 2], scalar=1.0 / FEAT, in1=var, op0=ALU.mult,
                                  op1=ALU.add))
    link(dve.scalar_tensor_tensor(out=var, in0=st[:, :, 5], scalar=1.0 / FEAT, in1=var, op0=ALU.mult,
                                  op1=ALU.add))


def one(n):
    return bass.ds(n, 1)


def at1(t, n):
    return t[:, bass.ds(n, 1), :].squeeze(1)


def build_constants(nc, M, K):
    ident = M.sb("ident", [P, P])
    ones = M.sb("ones", [P, P])
    zeros = M.sb("zeros", [P, WIDE])
    count_i = M.sb("count_i", [P, P], I32)
    count = M.sb("count", [P, P])
    part_i = M.sb("part_i", [P, 1], I32)
    part = M.sb("part", [P, 1])
    eps = M.sb("eps", [P, 1])
    K.update(ident=ident, ones=ones, zeros=zeros, count=count, part=part, eps=eps)
    filled, counted = M.sem("const_filled"), M.sem("const_counted")
    with nc.Block() as block:
        @block.gpsimd
        def _(pool):
            pool.memset(ident[:, :], 0.0).then_inc(filled, 1)
            pool.wait_ge(filled, 1)
            pool.affine_select(out=ident[:, :], in_=ident[:, :], compare_op=ALU.not_equal, fill=1.0, base=0,
                               pattern=[[-1, P]], channel_multiplier=1)
            pool.iota(count_i[:, :], pattern=[[1, P]], base=0, channel_multiplier=0)
            pool.iota(part_i[:, :], pattern=[[1, 1]], base=0, channel_multiplier=1).then_inc(counted, 1)

        @block.vector
        def _(dve):
            dve.memset(ones[:, :], 1.0)
            dve.memset(zeros[:, :], 0.0)
            dve.memset(eps[:, :], EPS)
            dve.wait_ge(counted, 1)
            dve.tensor_copy(count[:, :], count_i[:, :])
            dve.tensor_copy(part[:, :], part_i[:, :])


def build_edge_tables(nc, M, K, S, src, dst, mod_rows):
    N, E, NG, NT, GT, LAST = S.N, S.E, S.NG, S.NT, S.GT, S.LAST
    src_t = M.sb("src_t", [P, NG, CH], I32)
    mod_t = M.sb("mod_t", [P, NG, CH])
    win_t = M.sb("win_t", [P, NG, CH])
    first_w = M.sb("first_w", [P, NG], I32)
    in_first = M.sb("in_first", [P, NG])
    in_next = M.sb("in_next", [P, NG])
    spread_ok = M.sb("spread_ok", [1, 1], I32)
    K.update(src_t=src_t, mod_t=mod_t, win_t=win_t, first_w=first_w, in_first=in_first, in_next=in_next,
             spread_ok=spread_ok)
    loaded_d, loaded_s, filled = M.sem("edge_dst_loaded"), M.sem("edge_src_loaded"), M.sem("edge_filled")
    step, rows_ready, padded = M.sem("edge_step"), M.sem("edge_rows_ready"), M.sem("edge_padded")
    stored, turned, taken = M.sem("edge_mod_stored"), M.sem("edge_turned"), M.sem("edge_taken")
    spread_max, spread_in = M.sem("edge_spread_max"), M.sem("edge_spread_in")
    with ExitStack() as scope:
        T = Mem(nc, scope)
        raw_d = T.sb("raw_d", [GT, NT, GE], I32)
        raw_s = T.sb("raw_s", [GT, NT, GE], I32)
        win_i = T.sb("win_i", [GT, NT, GE], I32)
        mod_i = T.sb("mod_i", [GT, NT, GE], I32)
        flat = K["feat"][0:GT, :, :].rearrange("p w f -> p (w f)")
        f_dst, f_src, f_win = [flat[:, n * NT * GE:(n + 1) * NT * GE].rearrange("p (t e) -> p t e", t=NT)
                               for n in range(3)]
        f_mod = T.sb("f_mod", [GT, NT, GE])
        b_mod = T.sb("b_mod", [GT, NT, GE], BF16)
        least = T.sb("least", [GT, NT])
        most = T.sb("most", [GT, NT])
        least_i = T.sb("least_i", [GT, NT], I32)
        lw_i = T.sb("lw_i", [GT, NT], I32)
        lm_i = T.sb("lm_i", [GT, NT], I32)
        lw = T.sb("lw", [GT, NT])
        lm = T.sb("lm", [GT, NT])
        wide = T.sb("wide", [GT, 1])
        widest = T.sb("widest", [GT, 1])
        spread1 = T.sb("spread1", [1, 1])
        lwb = T.sb("lwb", [GT, NT, P])
        lmb = T.sb("lmb", [GT, NT, P])
        nowhere = T.sb("nowhere", [1, GE])
        turn = [T.ps(f"turn{i}") for i in range(2)]

        def rows(x, t, full):
            return x[t * GT * GE:(t * GT + full) * GE].rearrange("(g e) -> g e", e=GE)

        @nc_block(nc)
        def _(block):
            @block.sync
            def _(sp):
                for raw, x, got in ((raw_d, dst, loaded_d), (raw_s, src, loaded_s)):
                    if raw is raw_s:
                        sp.wait_ge(filled, 1)
                    for t in range(NT):
                        full = GT if t < NT - 1 else GT - 1
                        if full:
                            sp.dma_start(raw[0:full, t, :], rows(x, t, full)).then_inc(got, 16)
                    tail = x[(NG - 1) * GE:E].rearrange("(a e) -> a e", a=1)
                    sp.dma_start(raw[GT - 1:GT, NT - 1, 0:LAST], tail).then_inc(got, 16)
                if LAST < GE:
                    before = dst[(NG - 1) * GE - (GE - LAST):(NG - 1) * GE].rearrange("(a e) -> a e", a=1)
                    sp.dma_start(raw_d[GT - 1:GT, NT - 1, LAST:GE], before).then_inc(loaded_d, 16)
                sp.wait_ge(rows_ready, 1)
                for t in range(NT):
                    sp.dma_start(mod_rows[t * GT:(t + 1) * GT, :], b_mod[:, t, :]).then_inc(stored, 16)
                if LAST < GE:
                    sp.dma_start(f_mod[GT - 1:GT, NT - 1, LAST:GE], nowhere[0:1, LAST:GE]).then_inc(padded, 16)
                sp.wait_ge(stored, 16 * NT)

            @block.gpsimd
            def _(pool):
                pool.memset(raw_s[:, NT - 1, :], 0).then_inc(filled, 1)
                pool.wait_ge(spread_in, 1)
                pool.partition_all_reduce(widest[:, :], wide[:, :], GT, MAX).then_inc(spread_max, 1)

            @block.vector
            def _(dve):
                link = Chain(dve, step)
                dve.memset(nowhere[:, :], NOWHERE)
                dve.wait_ge(loaded_d, 16 * (NT - (GT == 1) + 1 + (LAST < GE)))
                dve.tensor_scalar(win_i[:, :, :], raw_d[:, :, :], 7, None, ALU.logical_shift_right)
                dve.tensor_scalar(mod_i[:, :, :], raw_d[:, :, :], P - 1, None, ALU.bitwise_and)
                link(dve.tensor_copy(f_dst[:, :, :], raw_d[:, :, :]))
                dve.tensor_copy(f_win[:, :, :], win_i[:, :, :])
                dve.tensor_copy(f_mod[:, :, :], mod_i[:, :, :])
                dve.tensor_copy(b_mod[:, :, :], mod_i[:, :, :]).then_inc(rows_ready, 1)
                dve.tensor_reduce(least[:, :], f_dst[:, :, :], AX, ALU.min)
                link(dve.tensor_reduce(most[:, :], f_dst[:, :, :], AX, ALU.max))
                dve.tensor_copy(least_i[:, :], least[:, :])
                link(dve.tensor_tensor(most[:, :], most[:, :], least[:, :], ALU.subtract))
                dve.tensor_reduce(wide[:, :], most[:, :], AX, ALU.max).then_inc(spread_in, 1)
                dve.tensor_scalar(lw_i[:, :], least_i[:, :], 7, None, ALU.logical_shift_right)
                link(dve.tensor_scalar(lm_i[:, :], least_i[:, :], P - 1, None, ALU.bitwise_and))
                dve.tensor_copy(lw[:, :], lw_i[:, :])
                link(dve.tensor_copy(lm[:, :], lm_i[:, :]))
                dve.tensor_copy(lwb[:, :, :], lw[:, :].unsqueeze(2).to_broadcast([GT, NT, P]))
                dve.tensor_copy(lmb[:, :, :], lm[:, :].unsqueeze(2).to_broadcast([GT, NT, P]))
                dve.wait_ge(loaded_s, 16 * (NT - (GT == 1) + 1))
                dve.tensor_copy(f_src[:, :, :], raw_s[:, :, :]).then_inc(rows_ready, 1)
                dve.wait_ge(spread_max, 1)
                dve.tensor_scalar(spread1[:, :], widest[0:1, :], float(P - 1), None, ALU.is_le).then_inc(rows_ready, 1)
                dve.wait_ge(rows_ready, 3)
                dve.tensor_copy(spread_ok[:, :], spread1[:, :])
                n = 0
                for t in range(NT):
                    g = slice(t * GT, (t + 1) * GT)
                    for f, out in ((f_src, src_t), (f_win, win_t), (f_mod, mod_t)):
                        dve.wait_ge(turned, n + 1)
                        v = turn[n % 2][:, 0:CH * GT].rearrange("p (c g) -> p g c", c=CH)
                        dve.tensor_copy(out[:, g, :], v).then_inc(taken, 1)
                        n += 1
                    dve.wait_ge(turned, n + 1)
                    lo, hi = turn[n % 2][:, 0:GT], turn[n % 2][:, P:P + GT]
                    dve.tensor_copy(first_w[:, g], lo)
                    dve.tensor_scalar(in_first[:, g], hi, K["part"][:, 0:1], None, ALU.is_le)
                    dve.tensor_scalar(in_next[:, g], hi, K["part"][:, 0:1], None, ALU.is_gt).then_inc(taken, 1)
                    n += 1

            @block.tensor
            def _(pe):
                n = 0
                pe.wait_ge(rows_ready, 3)
                if LAST < GE:
                    pe.wait_ge(padded, 16)
                for t in range(NT):
                    for f in (f_src, f_win, f_mod):
                        if n >= 2:
                            pe.wait_ge(taken, n - 1)
                        for c in range(CH):
                            mm = pe.transpose(turn[n % 2][:, c * GT:(c + 1) * GT], f[:, t, c * P:(c + 1) * P],
                                              K["ident"][0:GT, 0:GT])
                        mm.then_inc(turned, 1)
                        n += 1
                    if n >= 2:
                        pe.wait_ge(taken, n - 1)
                    pe.matmul(turn[n % 2][:, 0:GT], lwb[:, t, :], K["ident"][0:GT, 0:GT], start=True, stop=True)
                    pe.matmul(turn[n % 2][:, P:P + GT], lmb[:, t, :], K["ident"][0:GT, 0:GT],
                              start=True, stop=True).then_inc(turned, 1)
                    n += 1


def nc_block(nc):
    def run(body):
        with nc.Block() as block:
            body(block)
    return run


def build_degrees(nc, M, K, S):
    NG, NW = S.NG, S.NW
    dinv = M.sb("dinv", [P, NW])
    K["dinv"] = dinv
    built, used, done, step = M.sem("deg_built"), M.sem("deg_used"), M.sem("deg_done"), M.sem("deg_step")
    root = M.sem("deg_root")
    Q = 4 * CH
    with ExitStack() as scope:
        T = Mem(nc, scope)
        cb = T.sb("deg_count", [P, P], BF16)
        mb = T.sb("deg_mod", [P, NG * CH], BF16)
        wb = T.sb("deg_win", [P, NG * CH], BF16)
        hot_m = T.sb("hot_m", [P, 2, Q, P], BF16)
        hot_w = T.sb("hot_w", [P, 2, Q, NW], BF16)
        zb = T.sb("deg_zero", [P, P], BF16)
        deg = T.sb("deg", [P, NW])
        acc = T.ps("deg_ps")

        @nc_block(nc)
        def _(block):
            @block.vector
            def _(dve):
                link = Chain(dve, step)
                dve.memset(zb[:, :], 0.0).then_inc(built, 1)
                dve.tensor_copy(cb[:, :], K["count"][:, :])
                dve.tensor_copy(mb[:, :], K["mod_t"][:, :, :].rearrange("p g c -> p (g c)"))
                link(dve.tensor_copy(wb[:, :], K["win_t"][:, :, :].rearrange("p g c -> p (g c)")))

                def hots(i, b):
                    t = 2 * i + b
                    at = bass.ds(t * Q, Q)
                    wait(dve, used, t - 1)
                    dve.tensor_tensor(hot_m[:, b, :, :], cb[:, :].unsqueeze(1).to_broadcast([P, Q, P]),
                                      mb[:, at].unsqueeze(2).to_broadcast([P, Q, P]), ALU.is_equal)
                    dve.tensor_tensor(hot_w[:, b, :, :], cb[:, 0:NW].unsqueeze(1).to_broadcast([P, Q, NW]),
                                      wb[:, at].unsqueeze(2).to_broadcast([P, Q, NW]),
                                      ALU.is_equal).then_inc(built, 1)

                hots(0, 0)
                hots(0, 1)
                with dve.Fori(1, NG // 8) as i:
                    hots(i, 0)
                    hots(i, 1)
                dve.wait_ge(done, 1)
                link(dve.tensor_scalar(deg[:, :], acc[:, 0:NW], 1.0, 1.0, ALU.add, ALU.max))
                dve.wait_ge(root, 1)
                dve.reciprocal(dinv[:, :], deg[:, :])

            @block.scalar
            def _(act):
                act.wait_ge(step, 2)
                act.activation(deg[:, :], deg[:, :], ACT.Sqrt).then_inc(root, 1)

            @block.tensor
            def _(pe):
                pe.wait_ge(built, 1)
                pe.matmul(acc[:, 0:NW], zb[:, :], zb[:, 0:NW], start=True, stop=False)
                with pe.Fori(0, NG // 8) as i:
                    for b in range(2):
                        pe.wait_ge(built, 2 * i + b + 2)
                        for q in range(Q):
                            mm = pe.matmul(acc[:, 0:NW], hot_m[:, b, q, :], hot_w[:, b, q, :], start=False,
                                           stop=False)
                        mm.then_inc(used, 1)
                pe.matmul(acc[:, 0:NW], zb[:, :], zb[:, 0:NW], start=False,
                          stop=True).then_inc(done, 1)


def build_gcn_input(nc, M, K, S, x, W_gcn, table):
    N, NW, NWP, TAIL, WB, NB = S.N, S.NW, S.NWP, S.TAIL, S.WB, S.NB
    feat = K["feat"]
    cleared, w_in, step = M.sem("gi_cleared"), M.sem("gi_weights"), M.sem("gi_step")
    x_in = [M.sem(f"gi_x{b}") for b in range(NB)]
    rooted, scaled = M.sem("gi_rooted"), M.sem("gi_scaled")
    staged, turned, copied = M.sem("gi_staged"), M.sem("gi_turned"), M.sem("gi_copied")
    product, placed, stored = M.sem("gi_product"), M.sem("gi_placed"), M.sem("gi_stored")
    with ExitStack() as scope:
        T = Mem(nc, scope)
        wg = T.sb("w_gcn", [P, 2, HID])
        st = T.sb("gi_st", [P, NW, 6])
        mean, var = T.sb("gi_mean", [P, NW]), T.sb("gi_var", [P, NW])
        std = T.sb("gi_std", [P, NW])
        rstd = T.sb("gi_rstd", [P, NW])
        stage = T.sb("gi_stage", [P, 2, FEAT])
        xt = T.sb("gi_xt", [P, 2, FEAT])
        ps_t = [T.ps(f"gi_pt{i}") for i in range(2)]
        ps_o = [T.ps(f"gi_po{i}") for i in range(2)]

        @nc_block(nc)
        def _(block):
            @block.sync
            def _(sp):
                sp.wait_ge(cleared, 1)
                for b in range(NB):
                    w0, w1 = b * WB, min((b + 1) * WB, NW - 1)
                    sp.dma_start(feat[:, w0:w1, 0:FEAT],
                                 x[w0 * P:w1 * P, :].rearrange("(w p) f -> p w f", p=P)).then_inc(x_in[b], 16)
                sp.dma_start(feat[0:TAIL, NW - 1, 0:FEAT], x[(NW - 1) * P:N, :]).then_inc(x_in[NB - 1], 16)
                sp.dma_start(wg[:, :, :], W_gcn.rearrange("(k p) f -> p k f", p=P)).then_inc(w_in, 16)
                for b in range(NB):
                    sp.wait_ge(placed, (b + 1) * WB)
                    rows = table[b * WB * P:(b + 1) * WB * P, :].rearrange("(w p) f -> p w f", p=P)
                    sp.dma_start(rows, feat[:, b * WB:(b + 1) * WB, 0:HID]).then_inc(stored, 16)
                sp.wait_ge(stored, 16 * NB)

            @block.vector
            def _(dve):
                dve.memset(feat[:, NW - 1:NWP, :], 0.0).then_inc(cleared, 1)
                link = Chain(dve, step)
                for b in range(NB):
                    dve.wait_ge(x_in[b], 16 * (1 + (b == NB - 1)))
                    with dve.Fori(b * WB, (b + 1) * WB) as w:
                        dve.bn_stats(at1(st, w), feat[:, one(w), 0:FEAT].squeeze(1)).then_inc(scaled, 1)
                dve.wait_ge(scaled, NW)
                spread_of(dve, link, st, mean[:, :], var[:, :])
                dve.wait_ge(rooted, 1)
                link(dve.reciprocal(rstd[:, :], std[:, :]))

                def put(i, c):
                    w, slot = 2 * i + c, c % 2
                    wait(dve, turned, w - 1)
                    dve.tensor_scalar(stage[:, slot, :], feat[:, bass.ds(w, 1), 0:FEAT].squeeze(1),
                                      mean[:, one(w)], rstd[:, bass.ds(w, 1)],
                                      ALU.subtract, ALU.mult).then_inc(staged, 1)

                def take(i, c):
                    w, slot = 2 * i + c, c % 2
                    dve.wait_ge(product, w + 1)
                    dve.wait_ge(staged, w + 1)
                    dve.tensor_scalar(feat[:, bass.ds(w, 1), 0:HID].squeeze(1), ps_o[slot][:, 0:HID],
                                      K["dinv"][:, bass.ds(w, 1)], None, ALU.mult).then_inc(placed, 1)

                pace(dve, NW, [(put, 2), (take, 0)])

            @block.scalar
            def _(act):
                act.wait_ge(step, 6)
                act.activation(std[:, :], var[:, :], ACT.Sqrt, bias=K["eps"][:, 0:1]).then_inc(rooted, 1)

                def copy(i, c):
                    w, slot = 2 * i + c, c % 2
                    act.wait_ge(turned, w + 1)
                    wait(act, product, w - 1)
                    act.copy(xt[:, slot, :], ps_t[slot][:, 0:FEAT]).then_inc(copied, 1)

                pace(act, NW, [(copy, 0)])

            @block.tensor
            def _(pe):
                pe.wait_ge(w_in, 16)
                linear(pe, K, S, (2, P), stage, ps_t, xt, ps_o, wg, HID, staged, turned, copied, product, placed)


def linear(pe, K, S, parts, stage, ps_t, xt, ps_o, weights, width, staged, turned, copied, product, placed):
    def turn(i, c):
        w, slot = 2 * i + c, c % 2
        pe.wait_ge(staged, w + 1)
        wait(pe, copied, w - 1)
        for k in range(parts[0]):
            mm = pe.transpose(ps_t[slot][:, k * P:k * P + P], stage[:, slot, k * P:k * P + P], K["ident"][:, :])
        mm.then_inc(turned, 1)

    def multiply(i, c):
        w, slot = 2 * i + c, c % 2
        pe.wait_ge(copied, w + 1)
        wait(pe, placed, w - 1)
        for k in range(parts[0]):
            mm = pe.matmul(ps_o[slot][:, 0:width], xt[0:parts[1], slot, k * P:k * P + P], weights[0:parts[1], k, 0:width],
                           start=(k == 0), stop=(k == parts[0] - 1))
        mm.then_inc(product, 1)

    pace(pe, S.NW, [(turn, 1), (multiply, 0)])


def edge_buffers(T, width, gat):
    B = dict(idx=T.sb("idx", [P, RING, CH], I32), rows=T.sb("rows", [P, RING, CH, width]),
             hot=T.sb("hot", [P, RING, CH, P]), ps_sum=[T.ps(f"ps_sum{i}") for i in range(2)])
    if gat:
        B.update(mod=T.sb("mod", [P, RING, GE], BF16), hot_t=T.sb("hot_t", [P, RING, GE], BF16),
                 tab=T.sb("tab", [P, RING, 2, 24], BF16), near=T.sb("near", [P, 2, CH, 2 * HEADS]),
                 logit=T.sb("logit", [P, 2, CH, HEADS]), msg=T.sb("msg", [P, 2, CH, ROW]),
                 ps_near=[T.ps(f"ps_near{i}") for i in range(2)])
    return B


def fast_edges(L, M, K, S, B, table, mod_rows, width, gat):
    NG = S.NG
    feat = K["feat"]
    idx_staged, begun = M.sem(L + "idx_staged"), M.sem(L + "begun")
    rows_in = [M.sem(f"{L}rows_in{j}") for j in range(RING)]
    hot_built, summed, added = M.sem(L + "hot_built"), M.sem(L + "summed"), M.sem(L + "added")
    if gat:
        mod_in = [M.sem(f"{L}mod_in{j}") for j in range(RING)]
        tab_staged, near_made = M.sem(L + "tab_staged"), M.sem(L + "near_made")
        logit_step, weighed, msg_made = M.sem(L + "logit_step"), M.sem(L + "weighed"), M.sem(L + "msg_made")
    rows_used = msg_made if gat else summed

    def gather(pool):
        def group(i, c):
            g = RING * i + c
            pool.wait_ge(idx_staged, g + 1)
            wait(pool, rows_used, g - 3)
            pool.sem_inc(begun, 1)
            for k in range(CH):
                pool.indirect_dma_start(B["rows"][:, c, k, :], None, table,
                                        bass.IndirectOffsetOnAxis(ap=B["idx"][:, c, k:k + 1], axis=0)
                                        ).then_inc(rows_in[c], 16)
        pace(pool, NG, [(group, 0)], RING)

    def send_mods(sp):
        def group(i, c):
            g = RING * i + c
            wait(sp, hot_built, g - 3)
            sp.dma_start(B["mod"][:, c, :], mod_rows[one(g), :].to_broadcast([P, GE])).then_inc(mod_in[c], 16)
        pace(sp, NG, [(group, 0)], RING)

    def act_program(act):
        regs = [act.alloc_register(f"{L}act_w{j}") for j in range(RING)]

        def stage(i, c):
            j, g = c % RING, RING * i + c
            wait(act, rows_in[j], 64 * (i + c // RING))
            act.copy(B["idx"][:, j, :], at1(K["src_t"], g)).then_inc(idx_staged, 1)
            if not gat:
                return
            wait(act, near_made, g - 3)
            if j == 0:
                act.load(regs, K["first_w"][0:1, bass.ds(g, RING)])
            w = act.snap(regs[j], min_val=0, max_val=S.NW - 1)
            for side, mask in enumerate(("in_first", "in_next")):
                ins = act.activation(B["tab"][:, j, side, :], K["tab24"][:, bass.ds(w + side, 1), :].squeeze(1),
                                     ACT.Copy, scale=K[mask][:, one(g)])
            ins.then_inc(tab_staged, 1)

        def weigh(i, c):
            g = RING * i + c
            act.wait_ge(logit_step, 4 * g + 4)
            wait(act, summed, g - 1)
            act.activation(B["msg"][:, c % 2, :, FEAT:ROW], B["logit"][:, c % 2, :, :], ACT.Exp).then_inc(weighed, 1)

        pace(act, NG, [(weigh, 2), (stage, RING + 2)] if gat else [(stage, RING)], RING)

    def pe_program(pe):
        def look(i, c):
            j, g, b = c % RING, RING * i + c, c % 2
            pe.wait_ge(hot_built, g + 1)
            pe.wait_ge(tab_staged, g + 1)
            wait(pe, logit_step, 4 * (g - 2) + 1)
            for k in range(CH):
                for side in range(2):
                    mm = pe.matmul(B["ps_near"][b][:, 24 * k:24 * k + 24], B["hot_t"][:, j, k * P:(k + 1) * P],
                                   B["tab"][:, j, side, :], start=(side == 0), stop=(side == 1))
            mm.then_inc(near_made, 1)

        def total(i, c):
            j, g, b = c % RING, RING * i + c, c % 2
            if gat:
                pe.wait_ge(msg_made, g + 1)
            else:
                pe.wait_ge(hot_built, g + 1)
                pe.wait_ge(rows_in[j], 64 * (i + c // RING + 1))
            wait(pe, added, g - 1)
            for k in range(CH):
                rhs = B["msg"][:, b, k, :] if gat else B["rows"][:, j, k, :]
                mm = pe.matmul(B["ps_sum"][b][:, 0:width], B["hot"][:, j, k, :], rhs, start=(k == 0),
                               stop=(k == CH - 1))
            mm.then_inc(summed, 1)

        pace(pe, NG, [(total, 1), (look, 3)] if gat else [(total, 0)], RING)

    def dve_program(dve):
        regs = [dve.alloc_register(f"{L}dve_w{j}") for j in range(RING)]

        def add(i, c):
            g, b = RING * i + c, c % 2
            if c % RING == 0:
                dve.load(regs, K["first_w"][0:1, bass.ds(g, RING)])
            w = dve.snap(regs[c % RING], min_val=0, max_val=S.NW - 1)
            dve.wait_ge(summed, g + 1)
            wait(dve, added, g)
            for side, mask in enumerate(("in_first", "in_next")):
                to = feat[:, bass.ds(w + side, 1), 0:width].squeeze(1)
                ins = dve.scalar_tensor_tensor(out=to, in0=B["ps_sum"][b][:, 0:width],
                                               scalar=K[mask][:, one(g)], in1=to, op0=ALU.mult,
                                               op1=ALU.add)
            ins.then_inc(added, 1)

        def hots(i, c):
            j, g = c % RING, RING * i + c
            wait(dve, summed, g - 3)
            if gat:
                wait(dve, near_made, g - 3)
                dve.wait_ge(mod_in[j], 16 * (i + c // RING + 1))
                dve.tensor_scalar(B["hot_t"][:, j, :], B["mod"][:, j, :], K["part"][:, 0:1], None, ALU.is_equal)
            dve.tensor_tensor(B["hot"][:, j, :, :], K["count"][:, :].unsqueeze(1).to_broadcast([P, CH, P]),
                              at1(K["mod_t"], g).unsqueeze(2).to_broadcast([P, CH, P]),
                              ALU.is_equal).then_inc(hot_built, 1)

        def logits(i, c):
            j, g, b = c % RING, RING * i + c, c % 2
            near, logit = B["near"][:, b, :, :], B["logit"][:, b, :, :]
            dve.wait_ge(near_made, g + 1)
            link = Chain(dve, logit_step, 4 * g)
            link(dve.tensor_reduce(near, B["ps_near"][b][:, 0:24 * CH].rearrange("p (c v s) -> p c v s", c=CH, s=3),
                                   AX, ALU.add))
            dve.wait_ge(rows_in[j], 64 * (i + c // RING + 1))
            link(dve.tensor_tensor(logit, B["rows"][:, j, :, FEAT:ROW], near[:, :, 0:HEADS], ALU.add))
            link(dve.scalar_tensor_tensor(out=logit, in0=logit, scalar=SLOPE, in1=logit, op0=ALU.mult, op1=ALU.max))
            dve.tensor_tensor(logit, logit, near[:, :, HEADS:2 * HEADS], ALU.subtract).then_inc(logit_step, 1)

        def messages(i, c):
            j, g, b = c % RING, RING * i + c, c % 2
            dve.wait_ge(weighed, g + 1)
            rows = B["rows"][:, j, :, 0:FEAT].rearrange("p c (h f) -> p c h f", h=HEADS)
            out = B["msg"][:, b, :, 0:FEAT].rearrange("p c (h f) -> p c h f", h=HEADS)
            w = B["msg"][:, b, :, FEAT:ROW].unsqueeze(3).to_broadcast([P, CH, HEADS, HID])
            dve.tensor_tensor(out, rows, w, ALU.mult).then_inc(msg_made, 1)

        steps = [(messages, 1), (add, -1), (logits, 2), (hots, 3)] if gat else [(add, 0), (hots, 3)]
        pace(dve, NG, steps, RING)

    return dict(gather=gather, send_mods=send_mods, act=act_program, pe=pe_program, dve=dve_program)


def general_buffers(T, gat):
    G = dict(rel=T.sb("rel", [P, CH]), win=T.sb("win_now", [P, 1]))
    if gat:
        G.update(relb=T.sb("relb", [P, CH, P]), hot_t=T.sb("hot_tf", [P, GE]), ps_rel=T.ps("ps_rel"),
                 ps_as=T.ps("ps_as"), asb=T.sb("asb", [P, CH, P]), top=T.sb("top", [P, 1]),
                 masked=T.sb("masked", [P, GE]))
    return G


def any_edges(L, M, K, S, B, G, table, width, gat, maxima=False):
    NG, NW = S.NG, S.NW
    feat = K["feat"]
    names = ("step", "rows_in", "spread", "looked", "weighed", "summed", "window", "begun")
    step, rows_in, spread, looked, weighed, summed, window, begun = [M.sem(L + "any_" + n) for n in names]
    STEPS = 5 + 4 * HEADS if maxima else 11 if gat else 4
    rel, win = G["rel"], G["win"]

    def pairs(eng, body):
        with eng.Fori(0, NW) as w:
            with eng.Fori(0, NG) as g:
                body(w, g, w * NG + g)

    def gather(pool):
        def pair(w, g, n):
            pool.wait_ge(step, STEPS * n + 2)
            pool.sem_inc(begun, 1)
            for k in range(CH):
                pool.indirect_dma_start(B["rows"][:, 0, k, :], None, table,
                                        bass.IndirectOffsetOnAxis(ap=B["idx"][:, 0, k:k + 1], axis=0)
                                        ).then_inc(rows_in, 16)
        pairs(pool, pair)

    def act_program(act):
        def pair(w, g, n):
            act.wait_ge(step, STEPS * n + 9)
            act.activation(B["msg"][:, 0, :, FEAT:ROW], B["logit"][:, 0, :, :], ACT.Exp).then_inc(weighed, 1)
        if gat and not maxima:
            pairs(act, pair)

    def pe_program(pe):
        def row_of(ps, cols):
            for k in range(CH):
                mm = pe.matmul(ps[:, k * P:(k + 1) * P], cols[:, k, :], K["ident"][:, :], start=True, stop=True)
            return mm

        def pair(w, g, n):
            if gat:
                pe.wait_ge(step, STEPS * n + 3)
                row_of(G["ps_rel"], G["relb"]).then_inc(spread, 1)
            if maxima:
                for h in range(HEADS):
                    pe.wait_ge(step, STEPS * n + (6 + 4 * h))
                    row_of(G["ps_as"], G["asb"]).then_inc(looked, 1)
                return
            if gat:
                pe.wait_ge(step, STEPS * n + 5)
                for k in range(CH):
                    mm = pe.matmul(B["ps_near"][0][:, 8 * k:8 * k + 8], G["hot_t"][:, k * P:(k + 1) * P],
                                   at1(K["near_tab"], w), start=True, stop=True)
                mm.then_inc(looked, 1)
            pe.wait_ge(step, STEPS * n + (STEPS - 1))
            pe.wait_ge(rows_in, 64 * n + 64)
            for k in range(CH):
                rhs = B["msg"][:, 0, k, :] if gat else B["rows"][:, 0, k, :]
                mm = pe.matmul(B["ps_sum"][0][:, 0:width], B["hot"][:, 0, k, :], rhs, start=(k == 0),
                               stop=(k == CH - 1))
            mm.then_inc(summed, 1)
        pairs(pe, pair)

    def dve_program(dve):
        count = K["count"][:, :].unsqueeze(1).to_broadcast([P, CH, P])
        relc = rel[:, :].unsqueeze(2).to_broadcast([P, CH, P])

        def largest(link, w, n):
            link(dve.tensor_scalar(G["hot_t"][:, :], G["ps_rel"][:, :], K["part"][:, 0:1], None, ALU.is_equal))
            link(dve.tensor_scalar(G["hot_t"][:, :], G["hot_t"][:, :], 1.0, 1.0e30, ALU.subtract, ALU.mult))
            dve.wait_ge(rows_in, 64 * n + 64)
            for h in range(HEADS):
                a_s = B["rows"][:, 0, :, FEAT + h:FEAT + h + 1].to_broadcast([P, CH, P])
                link(dve.tensor_copy(G["asb"][:, :, :], a_s))
                dve.wait_ge(looked, HEADS * n + (h + 1))
                link(dve.tensor_tensor(G["masked"][:, :], G["ps_as"][:, :], G["hot_t"][:, :], ALU.add))
                link(dve.tensor_reduce(G["top"][:, :], G["masked"][:, :], AX, ALU.max))
                to = K["shift_src"][:, one(w), h:h + 1].squeeze(1)
                link(dve.tensor_tensor(to, to, G["top"][:, :], ALU.max))

        def sums(link, w, n):
            link(dve.tensor_tensor(B["hot"][:, 0, :, :], count, relc, ALU.is_equal))
            if gat:
                near = B["ps_near"][0][:, 0:8 * CH].rearrange("p (c v) -> p c v", c=CH)
                logit = B["logit"][:, 0, :, :]
                dve.wait_ge(spread, n + 1)
                link(dve.tensor_scalar(G["hot_t"][:, :], G["ps_rel"][:, :], K["part"][:, 0:1], None,
                                       ALU.is_equal))
                dve.wait_ge(looked, n + 1)
                dve.wait_ge(rows_in, 64 * n + 64)
                link(dve.tensor_tensor(logit, B["rows"][:, 0, :, FEAT:ROW], near[:, :, 0:HEADS], ALU.add))
                link(dve.scalar_tensor_tensor(out=logit, in0=logit, scalar=SLOPE, in1=logit, op0=ALU.mult,
                                              op1=ALU.max))
                link(dve.tensor_tensor(logit, logit, near[:, :, HEADS:2 * HEADS], ALU.subtract))
                link(dve.tensor_scalar(logit, logit, 0.0, None, ALU.min))
                dve.wait_ge(weighed, n + 1)
                out = B["msg"][:, 0, :, 0:FEAT].rearrange("p c (h f) -> p c h f", h=HEADS)
                rows = B["rows"][:, 0, :, 0:FEAT].rearrange("p c (h f) -> p c h f", h=HEADS)
                link(dve.tensor_tensor(out, rows, B["msg"][:, 0, :, FEAT:ROW].unsqueeze(3).to_broadcast(
                    [P, CH, HEADS, HID]), ALU.mult))
            dve.wait_ge(summed, n + 1)
            to = feat[:, one(w), 0:width].squeeze(1)
            link(dve.tensor_tensor(to, to, B["ps_sum"][0][:, 0:width], ALU.add))

        dve.memset(win[:, :], -1.0).then_inc(window, 1)
        with dve.Fori(0, NW) as w:
            dve.wait_ge(window, w + 1)
            dve.tensor_scalar(win[:, :], win[:, :], 1.0, None, ALU.add).then_inc(window, 1)
            with dve.Fori(0, NG) as g:
                n = w * NG + g
                link = Chain(dve, step, STEPS * n)
                dve.wait_ge(window, w + 2)
                dve.tensor_copy(B["idx"][:, 0, :], at1(K["src_t"], g))
                link(dve.tensor_scalar(rel[:, :], at1(K["win_t"], g), win[:, 0:1], float(P), ALU.subtract,
                                       ALU.mult))
                link(dve.tensor_tensor(rel[:, :], rel[:, :], at1(K["mod_t"], g), ALU.add))
                if gat:
                    link(dve.tensor_copy(G["relb"][:, :, :], relc))
                if maxima:
                    dve.wait_ge(spread, n + 1)
                    largest(link, w, n)
                else:
                    sums(link, w, n)

    return dict(gather=gather, act=act_program, pe=pe_program, dve=dve_program)


def build_edges(nc, L, M, K, S, table, mod_rows, width, gat, flag):
    with ExitStack() as scope:
        T = Mem(nc, scope, L)
        B = edge_buffers(T, width, gat)
        G = general_buffers(T, gat)
        fast = fast_edges(L, M, K, S, B, table, mod_rows, width, gat)
        slow = any_edges(L, M, K, S, B, G, table, width, gat)

        def either(eng, one_way, other_way):
            ok = eng.value_load(flag[0:1, 0:1], min_val=0, max_val=1)
            with eng.If(ok != 0):
                one_way(eng)
            if other_way:
                with eng.Else():
                    other_way(eng)

        with nc.Block() as block:
            @block.gpsimd
            def _(pool):
                either(pool, fast["gather"], slow["gather"])

            @block.scalar
            def _(act):
                either(act, fast["act"], slow["act"] if gat else None)

            @block.tensor
            def _(pe):
                either(pe, fast["pe"], slow["pe"])

            @block.vector
            def _(dve):
                either(dve, fast["dve"], slow["dve"])

            if gat:
                @block.sync
                def _(sp):
                    either(sp, fast["send_mods"], None)


def build_attention(nc, L, M, K, S, table):
    NW, NWP, NG = S.NW, S.NWP, S.NG
    feat = K["feat"]
    step, ranged, all_max, selfed = M.sem(L + "att_step"), M.sem(L + "att_ranged"), M.sem(L + "att_max"), M.sem(L + "att_self")
    shift, near = K["shift_src"], K["near_tab"]
    flag = M.sb(L + "flag", [1, 1], I32)
    a_s = feat[:, :, FEAT:ROW]
    a_d = feat[:, :, ROW:WIDE]
    with ExitStack() as scope:
        T = Mem(nc, scope, L + "att_")
        own = T.sb("own_range", [P, 2 * HEADS])
        all_ = T.sb("all_range", [P, 2 * HEADS])
        least = T.sb("least_as", [P, HEADS])
        span = T.sb("span", [P, HEADS])
        widest = T.sb("widest_span", [P, 1])
        okf = T.sb("ok_f", [1, 2])

        with nc.Block() as block:
            @block.gpsimd
            def _(pool):
                pool.wait_ge(ranged, 1)
                pool.partition_all_reduce(all_[:, :], own[:, :], P, MAX).then_inc(all_max, 1)

            @block.vector
            def _(dve):
                link = Chain(dve, step)
                by_head = feat[:, 0:NW, FEAT:ROW].rearrange("p w h -> p h w")
                dve.tensor_reduce(own[:, 0:HEADS], by_head, AX, ALU.max)
                link(dve.tensor_reduce(least[:, :], by_head, AX, ALU.min))
                dve.tensor_scalar(own[:, HEADS:2 * HEADS], least[:, :], -1.0, None, ALU.mult).then_inc(ranged, 1)
                dve.wait_ge(all_max, 1)
                dve.tensor_copy(shift[:, :, :], all_[:, 0:HEADS].unsqueeze(1).to_broadcast([P, NWP, HEADS]))
                link(dve.tensor_tensor(span[:, :], all_[:, 0:HEADS], all_[:, HEADS:2 * HEADS], ALU.add))
                dve.tensor_copy(okf[:, 1:2], K["spread_ok"][:, :])
                link(dve.tensor_reduce(widest[:, :], span[:, :], AX, ALU.max))
                link(dve.tensor_scalar(okf[:, 0:1], widest[0:1, :], SAFE, None, ALU.is_le))
                dve.tensor_tensor(flag[:, :], okf[:, 0:1], okf[:, 1:2], ALU.mult)

    with ExitStack() as scope:
        T = Mem(nc, scope, L + "att_")
        B = dict(idx=T.sb("idx", [P, 1, CH], I32), rows=T.sb("rows", [P, 1, CH, ROW]))
        G = general_buffers(T, True)
        own_max = any_edges(L + "max_", M, K, S, B, G, table, ROW, True, maxima=True)
        begun = M.sem(L + "att_begun")

        def unless_flag(eng, program):
            ok = eng.value_load(flag[0:1, 0:1], min_val=0, max_val=1)
            with eng.If(ok == 0):
                program(eng)

        with nc.Block() as block:
            @block.gpsimd
            def _(pool):
                unless_flag(pool, own_max["gather"])

            @block.tensor
            def _(pe):
                unless_flag(pe, own_max["pe"])

            @block.vector
            def _(dve):
                def program(dve):
                    dve.tensor_copy(shift[:, 0:NW, :], feat[:, 0:NW, FEAT:ROW]).then_inc(begun, 1)
                    dve.wait_ge(begun, 1)
                    own_max["dve"](dve)
                unless_flag(dve, program)

    with ExitStack() as scope:
        T = Mem(nc, scope, L + "att_")
        own_l = T.sb("own_logit", [P, NWP, HEADS])
        own_w = T.sb("own_weight", [P, NWP, HEADS])
        rest = T.sb("tab_rest", [P, NWP, 2 * HEADS])
        part = K["tab24"][:, :, :].rearrange("p w (v s) -> p w v s", s=3)
        with nc.Block() as block:
            @block.scalar
            def _(act):
                act.wait_ge(step, 9)
                act.activation(own_w[:, :, :], own_l[:, :, :], ACT.Exp).then_inc(selfed, 1)

            @block.vector
            def _(dve):
                link = Chain(dve, step, 4)
                hi = near[:, :, HEADS:2 * HEADS]
                dve.tensor_copy(near[:, :, 0:HEADS], a_d)
                dve.tensor_tensor(hi, a_d, shift[:, :, :], ALU.add)
                link(dve.tensor_tensor(own_l[:, :, :], a_s, a_d, ALU.add))
                link(dve.scalar_tensor_tensor(out=hi, in0=hi, scalar=SLOPE, in1=hi, op0=ALU.mult, op1=ALU.max))
                link(dve.scalar_tensor_tensor(out=own_l[:, :, :], in0=own_l[:, :, :], scalar=SLOPE,
                                              in1=own_l[:, :, :], op0=ALU.mult, op1=ALU.max))
                link(dve.tensor_tensor(own_l[:, :, :], own_l[:, :, :], hi, ALU.subtract))
                link(dve.tensor_scalar(own_l[:, :, :], own_l[:, :, :], 0.0, None, ALU.min))
                link(dve.tensor_copy(part[:, :, :, 0], near[:, :, :]))
                link(dve.tensor_tensor(rest[:, :, :], near[:, :, :], part[:, :, :, 0], ALU.subtract))
                link(dve.tensor_copy(part[:, :, :, 1], rest[:, :, :]))
                link(dve.tensor_tensor(rest[:, :, :], rest[:, :, :], part[:, :, :, 1], ALU.subtract))
                link(dve.tensor_copy(part[:, :, :, 2], rest[:, :, :]))
                dve.wait_ge(selfed, 1)
                body = feat[:, 0:NW, 0:FEAT].rearrange("p w (h f) -> p w h f", h=HEADS)
                dve.tensor_tensor(body, body, own_w[:, 0:NW, :].unsqueeze(3).to_broadcast([P, NW, HEADS, HID]),
                                  ALU.mult)
                dve.tensor_copy(a_s, own_w[:, :, :])
    return flag


def build_batch_norm(nc, L, M, K, S, F, bias, gamma, beta, gat):
    N, NW, WB, NB, TAIL = S.N, S.NW, S.WB, S.NB, S.TAIL
    feat = K["feat"]
    params, rec_made, step = M.sem(L + "bn_params"), M.sem(L + "bn_rec"), M.sem(L + "bn_step")
    shaped, meaned, centred = M.sem(L + "bn_shaped"), M.sem(L + "bn_meaned"), M.sem(L + "bn_centred")
    squared, used, varied, rooted = (M.sem(L + "bn_squared"), M.sem(L + "bn_used"), M.sem(L + "bn_varied"),
                                     M.sem(L + "bn_rooted"))
    scale, offset = K["bn_scale"], K["bn_offset"]
    with ExitStack() as scope:
        T = Mem(nc, scope, L)
        bias_b = T.sb("bias_b", [P, F])
        mean = T.sb("mean", [P, F])
        std = T.sb("std", [P, F])
        rec = T.sb("rec", [P, NW, HEADS])
        square = T.sb("square", [P, 2, WB, F])
        ps_m, ps_v = T.ps("ps_mean"), T.ps("ps_var")

        def batch(b, lo=0, hi=F):
            return feat[:, bass.ds(b * WB, WB), lo:hi]

        def nodes_sum(pe, ps, source, ready, done):
            pe.matmul(ps[:, 0:F], K["zeros"][:, 0:P], K["zeros"][:, 0:F], start=True, stop=False)

            def windows(b, upto, static):
                pe.wait_ge(ready, b + 1)
                for j in range(upto):
                    mm = pe.matmul(ps[:, 0:F], K["ones"][:, :], source(b, j), start=False, stop=False)
                return mm
            with pe.Fori(0, NB - 1) as b:
                mm = windows(b, WB, False)
                if done is not None:
                    mm.then_inc(done, 1)
            windows(NB - 1, WB - 1, True)
            return pe.matmul(ps[:, 0:F], K["ones"][0:TAIL, :], source(NB - 1, WB - 1)[0:TAIL], start=False, stop=True)

        with nc.Block() as block:
            @block.sync
            def _(sp):
                for to, x in ((bias_b, bias), (scale, gamma), (offset, beta)):
                    sp.dma_start(to[:, 0:F], x.rearrange("(a f) -> a f", a=1).to_broadcast([P, F])
                                 ).then_inc(params, 16)

            @block.vector
            def _(dve):
                link = Chain(dve, step)
                dve.wait_ge(params, 48)
                if gat:
                    link(dve.reciprocal(rec[:, :, :], feat[:, 0:NW, FEAT:ROW]))
                else:
                    link(dve.memset(rec[:, 0, :], 0.0))
                K_ = 2 if gat else 3
                with dve.Fori(0, NB) as b:
                    chain = Chain(dve, step, 1 + K_ * b)
                    if gat:
                        v = batch(b).rearrange("p w (h f) -> p w h f", h=HEADS)
                        chain(dve.tensor_tensor(v, v, rec[:, bass.ds(b * WB, WB), :].unsqueeze(3).to_broadcast(
                            [P, WB, HEADS, HID]), ALU.mult))
                    else:
                        chain(dve.tensor_tensor(batch(b), batch(b), K["dinv"][:, bass.ds(b * WB, WB)].unsqueeze(
                            2).to_broadcast([P, WB, F]), ALU.mult))
                    chain(dve.tensor_tensor(batch(b), batch(b), bias_b[:, :].unsqueeze(1).to_broadcast([P, WB, F]),
                                            ALU.add))
                    if not gat:
                        chain(dve.tensor_scalar(batch(b), batch(b), 0.0, None, ALU.max))
                    dve.sem_inc(shaped, 1)
                base = 1 + K_ * NB
                link = Chain(dve, step, base)
                dve.wait_ge(meaned, 1)
                link(dve.tensor_scalar(mean[:, :], ps_m[:, 0:F], 1.0 / N, None, ALU.mult))
                with dve.Fori(0, NB) as b:
                    dve.tensor_tensor(batch(b), batch(b), mean[:, :].unsqueeze(1).to_broadcast([P, WB, F]),
                                      ALU.subtract).then_inc(centred, 1)
                dve.wait_ge(rooted, 1)
                link(dve.reciprocal(std[:, :], std[:, :]))
                dve.tensor_tensor(scale[:, 0:F], scale[:, 0:F], std[:, :], ALU.mult)

            @block.scalar
            def _(act):
                def squares(i, c):
                    b = 2 * i + c
                    act.wait_ge(centred, b + 1)
                    wait(act, used, b - 1)
                    act.activation(square[:, c % 2, :, :], batch(b), ACT.Square).then_inc(squared, 1)
                pace(act, NB, [(squares, 0)])
                act.wait_ge(varied, 1)
                act.activation(std[:, :], ps_v[:, 0:F], ACT.Sqrt, scale=1.0 / N, bias=K["eps"][:, 0:1]
                               ).then_inc(rooted, 1)

            @block.tensor
            def _(pe):
                nodes_sum(pe, ps_m, lambda b, j: feat[:, one(b * WB + j), 0:F].squeeze(1), shaped, None
                          ).then_inc(meaned, 1)
                pe.matmul(ps_v[:, 0:F], K["zeros"][:, 0:P], K["zeros"][:, 0:F], start=True, stop=False)

                def add_squares(i, c):
                    b = 2 * i + c
                    pe.wait_ge(squared, b + 1)
                    tail = isinstance(i, int) and b == NB - 1
                    for j in range(WB):
                        rows = TAIL if tail and j == WB - 1 else P
                        mm = pe.matmul(ps_v[:, 0:F], K["ones"][0:rows, :], square[0:rows, c % 2, j, :],
                                       start=False, stop=rows < P or (tail and j == WB - 1))
                    mm.then_inc(used, 1)
                pace(pe, NB, [(add_squares, 0)])
                pe.matmul(ps_m[:, 0:F], K["zeros"][:, 0:P], K["zeros"][:, 0:F], start=True,
                          stop=True).then_inc(varied, 1)


def build_gat_input(nc, L, M, K, S, F, elu, W, a_src, a_dst, table):
    NW, WB, NB = S.NW, S.WB, S.NB
    feat, scale, offset = K["feat"], K["bn_scale"], K["bn_offset"]
    KP = 1 if F <= P else 2
    KF = F // KP
    sems = ("w_in", "cleared", "wt", "wt_got", "wa", "wa_got", "scaled", "shifted", "clipped", "exped", "staged",
            "turned", "copied", "product", "placed", "stored")
    (w_in, cleared, wt_made, wt_got, wa_made, wa_got, scaled, shifted, clipped, exped, staged, turned, copied,
     product, placed, stored) = [M.sem(f"{L}gat_{n}") for n in sems]
    with ExitStack() as scope:
        T = Mem(nc, scope, L)
        w = T.sb("w_gat", [P, KP, WIDE])
        wt = T.sb("w_turned", [P, 2, F])
        heads = T.sb("heads", [P, 2, 2 * HEADS])
        scl = T.sb("scl", [P, 2, F])
        shf = T.sb("shf", [P, 2, F])
        clp = T.sb("clp", [P, 2, F])
        ex = T.sb("ex", [P, 2, F])
        stage = T.sb("stage", [P, 2, KP * P])
        xt = T.sb("xt", [P, 2, KP * P])
        ps_t = [T.ps(f"pt{i}") for i in range(2)]
        ps_o = [T.ps(f"po{i}") for i in range(2)]
        ps_w, ps_a = T.ps("pw"), T.ps("pa")

        with nc.Block() as block:
            @block.sync
            def _(sp):
                sp.dma_start(w[0:KF, :, 0:FEAT], W.rearrange("(k p) f -> p k f", p=KF)).then_inc(w_in, 16)
                sp.wait_ge(cleared, 1)
                with nc.allow_non_contiguous_dma(reason="a head's 64 values down the partitions"):
                    for h in range(HEADS):
                        rows = slice(HID * (h % 2), HID * (h % 2) + HID)
                        for q, a in enumerate((a_src, a_dst)):
                            col = q * HEADS + h
                            sp.dma_start(heads[rows, h // 2, col:col + 1],
                                         a[h:h + 1, :].rearrange("a f -> f a")).then_inc(w_in, 16)
                for b in range(NB):
                    sp.wait_ge(placed, (b + 1) * WB)
                    rows = table[b * WB * P:(b + 1) * WB * P, :].rearrange("(w p) f -> p w f", p=P)
                    sp.dma_start(rows, feat[:, b * WB:(b + 1) * WB, 0:ROW]).then_inc(stored, 16)
                sp.wait_ge(stored, 16 * NB)

            @block.gpsimd
            def _(pool):
                pool.memset(heads[:, :, :], 0.0).then_inc(cleared, 1)

                def scaling(i, c):
                    n, slot = 2 * i + c, c % 2
                    wait(pool, shifted, n - 1)
                    pool.tensor_tensor(scl[:, slot, :], feat[:, one(n), 0:F].squeeze(1), scale[:, 0:F],
                                       ALU.mult).then_inc(scaled, 1)
                pace(pool, NW, [(scaling, 0)])

            @block.vector
            def _(dve):
                if F < P:
                    dve.memset(stage[:, :, F:P], 0.0)

                def widen(n, src, out, made, got):
                    dve.wait_ge(made, n)
                    dve.tensor_copy(out, src).then_inc(got, 1)
                for j in range(2):
                    for k in range(KP):
                        n = j * KP + k
                        widen(n + 1, ps_w[:, 0:KF], wt[:, j, k * KF:(k + 1) * KF], wt_made, wt_got)
                for k in range(KP):
                    widen(k + 1, ps_a[0:KF, 0:2 * HEADS], w[0:KF, k, FEAT:WIDE], wa_made, wa_got)

                def shift(i, c):
                    n, slot = 2 * i + c, c % 2
                    dve.wait_ge(scaled, n + 1)
                    to = shf if elu else stage
                    wait(dve, staged if elu else turned, n - 1)
                    dve.tensor_tensor(to[:, slot, 0:F], scl[:, slot, :], offset[:, 0:F], ALU.add
                                      ).then_inc(shifted, 1)
                    if elu:
                        dve.wait_ge(shifted, n + 1)
                        wait(dve, exped, n - 1)
                        dve.tensor_scalar(clp[:, slot, :], shf[:, slot, :], 0.0, None, ALU.min
                                          ).then_inc(clipped, 1)

                def unite(i, c):
                    n, slot = 2 * i + c, c % 2
                    dve.wait_ge(exped, n + 1)
                    wait(dve, turned, n - 1)
                    dve.scalar_tensor_tensor(out=stage[:, slot, :], in0=ex[:, slot, :], scalar=-1.0,
                                             in1=shf[:, slot, :], op0=ALU.add, op1=ALU.max).then_inc(staged, 1)
                pace(dve, NW, [(shift, 1), (unite, 0)] if elu else [(shift, 0)])

            @block.scalar
            def _(act):
                def expo(i, c):
                    n, slot = 2 * i + c, c % 2
                    act.wait_ge(clipped, n + 1)
                    wait(act, staged, n - 1)
                    act.activation(ex[:, slot, :], clp[:, slot, :], ACT.Exp).then_inc(exped, 1)

                def copy(i, c):
                    n, slot = 2 * i + c, c % 2
                    act.wait_ge(turned, n + 1)
                    wait(act, product, n - 1)
                    act.copy(xt[0:KF, slot, :], ps_t[slot][0:KF, 0:KP * P]).then_inc(copied, 1)

                def place(i, c):
                    n, slot = 2 * i + c, c % 2
                    act.wait_ge(product, n + 1)
                    act.copy(feat[:, one(n), 0:WIDE].squeeze(1), ps_o[slot][:, 0:WIDE]).then_inc(placed, 1)
                pace(act, NW, ([(expo, 2)] if elu else []) + [(copy, 1), (place, 0)])

            @block.tensor
            def _(pe):
                pe.wait_ge(w_in, 16 * (1 + 2 * HEADS))
                for j in range(2):
                    for k in range(KP):
                        n = j * KP + k
                        wait(pe, wt_got, n)
                        pe.transpose(ps_w[:, 0:KF], w[0:KF, k, j * P:(j + 1) * P], K["ident"][0:KF, 0:KF]
                                     ).then_inc(wt_made, 1)
                pe.wait_ge(wt_got, 2 * KP)
                for k in range(KP):
                    wait(pe, wa_got, k)
                    for j in range(2):
                        mm = pe.matmul(ps_a[0:KF, 0:2 * HEADS], wt[:, j, k * KF:(k + 1) * KF], heads[:, j, :],
                                       start=(j == 0), stop=(j == 1))
                    mm.then_inc(wa_made, 1)
                pe.wait_ge(wa_got, KP)
                linear(pe, K, S, (KP, KF), stage, ps_t, xt, ps_o, w, WIDE, staged if elu else shifted, turned,
                       copied, product, placed)


def build_gnn(nc, M, K, S, x, src, dst, W_gcn, gcn, gats):
    mod_rows = nc.dram_tensor("mod_rows", (S.NG, GE), BF16).ap()
    table0 = nc.dram_tensor("gcn_table", (S.NW * P, HID), F32).ap()
    K["bn_scale"], K["bn_offset"] = M.sb("bn_scale", [P, FEAT]), M.sb("bn_offset", [P, FEAT])
    build_constants(nc, M, K)
    K["feat"] = M.sb("feat", [P, S.NWP, WIDE])
    with ExitStack() as scope:
        T = Mem(nc, scope)
        K["shift_src"] = T.sb("shift_src", [P, S.NWP, HEADS])
        K["near_tab"] = T.sb("near_tab", [P, S.NWP, 2 * HEADS])
        K["tab24"] = T.sb("tab24", [P, S.NWP, 24], BF16)
        build_edge_tables(nc, T, K, S, src, dst, mod_rows)
        build_degrees(nc, T, K, S)
        build_gcn_input(nc, T, K, S, x, W_gcn, table0)
        build_edges(nc, "gcn_", T, K, S, table0, mod_rows, HID, False, K["spread_ok"])
        build_batch_norm(nc, "gcn_", T, K, S, HID, *gcn, gat=False)
        Mem.clear_signals(nc)
        for n, (W, a_src, a_dst, bias, gamma, beta) in enumerate(gats):
            L = f"gat{n}_"
            table = nc.dram_tensor(L + "table", (S.NW * P, ROW), F32).ap()
            build_gat_input(nc, L, T, K, S, W.shape[0], n > 0, W, a_src, a_dst, table)
            flag = build_attention(nc, L, T, K, S, table)
            build_edges(nc, L, T, K, S, table, mod_rows, ROW, True, flag)
            build_batch_norm(nc, L, T, K, S, FEAT, bias, gamma, beta, gat=True)
            Mem.clear_signals(nc)


def build_ffn_input(nc, M, K, S, x, gamma, beta, Wr, br, b2, xn_rows):
    N, NW, WB, NB, TAIL, EX = S.N, S.NW, S.WB, S.NB, S.TAIL, S.EX
    feat, scale, offset, gates = K["feat"], K["bn_scale"], K["bn_offset"], K["gates"]
    names = ("params x_in cleared scaled step exped rooted staged turned copied routed picked bias_rows bias_got "
             "stored biased placed").split()
    (params, x_in, cleared, scaled, step, exped, rooted, staged, turned, copied, routed, picked, rows_made,
     rows_got, stored, biased, placed) = [M.sem("ffi_" + n) for n in names]
    with ExitStack() as scope:
        T = Mem(nc, scope, "ffi_")
        xr = T.sb("xr", [P, WB, FEAT])
        z = T.sb("z", [P, WB, FEAT])
        zt = T.sb("zt", [P, 2, WB * P])
        st = T.sb("st", [P, WB, 6])
        mean, var = T.sb("mean", [P, WB]), T.sb("var", [P, WB])
        std = T.sb("std", [P, WB])
        rstd = T.sb("rstd", [P, WB])
        gm, bt = T.sb("gm", [P, FEAT]), T.sb("bt", [P, FEAT])
        wr = T.sb("wr", [P, 2, EX])
        brb = T.sb("brb", [P, EX])
        b2s = T.sb("b2s", [EX, FEAT])
        lg, top, idx = T.sb("lg", [P, WB, EX]), T.sb("top", [P, WB, 8]), T.sb("idx", [P, WB, 8], U32)
        idf = T.sb("idf", [P, WB, 8])
        hot1, hot2 = T.sb("hot1", [P, WB, EX]), T.sb("hot2", [P, WB, EX])
        g1, g2, ge, gs = T.sb("g1", [P, WB]), T.sb("g2", [P, WB]), T.sb("ge", [P, WB]), T.sb("gs", [P, WB])
        gt = T.sb("gt", [EX, 2, P])
        ps_t = [T.ps(f"pt{i}") for i in range(2)]
        ps_l = T.ps("pl")
        ps_g = [T.ps(f"pg{i}") for i in range(2)]
        ps_b = [T.ps(f"pb{i}") for i in range(2)]
        per = 30 + 6 * WB

        with nc.Block() as block:
            @block.sync
            def _(sp):
                for to, v in ((gm, gamma), (bt, beta), (brb, br)):
                    sp.dma_start(to[:, :], v.rearrange("(a f) -> a f", a=1).to_broadcast(
                        [P, v.shape[0]])).then_inc(params, 16)
                sp.dma_start(wr[:, :, :], Wr.rearrange("(k p) e -> p k e", p=P)).then_inc(params, 16)
                sp.dma_start(b2s[:, :], b2).then_inc(params, 16)
                sp.wait_ge(cleared, 1)
                for b in range(NB):
                    wait(sp, placed, b)
                    w0, w1 = b * WB, min((b + 1) * WB, NW - 1)
                    sp.dma_start(xr[:, 0:w1 - w0, :],
                                 x[w0 * P:w1 * P, :].rearrange("(w p) f -> p w f", p=P)).then_inc(x_in, 16)
                    if b == NB - 1:
                        sp.dma_start(xr[0:TAIL, WB - 1, :], x[(NW - 1) * P:N, :]).then_inc(x_in, 16)
                    sp.wait_ge(copied, (b + 1) * WB)
                    for k in range(2):
                        sp.dma_start(xn_rows[k, :, b * WB * P:(b + 1) * WB * P], zt[:, k, :]).then_inc(stored, 16)
                sp.wait_ge(stored, 32 * NB)

            @block.gpsimd
            def _(pool):
                pool.memset(xr[:, :, :], 0.0).then_inc(cleared, 1)
                with pool.Fori(0, NW) as w:
                    v = feat[:, one(w), 0:FEAT].squeeze(1)
                    pool.tensor_tensor(v, v, scale[:, :], ALU.mult).then_inc(scaled, 1)

            @block.vector
            def _(dve):
                dve.wait_ge(params, 80)

                def layer_norm(link, src, dst, n):
                    for w in range(WB):
                        link(dve.bn_stats(st[:, w, :], src(w)))
                    spread_of(dve, link, st, mean[:, :], var[:, :])
                    dve.wait_ge(rooted, n)
                    link(dve.reciprocal(rstd[:, :], std[:, :]))
                    for w in range(WB):
                        link(dve.tensor_scalar(dst(w), src(w), mean[:, w:w + 1], rstd[:, w:w + 1], ALU.subtract,
                                               ALU.mult))

                for b in range(NB):
                    link = Chain(dve, step, b * per)
                    body = feat[:, b * WB:(b + 1) * WB, 0:FEAT]

                    def every(v):
                        return v[:, :].unsqueeze(1).to_broadcast([P, WB, v.shape[1]])

                    def heads8(v):
                        return v[:, :].unsqueeze(2).to_broadcast([P, WB, EX])
                    dve.wait_ge(scaled, (b + 1) * WB)
                    wait(dve, turned, b * WB)
                    link(dve.tensor_tensor(body, body, every(offset), ALU.add))
                    link(dve.tensor_scalar(z[:, :, :], body, 0.0, None, ALU.min))
                    dve.wait_ge(exped, 2 * b + 1)
                    link(dve.scalar_tensor_tensor(out=body, in0=z[:, :, :], scalar=-1.0, in1=body, op0=ALU.add,
                                                  op1=ALU.max))
                    dve.wait_ge(x_in, 16 * (b + 1 + (b == NB - 1)))
                    link(dve.tensor_tensor(body, body, xr[:, :, :], ALU.add))
                    layer_norm(link, lambda w: body[:, w, :], lambda w: z[:, w, :], 2 * b + 1)
                    layer_norm(link, lambda w: z[:, w, :], lambda w: z[:, w, :], 2 * b + 2)
                    link(dve.tensor_tensor(z[:, :, :], z[:, :, :], every(gm), ALU.mult))
                    dve.tensor_tensor(z[:, :, :], z[:, :, :], every(bt), ALU.add).then_inc(staged, 1)
                    dve.wait_ge(routed, b + 1)
                    link(dve.tensor_tensor(lg[:, :, :], ps_l[:, 0:WB * EX].rearrange("p (w e) -> p w e", e=EX),
                                           every(brb), ALU.add))
                    for w in range(WB):
                        link(dve.max(top[:, w, :], lg[:, w, :]))
                        link(dve.max_index(idx[:, w, :], top[:, w, :], lg[:, w, :]))
                    link(dve.tensor_copy(idf[:, :, :], idx[:, :, :]))
                    link(dve.tensor_tensor(g2[:, :], top[:, :, 1], top[:, :, 0], ALU.subtract))
                    dve.wait_ge(exped, 2 * b + 2)
                    link(dve.tensor_scalar(gs[:, :], ge[:, :], 1.0, None, ALU.add))
                    link(dve.reciprocal(g1[:, :], gs[:, :]))
                    link(dve.tensor_tensor(g2[:, :], ge[:, :], g1[:, :], ALU.mult))
                    count8 = K["count"][:, 0:EX].unsqueeze(1).to_broadcast([P, WB, EX])
                    for n, (hot, g) in enumerate(((hot1, g1), (hot2, g2))):
                        link(dve.tensor_tensor(hot[:, :, :], count8, idf[:, :, n:n + 1].to_broadcast([P, WB, EX]),
                                               ALU.is_equal))
                        link(dve.tensor_tensor(hot[:, :, :], hot[:, :, :], heads8(g), ALU.mult))
                    link(dve.tensor_tensor(gates[:, b * WB:(b + 1) * WB, :], hot1[:, :, :], hot2[:, :, :],
                                           ALU.add))
                    assert link.n == per
                    for w in range(WB):
                        n = b * WB + w
                        dve.wait_ge(rows_made, n + 1)
                        dve.tensor_copy(gt[:, n % 2, :], ps_g[n % 2][0:EX, 0:P]).then_inc(rows_got, 1)
                        dve.wait_ge(biased, n + 1)
                        last = dve.tensor_tensor(body[:, w, :], body[:, w, :], ps_b[n % 2][:, 0:FEAT], ALU.add)
                    last.then_inc(placed, 1)

            @block.scalar
            def _(act):
                for b in range(NB):
                    base = b * per
                    act.wait_ge(step, base + 2)
                    act.activation(z[:, :, :], z[:, :, :], ACT.Exp).then_inc(exped, 1)
                    for n in range(2):
                        act.wait_ge(step, base + 4 + (WB + 6) * (n + 1) + (1 + WB) * n)
                        act.activation(std[:, :], var[:, :], ACT.Sqrt, bias=K["eps"][:, 0:1]).then_inc(rooted, 1)
                    wait(act, stored, 32 * b)
                    for w in range(WB):
                        n = b * WB + w
                        act.wait_ge(turned, n + 1)
                        act.copy(zt[:, :, w * P:(w + 1) * P], ps_t[n % 2][:, 0:2 * P].rearrange(
                            "p (k t) -> p k t", k=2)).then_inc(copied, 1)
                    act.wait_ge(step, base + 22 + 6 * WB)
                    act.activation(ge[:, :], g2[:, :], ACT.Exp).then_inc(exped, 1)

            @block.tensor
            def _(pe):
                pe.wait_ge(params, 80)
                for b in range(NB):
                    pe.wait_ge(staged, b + 1)
                    for w in range(WB + 1):
                        n = b * WB + w
                        if w < WB:
                            wait(pe, copied, n - 1)
                            for k in range(2):
                                mm = pe.transpose(ps_t[n % 2][:, k * P:(k + 1) * P], z[:, w, k * P:(k + 1) * P],
                                                  K["ident"][:, :])
                            mm.then_inc(turned, 1)
                        if w:
                            pe.wait_ge(copied, n)
                            for k in range(2):
                                mm = pe.matmul(ps_l[:, (w - 1) * EX:w * EX], zt[:, k, (w - 1) * P:w * P],
                                               wr[:, k, :], start=(k == 0), stop=(k == 1))
                    mm.then_inc(routed, 1)
                    pe.wait_ge(step, (b + 1) * per)
                    for w in range(WB):
                        n = b * WB + w
                        wait(pe, rows_got, n - 1)
                        pe.transpose(ps_g[n % 2][0:EX, 0:P], gates[:, n, :], K["ident"][:, :]).then_inc(rows_made, 1)
                        pe.wait_ge(rows_got, n + 1)
                        pe.matmul(ps_b[n % 2][:, 0:FEAT], gt[:, n % 2, :], b2s[:, :], start=True,
                                  stop=True).then_inc(biased, 1)


def build_experts(nc, M, K, S, W1, b1, W2, xn_rows, out):
    N, NW, TAIL, EX, HD = S.N, S.NW, S.TAIL, S.EX, S.HD
    feat, gates = K["feat"], K["gates"]
    HB = HD // P
    TW = 2
    TT = TW * P
    NT = NW // TW
    with ExitStack() as scope:
        T = Mem(nc, scope, "ffn_")
        w1 = T.sb("w1", [P, EX, 2, HD])
        w2 = T.sb("w2", [P, EX, HB, FEAT])
        b1t = T.sb("b1t", [P, EX, HB])
        b1r = T.sb("b1r", [EX * HB, P])
        xt = T.sb("xt", [P, 2, 2, TT])
        h = T.sb("h", [P, 2, HB, TT])
        ps_h = [T.ps(f"ph{i}") for i in range(4)]
        ps_y = [T.ps(f"py{i}") for i in range(4)]
        names = "w1_in w2_in b1_in b1_turned b1_got up acted down added stored".split()
        w1_in, w2_in, b1_in, b1_turned, b1_got, up, acted, down, added, stored = [M.sem("ffn_" + n) for n in names]
        xt_in = [M.sem(f"ffn_xt{j}") for j in range(2)]

        with nc.Block() as block:
            @block.sync
            def _(sp):
                sp.dma_start(b1r[:, :], b1.rearrange("e (k p) -> (e k) p", p=P)).then_inc(b1_in, 16)

                def tokens(i, c):
                    t, slot = 2 * i + c, c % 2
                    wait(sp, down, EX * TW * (t - 1) )
                    sp.dma_start(xt[:, slot, :, :], xn_rows[:, :, bass.ds(t * TT, TT)].rearrange(
                        "k p t -> p k t")).then_inc(xt_in[slot], 16)
                tokens(0, 0)
                for e in range(EX):
                    sp.dma_start(w1[:, e, :, :], W1[e].rearrange("(k p) h -> p k h", p=P)).then_inc(w1_in, 16)
                    sp.dma_start(w2[:, e, :, :], W2[e].rearrange("(k p) f -> p k f", p=P)).then_inc(w2_in, 16)
                tokens(0, 1)
                with sp.Fori(1, NT // 2) as i:
                    for c in range(2):
                        tokens(i, c)
                if NT % 2:
                    tokens(NT // 2, 0)

            @block.gpsimd
            def _(pool):
                def rows(w, n):
                    return out[w * P:(w + n) * P, :].rearrange("(w p) f -> p w f", p=P)
                with pool.Fori(0, NT - 1) as t:
                    pool.wait_ge(added, EX * TW * (t + 1))
                    pool.dma_start(out[bass.ds(t * TT, TT), :].rearrange("(w p) f -> p w f", p=P),
                                   feat[:, bass.ds(t * TW, TW), 0:FEAT]).then_inc(stored, 16)
                pool.wait_ge(added, EX * NW)
                pool.dma_start(rows(NW - 2, 1), feat[:, NW - 2:NW - 1, 0:FEAT]).then_inc(stored, 16)
                pool.dma_start(out[(NW - 1) * P:N, :], feat[0:TAIL, NW - 1, 0:FEAT]).then_inc(stored, 16)
                pool.wait_ge(stored, 16 * (NT + 1))

            @block.tensor
            def _(pe):
                pe.wait_ge(b1_in, 16)
                pe.transpose(ps_y[0][:, 0:EX * HB], b1r[:, :], K["ident"][0:EX * HB, 0:EX * HB]
                             ).then_inc(b1_turned, 1)
                pe.wait_ge(b1_got, 1)

                def upward(i, c, e, first=False):
                    t, slot = 2 * i + c, c % 2
                    if e == 0:
                        pe.wait_ge(xt_in[slot], 16 * (i + c // 2 + 1))
                    if first:
                        pe.wait_ge(w1_in, 16 * EX)
                    for k in range(HB):
                        n = (t * EX + e) * HB + k
                        wait(pe, acted, n - 3)
                        for d in range(2):
                            mm = pe.matmul(ps_h[k % 4][:, 0:TT], w1[:, e, d, k * P:(k + 1) * P],
                                           xt[:, slot, d, :], start=(d == 0), stop=(d == 1))
                        mm.then_inc(up, 1)

                def downward(i, c, e, first=False):
                    t = 2 * i + c
                    if first:
                        pe.wait_ge(w2_in, 16 * EX)
                    pe.wait_ge(acted, (t * EX + e + 1) * HB)
                    for j in range(TW):
                        m = (t * EX + e) * TW + j
                        wait(pe, added, m - 3)
                        for k in range(HB):
                            mm = pe.matmul(ps_y[(e * TW + j) % 4][:, 0:FEAT], h[:, e % 2, k, j * P:(j + 1) * P],
                                           w2[:, e, k, :], start=(k == 0), stop=(k == HB - 1))
                        mm.then_inc(down, 1)

                def experts(i, c):
                    static = isinstance(i, int) and 2 * i + c == 0
                    for e in range(1, EX):
                        upward(i, c, e, static and e == 1)
                        downward(i, c, e - 1, static and e == 1)
                    if not isinstance(i, int) or 2 * i + c + 1 < NT:
                        upward(i, c + 1, 0)
                    downward(i, c, EX - 1)
                upward(0, 0, 0, True)
                pace(pe, NT, [(experts, 0)])

            @block.scalar
            def _(act):
                act.wait_ge(b1_turned, 1)
                act.copy(b1t[:, :, :].rearrange("p e k -> p (e k)"), ps_y[0][:, 0:EX * HB]).then_inc(b1_got, 1)
                act.wait_ge(b1_got, 1)

                def gelus(i, c):
                    t = 2 * i + c
                    for e in range(EX):
                        wait(act, down, (t * EX + e - 1) * TW)
                        for k in range(HB):
                            n = (t * EX + e) * HB + k
                            act.wait_ge(up, n + 1)
                            act.activation(h[:, e % 2, k, :], ps_h[k % 4][:, 0:TT], ACT.Gelu,
                                           bias=b1t[:, e, k:k + 1]).then_inc(acted, 1)
                pace(act, NT, [(gelus, 0)])

            @block.vector
            def _(dve):
                def adds(i, c):
                    t = 2 * i + c
                    for e in range(EX):
                        for j in range(TW):
                            m = (t * EX + e) * TW + j
                            w = t * TW + j
                            dve.wait_ge(down, m + 1)
                            wait(dve, added, m - 1)
                            to = feat[:, one(w), 0:FEAT].squeeze(1)
                            dve.scalar_tensor_tensor(out=to, in0=ps_y[(e * TW + j) % 4][:, 0:FEAT],
                                                     scalar=at1(gates, w)[:, e:e + 1], in1=to, op0=ALU.mult,
                                                     op1=ALU.add).then_inc(added, 1)
                pace(dve, NT, [(adds, 0)])


def build(nc, x, src, dst, gnn, ffn, out):
    W_gcn, b_gcn, g0, beta0, W1, a_src1, a_dst1, b1, g1, beta1, W2, a_src2, a_dst2, b2, g2, beta2 = gnn
    gamma, beta, Wr, br, F1, c1, F2, c2 = ffn
    S = Shapes(x.shape[0], src.shape[0], Wr.shape[1], F1.shape[2])
    xn_rows = nc.dram_tensor("xn_rows", (2, P, S.NW * P), F32).ap()
    with ExitStack() as ctx:
        M, K = Mem(nc, ctx), {}
        build_gnn(nc, M, K, S, x, src, dst, W_gcn, (b_gcn, g0, beta0),
                  [(W1, a_src1, a_dst1, b1, g1, beta1), (W2, a_src2, a_dst2, b2, g2, beta2)])
        K["gates"] = M.sb("gates", [P, S.NW, S.EX])
        build_ffn_input(nc, M, K, S, x, gamma, beta, Wr, br, c2, xn_rows)
        build_experts(nc, M, K, S, F1, c1, F2, xn_rows, out)


_GNN = ["W_gcn", "b_gcn", "g0", "beta0", "W1", "a_src1", "a_dst1", "b1", "g1", "beta1", "W2", "a_src2", "a_dst2",
        "b2", "g2", "beta2"]
_FFN = ["gamma", "beta", "Wr", "br", "W1", "b1", "W2", "b2"]
_INS = ["x", "src", "dst"] + ["L0_gnn_" + n for n in _GNN] + ["L0_ffn_" + n for n in _FFN]


def kernel(**inputs):
    import numpy as _np
    import concourse.bacc as _bacc
    from concourse import mybir as _mybir
    from concourse.bass_utils import run_bass_kernel_spmd as _run

    nc = _bacc.Bacc("TRN2", target_bir_lowering=False, num_devices=1)
    arrays, args = {}, []
    for name in _INS:
        a = _np.ascontiguousarray(inputs[name])
        arrays[f"in_{name}_dram"] = a
        args.append(nc.dram_tensor(f"in_{name}_dram", a.shape, _mybir.dt.from_np(a.dtype),
                                   kind="ExternalInput").ap())
    shape = inputs["x"].shape
    out = nc.dram_tensor("out_0_dram", tuple(shape), _mybir.dt.float32, kind="ExternalOutput").ap()
    n = 3 + len(_GNN)
    build(nc, *args[:3], args[3:n], args[n:], out)
    r = _run(nc, [arrays], core_ids=[0])
    return r.results[0]["out_0_dram"]
```

```python
from contextlib import ExitStack

import concourse.bass as bass
from concourse import mybir

P = 128
F32 = mybir.dt.float32
BF16 = mybir.dt.bfloat16
I32 = mybir.dt.int32
U32 = mybir.dt.uint32
ALU = mybir.AluOpType
ACT = mybir.ActivationFunctionType
AX = mybir.AxisListType.X
MAX = bass.bass_isa.ReduceOp.max

HEADS, HID = 4, 64
FEAT = HEADS * HID
ROW = FEAT + HEADS
WIDE = FEAT + 2 * HEADS
CH = 4
GE = CH * P
RING = 4
SLOPE = 0.2
EPS = 1e-5
SAFE = 60.0
NOWHERE = -1.0e6


class Chain:

    def __init__(self, eng, sem, start=0):
        self.eng, self.sem, self.start, self.n = eng, sem, start, 0

    def __call__(self, ins):
        ins.then_inc(self.sem, 1)
        self.n += 1
        self.eng.wait_ge(self.sem, self.start + self.n)


def pace(eng, n, steps, ring=2):
    leads = [lead for _, lead in steps]
    low, high = -max(leads), n - min(leads)
    first = -(-(ring + max(0, -min(leads))) // ring)
    last = (n - max(leads)) // ring

    def turn(i, c, known):
        for fn, lead in steps:
            if not known or 0 <= ring * i + c + lead < n:
                fn(i, c + lead)

    first, last = (first, last) if last - first >= 2 else (n, n)
    for t in range(low, min(first * ring, high)):
        turn(t // ring, t % ring, True)
    if first < n:
        with eng.Fori(first, last) as i:
            for c in range(ring):
                turn(i, c, False)
        for t in range(last * ring, high):
            turn(t // ring, t % ring, True)


class Mem:

    taken = []

    def __init__(self, nc, ctx, stage=""):
        self.nc, self.ctx, self.stage = nc, ctx, stage

    def sb(self, name, shape, dt=F32):
        return self.ctx.enter_context(self.nc.sbuf_tensor(self.stage + name, shape, dt))

    def ps(self, name, shape=(P, 512), dt=F32):
        return self.ctx.enter_context(self.nc.psum_tensor(self.stage + name, list(shape), dt))

    def sem(self, name):
        handle = self.nc.alloc_semaphore(name=name)
        Mem.taken.append(handle)
        return handle

    @staticmethod
    def clear_signals(nc):
        nc.clear_and_free_semaphores(Mem.taken)
        nc.all_engine_barrier()
        Mem.taken = []


class Shapes:
    def __init__(self, n, e, experts, hidden):
        self.N, self.E = n, e
        self.NW = -(-n // P)
        self.TAIL = n - (self.NW - 1) * P
        self.NWP = -(-(self.NW + 1) // 4) * 4
        self.NG = -(-e // GE)
        self.LAST = e - (self.NG - 1) * GE
        self.NT = -(-self.NG // P)
        self.GT = self.NG // self.NT
        self.WB = next(b for b in (14, 7, 4, 2) if self.NW % b == 0)
        self.NB = self.NW // self.WB
        self.EX, self.HD = experts, hidden
        self.NS = -(-(2 * self.NW + experts - 1) // 4) * 4
        assert self.NS <= 256 and self.NW <= 128
        assert self.NG % 4 == 0 and self.GT * self.NT == self.NG and self.NW % 2 == 0


def wait(eng, sem, count):
    if not isinstance(count, int) or count > 0:
        eng.wait_ge(sem, count)


def spread_of(dve, link, st, mean, var):
    link(dve.tensor_tensor(var, st[:, :, 1], st[:, :, 4], ALU.subtract))
    link(dve.tensor_tensor(mean, st[:, :, 1], st[:, :, 4], ALU.add))
    link(dve.tensor_scalar(mean, mean, 0.5, None, ALU.mult))
    link(dve.scalar_tensor_tensor(out=var, in0=var, scalar=0.25, in1=var, op0=ALU.mult, op1=ALU.mult))
    link(dve.scalar_tensor_tensor(out=var, in0=st[:, :, 2], scalar=1.0 / FEAT, in1=var, op0=ALU.mult,
                                  op1=ALU.add))
    link(dve.scalar_tensor_tensor(out=var, in0=st[:, :, 5], scalar=1.0 / FEAT, in1=var, op0=ALU.mult,
                                  op1=ALU.add))


def one(n):
    return bass.ds(n, 1)


def at1(t, n):
    return t[:, bass.ds(n, 1), :].squeeze(1)


def build_constants(nc, M, K):
    ident = M.sb("ident", [P, P])
    ones = M.sb("ones", [P, P])
    zeros = M.sb("zeros", [P, WIDE])
    count_i = M.sb("count_i", [P, P], I32)
    count = M.sb("count", [P, P])
    part_i = M.sb("part_i", [P, 1], I32)
    part = M.sb("part", [P, 1])
    eps = M.sb("eps", [P, 1])
    K.update(ident=ident, ones=ones, zeros=zeros, count=count, part=part, eps=eps)
    filled, counted = M.sem("const_filled"), M.sem("const_counted")
    with nc.Block() as block:
        @block.gpsimd
        def _(pool):
            pool.memset(ident[:, :], 0.0).then_inc(filled, 1)
            pool.wait_ge(filled, 1)
            pool.affine_select(out=ident[:, :], in_=ident[:, :], compare_op=ALU.not_equal, fill=1.0, base=0,
                               pattern=[[-1, P]], channel_multiplier=1)
            pool.iota(count_i[:, :], pattern=[[1, P]], base=0, channel_multiplier=0)
            pool.iota(part_i[:, :], pattern=[[1, 1]], base=0, channel_multiplier=1).then_inc(counted, 1)

        @block.vector
        def _(dve):
            dve.memset(ones[:, :], 1.0)
            dve.memset(zeros[:, :], 0.0)
            dve.memset(eps[:, :], EPS)
            dve.wait_ge(counted, 1)
            dve.tensor_copy(count[:, :], count_i[:, :])
            dve.tensor_copy(part[:, :], part_i[:, :])


def build_edge_tables(nc, M, K, S, src, dst, mod_rows):
    N, E, NG, NT, GT, LAST = S.N, S.E, S.NG, S.NT, S.GT, S.LAST
    src_t = M.sb("src_t", [P, NG, CH], I32)
    mod_t = M.sb("mod_t", [P, NG, CH])
    win_t = M.sb("win_t", [P, NG, CH])
    first_w = M.sb("first_w", [P, NG], I32)
    in_first = M.sb("in_first", [P, NG])
    in_next = M.sb("in_next", [P, NG])
    spread_ok = M.sb("spread_ok", [1, 1], I32)
    K.update(src_t=src_t, mod_t=mod_t, win_t=win_t, first_w=first_w, in_first=in_first, in_next=in_next,
             spread_ok=spread_ok)
    loaded_d, loaded_s, filled = M.sem("edge_dst_loaded"), M.sem("edge_src_loaded"), M.sem("edge_filled")
    step, rows_ready, padded = M.sem("edge_step"), M.sem("edge_rows_ready"), M.sem("edge_padded")
    stored, turned, taken = M.sem("edge_mod_stored"), M.sem("edge_turned"), M.sem("edge_taken")
    spread_max, spread_in = M.sem("edge_spread_max"), M.sem("edge_spread_in")
    with ExitStack() as scope:
        T = Mem(nc, scope)
        raw_d = T.sb("raw_d", [GT, NT, GE], I32)
        raw_s = T.sb("raw_s", [GT, NT, GE], I32)
        win_i = T.sb("win_i", [GT, NT, GE], I32)
        mod_i = T.sb("mod_i", [GT, NT, GE], I32)
        flat = K["feat"][0:GT, :, :].rearrange("p w f -> p (w f)")
        f_dst, f_src, f_win = [flat[:, n * NT * GE:(n + 1) * NT * GE].rearrange("p (t e) -> p t e", t=NT)
                               for n in range(3)]
        f_mod = T.sb("f_mod", [GT, NT, GE])
        b_mod = T.sb("b_mod", [GT, NT, GE], BF16)
        least = T.sb("least", [GT, NT])
        most = T.sb("most", [GT, NT])
        least_i = T.sb("least_i", [GT, NT], I32)
        lw_i = T.sb("lw_i", [GT, NT], I32)
        lm_i = T.sb("lm_i", [GT, NT], I32)
        lw = T.sb("lw", [GT, NT])
        lm = T.sb("lm", [GT, NT])
        wide = T.sb("wide", [GT, 1])
        widest = T.sb("widest", [GT, 1])
        spread1 = T.sb("spread1", [1, 1])
        lwb = T.sb("lwb", [GT, NT, P])
        lmb = T.sb("lmb", [GT, NT, P])
        nowhere = T.sb("nowhere", [1, GE])
        turn = [T.ps(f"turn{i}") for i in range(2)]

        def rows(x, t, full):
            return x[t * GT * GE:(t * GT + full) * GE].rearrange("(g e) -> g e", e=GE)

        @nc_block(nc)
        def _(block):
            @block.sync
            def _(sp):
                for raw, x, got in ((raw_d, dst, loaded_d), (raw_s, src, loaded_s)):
                    if raw is raw_s:
                        sp.wait_ge(filled, 1)
                    for t in range(NT):
                        full = GT if t < NT - 1 else GT - 1
                        if full:
                            sp.dma_start(raw[0:full, t, :], rows(x, t, full)).then_inc(got, 16)
                    tail = x[(NG - 1) * GE:E].rearrange("(a e) -> a e", a=1)
                    sp.dma_start(raw[GT - 1:GT, NT - 1, 0:LAST], tail).then_inc(got, 16)
                if LAST < GE:
                    before = dst[(NG - 1) * GE - (GE - LAST):(NG - 1) * GE].rearrange("(a e) -> a e", a=1)
                    sp.dma_start(raw_d[GT - 1:GT, NT - 1, LAST:GE], before).then_inc(loaded_d, 16)
                sp.wait_ge(rows_ready, 1)
                for t in range(NT):
                    sp.dma_start(mod_rows[t * GT:(t + 1) * GT, :], b_mod[:, t, :]).then_inc(stored, 16)
                if LAST < GE:
                    sp.dma_start(f_mod[GT - 1:GT, NT - 1, LAST:GE], nowhere[0:1, LAST:GE]).then_inc(padded, 16)
                sp.wait_ge(stored, 16 * NT)

            @block.gpsimd
            def _(pool):
                pool.memset(raw_s[:, NT - 1, :], 0).then_inc(filled, 1)
                pool.wait_ge(spread_in, 1)
                pool.partition_all_reduce(widest[:, :], wide[:, :], GT, MAX).then_inc(spread_max, 1)

            @block.vector
            def _(dve):
                link = Chain(dve, step)
                dve.memset(nowhere[:, :], NOWHERE)
                dve.wait_ge(loaded_d, 16 * (NT - (GT == 1) + 1 + (LAST < GE)))
                dve.tensor_scalar(win_i[:, :, :], raw_d[:, :, :], 7, None, ALU.logical_shift_right)
                dve.tensor_scalar(mod_i[:, :, :], raw_d[:, :, :], P - 1, None, ALU.bitwise_and)
                link(dve.tensor_copy(f_dst[:, :, :], raw_d[:, :, :]))
                dve.tensor_copy(f_win[:, :, :], win_i[:, :, :])
                dve.tensor_copy(f_mod[:, :, :], mod_i[:, :, :])
                dve.tensor_copy(b_mod[:, :, :], mod_i[:, :, :]).then_inc(rows_ready, 1)
                dve.tensor_reduce(least[:, :], f_dst[:, :, :], AX, ALU.min)
                link(dve.tensor_reduce(most[:, :], f_dst[:, :, :], AX, ALU.max))
                dve.tensor_copy(least_i[:, :], least[:, :])
                link(dve.tensor_tensor(most[:, :], most[:, :], least[:, :], ALU.subtract))
                dve.tensor_reduce(wide[:, :], most[:, :], AX, ALU.max).then_inc(spread_in, 1)
                dve.tensor_scalar(lw_i[:, :], least_i[:, :], 7, None, ALU.logical_shift_right)
                link(dve.tensor_scalar(lm_i[:, :], least_i[:, :], P - 1, None, ALU.bitwise_and))
                dve.tensor_copy(lw[:, :], lw_i[:, :])
                link(dve.tensor_copy(lm[:, :], lm_i[:, :]))
                dve.tensor_copy(lwb[:, :, :], lw[:, :].unsqueeze(2).to_broadcast([GT, NT, P]))
                dve.tensor_copy(lmb[:, :, :], lm[:, :].unsqueeze(2).to_broadcast([GT, NT, P]))
                dve.wait_ge(loaded_s, 16 * (NT - (GT == 1) + 1))
                dve.tensor_copy(f_src[:, :, :], raw_s[:, :, :]).then_inc(rows_ready, 1)
                dve.wait_ge(spread_max, 1)
                dve.tensor_scalar(spread1[:, :], widest[0:1, :], float(P - 1), None, ALU.is_le).then_inc(rows_ready, 1)
                dve.wait_ge(rows_ready, 3)
                dve.tensor_copy(spread_ok[:, :], spread1[:, :])
                n = 0
                for t in range(NT):
                    g = slice(t * GT, (t + 1) * GT)
                    for f, out in ((f_src, src_t), (f_win, win_t), (f_mod, mod_t)):
                        dve.wait_ge(turned, n + 1)
                        v = turn[n % 2][:, 0:CH * GT].rearrange("p (c g) -> p g c", c=CH)
                        dve.tensor_copy(out[:, g, :], v).then_inc(taken, 1)
                        n += 1
                    dve.wait_ge(turned, n + 1)
                    lo, hi = turn[n % 2][:, 0:GT], turn[n % 2][:, P:P + GT]
                    dve.tensor_copy(first_w[:, g], lo)
                    dve.tensor_scalar(in_first[:, g], hi, K["part"][:, 0:1], None, ALU.is_le)
                    dve.tensor_scalar(in_next[:, g], hi, K["part"][:, 0:1], None, ALU.is_gt).then_inc(taken, 1)
                    n += 1

            @block.tensor
            def _(pe):
                n = 0
                pe.wait_ge(rows_ready, 3)
                if LAST < GE:
                    pe.wait_ge(padded, 16)
                for t in range(NT):
                    for f in (f_src, f_win, f_mod):
                        if n >= 2:
                            pe.wait_ge(taken, n - 1)
                        for c in range(CH):
                            mm = pe.transpose(turn[n % 2][:, c * GT:(c + 1) * GT], f[:, t, c * P:(c + 1) * P],
                                              K["ident"][0:GT, 0:GT])
                        mm.then_inc(turned, 1)
                        n += 1
                    if n >= 2:
                        pe.wait_ge(taken, n - 1)
                    pe.matmul(turn[n % 2][:, 0:GT], lwb[:, t, :], K["ident"][0:GT, 0:GT], start=True, stop=True)
                    pe.matmul(turn[n % 2][:, P:P + GT], lmb[:, t, :], K["ident"][0:GT, 0:GT],
                              start=True, stop=True).then_inc(turned, 1)
                    n += 1


def nc_block(nc):
    def run(body):
        with nc.Block() as block:
            body(block)
    return run


def build_degrees(nc, M, K, S):
    NG, NW = S.NG, S.NW
    dinv = M.sb("dinv", [P, NW])
    K["dinv"] = dinv
    built, used, done, step = M.sem("deg_built"), M.sem("deg_used"), M.sem("deg_done"), M.sem("deg_step")
    root = M.sem("deg_root")
    Q = 4 * CH
    with ExitStack() as scope:
        T = Mem(nc, scope)
        cb = T.sb("deg_count", [P, P], BF16)
        mb = T.sb("deg_mod", [P, NG * CH], BF16)
        wb = T.sb("deg_win", [P, NG * CH], BF16)
        hot_m = T.sb("hot_m", [P, 2, Q, P], BF16)
        hot_w = T.sb("hot_w", [P, 2, Q, NW], BF16)
        zb = T.sb("deg_zero", [P, P], BF16)
        deg = T.sb("deg", [P, NW])
        acc = T.ps("deg_ps")

        @nc_block(nc)
        def _(block):
            @block.vector
            def _(dve):
                link = Chain(dve, step)
                dve.memset(zb[:, :], 0.0).then_inc(built, 1)
                dve.tensor_copy(cb[:, :], K["count"][:, :])
                dve.tensor_copy(mb[:, :], K["mod_t"][:, :, :].rearrange("p g c -> p (g c)"))
                link(dve.tensor_copy(wb[:, :], K["win_t"][:, :, :].rearrange("p g c -> p (g c)")))

                def hots(i, b):
                    t = 2 * i + b
                    at = bass.ds(t * Q, Q)
                    wait(dve, used, t - 1)
                    dve.tensor_tensor(hot_m[:, b, :, :], cb[:, :].unsqueeze(1).to_broadcast([P, Q, P]),
                                      mb[:, at].unsqueeze(2).to_broadcast([P, Q, P]), ALU.is_equal)
                    dve.tensor_tensor(hot_w[:, b, :, :], cb[:, 0:NW].unsqueeze(1).to_broadcast([P, Q, NW]),
                                      wb[:, at].unsqueeze(2).to_broadcast([P, Q, NW]),
                                      ALU.is_equal).then_inc(built, 1)

                hots(0, 0)
                hots(0, 1)
                with dve.Fori(1, NG // 8) as i:
                    hots(i, 0)
                    hots(i, 1)
                dve.wait_ge(done, 1)
                link(dve.tensor_scalar(deg[:, :], acc[:, 0:NW], 1.0, 1.0, ALU.add, ALU.max))
                dve.wait_ge(root, 1)
                dve.reciprocal(dinv[:, :], deg[:, :])

            @block.scalar
            def _(act):
                act.wait_ge(step, 2)
                act.activation(deg[:, :], deg[:, :], ACT.Sqrt).then_inc(root, 1)

            @block.tensor
            def _(pe):
                pe.wait_ge(built, 1)
                pe.matmul(acc[:, 0:NW], zb[:, :], zb[:, 0:NW], start=True, stop=False)
                with pe.Fori(0, NG // 8) as i:
                    for b in range(2):
                        pe.wait_ge(built, 2 * i + b + 2)
                        for q in range(Q):
                            mm = pe.matmul(acc[:, 0:NW], hot_m[:, b, q, :], hot_w[:, b, q, :], start=False,
                                           stop=False)
                        mm.then_inc(used, 1)
                pe.matmul(acc[:, 0:NW], zb[:, :], zb[:, 0:NW], start=False,
                          stop=True).then_inc(done, 1)


def build_gcn_input(nc, M, K, S, x, W_gcn, table):
    N, NW, NWP, TAIL, WB, NB = S.N, S.NW, S.NWP, S.TAIL, S.WB, S.NB
    feat = K["feat"]
    cleared, w_in, step = M.sem("gi_cleared"), M.sem("gi_weights"), M.sem("gi_step")
    x_in = [M.sem(f"gi_x{b}") for b in range(NB)]
    rooted, scaled = M.sem("gi_rooted"), M.sem("gi_scaled")
    staged, turned, copied = M.sem("gi_staged"), M.sem("gi_turned"), M.sem("gi_copied")
    product, placed, stored = M.sem("gi_product"), M.sem("gi_placed"), M.sem("gi_stored")
    with ExitStack() as scope:
        T = Mem(nc, scope)
        wg = T.sb("w_gcn", [P, 2, HID])
        st = T.sb("gi_st", [P, NW, 6])
        mean, var = T.sb("gi_mean", [P, NW]), T.sb("gi_var", [P, NW])
        std = T.sb("gi_std", [P, NW])
        rstd = T.sb("gi_rstd", [P, NW])
        stage = T.sb("gi_stage", [P, 2, FEAT])
        xt = T.sb("gi_xt", [P, 2, FEAT])
        ps_t = [T.ps(f"gi_pt{i}") for i in range(2)]
        ps_o = [T.ps(f"gi_po{i}") for i in range(2)]

        @nc_block(nc)
        def _(block):
            @block.sync
            def _(sp):
                sp.wait_ge(cleared, 1)
                for b in range(NB):
                    w0, w1 = b * WB, min((b + 1) * WB, NW - 1)
                    sp.dma_start(feat[:, w0:w1, 0:FEAT],
                                 x[w0 * P:w1 * P, :].rearrange("(w p) f -> p w f", p=P)).then_inc(x_in[b], 16)
                sp.dma_start(feat[0:TAIL, NW - 1, 0:FEAT], x[(NW - 1) * P:N, :]).then_inc(x_in[NB - 1], 16)
                sp.dma_start(wg[:, :, :], W_gcn.rearrange("(k p) f -> p k f", p=P)).then_inc(w_in, 16)
                for b in range(NB):
                    sp.wait_ge(placed, (b + 1) * WB)
                    rows = table[b * WB * P:(b + 1) * WB * P, :].rearrange("(w p) f -> p w f", p=P)
                    sp.dma_start(rows, feat[:, b * WB:(b + 1) * WB, 0:HID]).then_inc(stored, 16)
                sp.wait_ge(stored, 16 * NB)

            @block.vector
            def _(dve):
                dve.memset(feat[:, NW - 1:NWP, :], 0.0).then_inc(cleared, 1)
                link = Chain(dve, step)
                for b in range(NB):
                    dve.wait_ge(x_in[b], 16 * (1 + (b == NB - 1)))
                    with dve.Fori(b * WB, (b + 1) * WB) as w:
                        dve.bn_stats(at1(st, w), feat[:, one(w), 0:FEAT].squeeze(1)).then_inc(scaled, 1)
                dve.wait_ge(scaled, NW)
                spread_of(dve, link, st, mean[:, :], var[:, :])
                dve.wait_ge(rooted, 1)
                link(dve.reciprocal(rstd[:, :], std[:, :]))

                def put(i, c):
                    w, slot = 2 * i + c, c % 2
                    wait(dve, turned, w - 1)
                    dve.tensor_scalar(stage[:, slot, :], feat[:, bass.ds(w, 1), 0:FEAT].squeeze(1),
                                      mean[:, one(w)], rstd[:, bass.ds(w, 1)],
                                      ALU.subtract, ALU.mult).then_inc(staged, 1)

                def take(i, c):
                    w, slot = 2 * i + c, c % 2
                    dve.wait_ge(product, w + 1)
                    dve.wait_ge(staged, w + 1)
                    dve.tensor_scalar(feat[:, bass.ds(w, 1), 0:HID].squeeze(1), ps_o[slot][:, 0:HID],
                                      K["dinv"][:, bass.ds(w, 1)], None, ALU.mult).then_inc(placed, 1)

                pace(dve, NW, [(put, 2), (take, 0)])

            @block.scalar
            def _(act):
                act.wait_ge(step, 6)
                act.activation(std[:, :], var[:, :], ACT.Sqrt, bias=K["eps"][:, 0:1]).then_inc(rooted, 1)

                def copy(i, c):
                    w, slot = 2 * i + c, c % 2
                    act.wait_ge(turned, w + 1)
                    wait(act, product, w - 1)
                    act.copy(xt[:, slot, :], ps_t[slot][:, 0:FEAT]).then_inc(copied, 1)

                pace(act, NW, [(copy, 0)])

            @block.tensor
            def _(pe):
                pe.wait_ge(w_in, 16)
                linear(pe, K, S, (2, P), stage, ps_t, xt, ps_o, wg, HID, staged, turned, copied, product, placed)


def linear(pe, K, S, parts, stage, ps_t, xt, ps_o, weights, width, staged, turned, copied, product, placed):
    def turn(i, c):
        w, slot = 2 * i + c, c % 2
        pe.wait_ge(staged, w + 1)
        wait(pe, copied, w - 1)
        for k in range(parts[0]):
            mm = pe.transpose(ps_t[slot][:, k * P:k * P + P], stage[:, slot, k * P:k * P + P], K["ident"][:, :])
        mm.then_inc(turned, 1)

    def multiply(i, c):
        w, slot = 2 * i + c, c % 2
        pe.wait_ge(copied, w + 1)
        wait(pe, placed, w - 1)
        for k in range(parts[0]):
            mm = pe.matmul(ps_o[slot][:, 0:width], xt[0:parts[1], slot, k * P:k * P + P], weights[0:parts[1], k, 0:width],
                           start=(k == 0), stop=(k == parts[0] - 1))
        mm.then_inc(product, 1)

    pace(pe, S.NW, [(turn, 1), (multiply, 0)])


def edge_buffers(T, width, gat):
    B = dict(idx=T.sb("idx", [P, RING, CH], I32), rows=T.sb("rows", [P, RING, CH, width]),
             hot=T.sb("hot", [P, RING, CH, P]), ps_sum=[T.ps(f"ps_sum{i}") for i in range(2)])
    if gat:
        B.update(mod=T.sb("mod", [P, RING, GE], BF16), hot_t=T.sb("hot_t", [P, RING, GE], BF16),
                 tab=T.sb("tab", [P, RING, 2, 24], BF16), near=T.sb("near", [P, 2, CH, 2 * HEADS]),
                 logit=T.sb("logit", [P, 2, CH, HEADS]), msg=T.sb("msg", [P, 2, CH, ROW]),
                 ps_near=[T.ps(f"ps_near{i}") for i in range(2)])
    return B


def fast_edges(L, M, K, S, B, table, mod_rows, width, gat):
    NG = S.NG
    feat = K["feat"]
    idx_staged, begun = M.sem(L + "idx_staged"), M.sem(L + "begun")
    rows_in = [M.sem(f"{L}rows_in{j}") for j in range(RING)]
    hot_built, summed, added = M.sem(L + "hot_built"), M.sem(L + "summed"), M.sem(L + "added")
    if gat:
        mod_in = [M.sem(f"{L}mod_in{j}") for j in range(RING)]
        tab_staged, near_made = M.sem(L + "tab_staged"), M.sem(L + "near_made")
        logit_step, weighed, msg_made = M.sem(L + "logit_step"), M.sem(L + "weighed"), M.sem(L + "msg_made")
    rows_used = msg_made if gat else summed

    def gather(pool):
        def group(i, c):
            g = RING * i + c
            pool.wait_ge(idx_staged, g + 1)
            wait(pool, rows_used, g - 3)
            pool.sem_inc(begun, 1)
            for k in range(CH):
                pool.indirect_dma_start(B["rows"][:, c, k, :], None, table,
                                        bass.IndirectOffsetOnAxis(ap=B["idx"][:, c, k:k + 1], axis=0)
                                        ).then_inc(rows_in[c], 16)
        pace(pool, NG, [(group, 0)], RING)

    def send_mods(sp):
        def group(i, c):
            g = RING * i + c
            wait(sp, hot_built, g - 3)
            sp.dma_start(B["mod"][:, c, :], mod_rows[one(g), :].to_broadcast([P, GE])).then_inc(mod_in[c], 16)
        pace(sp, NG, [(group, 0)], RING)

    def act_program(act):
        regs = [act.alloc_register(f"{L}act_w{j}") for j in range(RING)]

        def stage(i, c):
            j, g = c % RING, RING * i + c
            wait(act, rows_in[j], 64 * (i + c // RING))
            act.copy(B["idx"][:, j, :], at1(K["src_t"], g)).then_inc(idx_staged, 1)
            if not gat:
                return
            wait(act, near_made, g - 3)
            if j == 0:
                act.load(regs, K["first_w"][0:1, bass.ds(g, RING)])
            w = act.snap(regs[j], min_val=0, max_val=S.NW - 1)
            for side, mask in enumerate(("in_first", "in_next")):
                ins = act.activation(B["tab"][:, j, side, :], K["tab24"][:, bass.ds(w + side, 1), :].squeeze(1),
                                     ACT.Copy, scale=K[mask][:, one(g)])
            ins.then_inc(tab_staged, 1)

        def weigh(i, c):
            g = RING * i + c
            act.wait_ge(logit_step, 4 * g + 4)
            wait(act, summed, g - 1)
            act.activation(B["msg"][:, c % 2, :, FEAT:ROW], B["logit"][:, c % 2, :, :], ACT.Exp).then_inc(weighed, 1)

        pace(act, NG, [(weigh, 2), (stage, RING + 2)] if gat else [(stage, RING)], RING)

    def pe_program(pe):
        def look(i, c):
            j, g, b = c % RING, RING * i + c, c % 2
            pe.wait_ge(hot_built, g + 1)
            pe.wait_ge(tab_staged, g + 1)
            wait(pe, logit_step, 4 * (g - 2) + 1)
            for k in range(CH):
                for side in range(2):
                    mm = pe.matmul(B["ps_near"][b][:, 24 * k:24 * k + 24], B["hot_t"][:, j, k * P:(k + 1) * P],
                                   B["tab"][:, j, side, :], start=(side == 0), stop=(side == 1))
            mm.then_inc(near_made, 1)

        def total(i, c):
            j, g, b = c % RING, RING * i + c, c % 2
            if gat:
                pe.wait_ge(msg_made, g + 1)
            else:
                pe.wait_ge(hot_built, g + 1)
                pe.wait_ge(rows_in[j], 64 * (i + c // RING + 1))
            wait(pe, added, g - 1)
            for k in range(CH):
                rhs = B["msg"][:, b, k, :] if gat else B["rows"][:, j, k, :]
                mm = pe.matmul(B["ps_sum"][b][:, 0:width], B["hot"][:, j, k, :], rhs, start=(k == 0),
                               stop=(k == CH - 1))
            mm.then_inc(summed, 1)

        pace(pe, NG, [(total, 1), (look, 3)] if gat else [(total, 0)], RING)

    def dve_program(dve):
        regs = [dve.alloc_register(f"{L}dve_w{j}") for j in range(RING)]

        def add(i, c):
            g, b = RING * i + c, c % 2
            if c % RING == 0:
                dve.load(regs, K["first_w"][0:1, bass.ds(g, RING)])
            w = dve.snap(regs[c % RING], min_val=0, max_val=S.NW - 1)
            dve.wait_ge(summed, g + 1)
            wait(dve, added, g)
            for side, mask in enumerate(("in_first", "in_next")):
                to = feat[:, bass.ds(w + side, 1), 0:width].squeeze(1)
                ins = dve.scalar_tensor_tensor(out=to, in0=B["ps_sum"][b][:, 0:width],
                                               scalar=K[mask][:, one(g)], in1=to, op0=ALU.mult,
                                               op1=ALU.add)
            ins.then_inc(added, 1)

        def hots(i, c):
            j, g = c % RING, RING * i + c
            wait(dve, summed, g - 3)
            if gat:
                wait(dve, near_made, g - 3)
                dve.wait_ge(mod_in[j], 16 * (i + c // RING + 1))
                dve.tensor_scalar(B["hot_t"][:, j, :], B["mod"][:, j, :], K["part"][:, 0:1], None, ALU.is_equal)
            dve.tensor_tensor(B["hot"][:, j, :, :], K["count"][:, :].unsqueeze(1).to_broadcast([P, CH, P]),
                              at1(K["mod_t"], g).unsqueeze(2).to_broadcast([P, CH, P]),
                              ALU.is_equal).then_inc(hot_built, 1)

        def logits(i, c):
            j, g, b = c % RING, RING * i + c, c % 2
            near, logit = B["near"][:, b, :, :], B["logit"][:, b, :, :]
            dve.wait_ge(near_made, g + 1)
            link = Chain(dve, logit_step, 4 * g)
            link(dve.tensor_reduce(near, B["ps_near"][b][:, 0:24 * CH].rearrange("p (c v s) -> p c v s", c=CH, s=3),
                                   AX, ALU.add))
            dve.wait_ge(rows_in[j], 64 * (i + c // RING + 1))
            link(dve.tensor_tensor(logit, B["rows"][:, j, :, FEAT:ROW], near[:, :, 0:HEADS], ALU.add))
            link(dve.scalar_tensor_tensor(out=logit, in0=logit, scalar=SLOPE, in1=logit, op0=ALU.mult, op1=ALU.max))
            dve.tensor_tensor(logit, logit, near[:, :, HEADS:2 * HEADS], ALU.subtract).then_inc(logit_step, 1)

        def messages(i, c):
            j, g, b = c % RING, RING * i + c, c % 2
            dve.wait_ge(weighed, g + 1)
            rows = B["rows"][:, j, :, 0:FEAT].rearrange("p c (h f) -> p c h f", h=HEADS)
            out = B["msg"][:, b, :, 0:FEAT].rearrange("p c (h f) -> p c h f", h=HEADS)
            w = B["msg"][:, b, :, FEAT:ROW].unsqueeze(3).to_broadcast([P, CH, HEADS, HID])
            dve.tensor_tensor(out, rows, w, ALU.mult).then_inc(msg_made, 1)

        steps = [(messages, 1), (add, -1), (logits, 2), (hots, 3)] if gat else [(add, 0), (hots, 3)]
        pace(dve, NG, steps, RING)

    return dict(gather=gather, send_mods=send_mods, act=act_program, pe=pe_program, dve=dve_program)


def general_buffers(T, gat):
    G = dict(rel=T.sb("rel", [P, CH]), win=T.sb("win_now", [P, 1]))
    if gat:
        G.update(relb=T.sb("relb", [P, CH, P]), hot_t=T.sb("hot_tf", [P, GE]), ps_rel=T.ps("ps_rel"),
                 ps_as=T.ps("ps_as"), asb=T.sb("asb", [P, CH, P]), top=T.sb("top", [P, 1]),
                 masked=T.sb("masked", [P, GE]))
    return G


def any_edges(L, M, K, S, B, G, table, width, gat, maxima=False):
    NG, NW = S.NG, S.NW
    feat = K["feat"]
    names = ("step", "rows_in", "spread", "looked", "weighed", "summed", "window", "begun")
    step, rows_in, spread, looked, weighed, summed, window, begun = [M.sem(L + "any_" + n) for n in names]
    STEPS = 5 + 4 * HEADS if maxima else 11 if gat else 4
    rel, win = G["rel"], G["win"]

    def pairs(eng, body):
        with eng.Fori(0, NW) as w:
            with eng.Fori(0, NG) as g:
                body(w, g, w * NG + g)

    def gather(pool):
        def pair(w, g, n):
            pool.wait_ge(step, STEPS * n + 2)
            pool.sem_inc(begun, 1)
            for k in range(CH):
                pool.indirect_dma_start(B["rows"][:, 0, k, :], None, table,
                                        bass.IndirectOffsetOnAxis(ap=B["idx"][:, 0, k:k + 1], axis=0)
                                        ).then_inc(rows_in, 16)
        pairs(pool, pair)

    def act_program(act):
        def pair(w, g, n):
            act.wait_ge(step, STEPS * n + 9)
            act.activation(B["msg"][:, 0, :, FEAT:ROW], B["logit"][:, 0, :, :], ACT.Exp).then_inc(weighed, 1)
        if gat and not maxima:
            pairs(act, pair)

    def pe_program(pe):
        def row_of(ps, cols):
            for k in range(CH):
                mm = pe.matmul(ps[:, k * P:(k + 1) * P], cols[:, k, :], K["ident"][:, :], start=True, stop=True)
            return mm

        def pair(w, g, n):
            if gat:
                pe.wait_ge(step, STEPS * n + 3)
                row_of(G["ps_rel"], G["relb"]).then_inc(spread, 1)
            if maxima:
                for h in range(HEADS):
                    pe.wait_ge(step, STEPS * n + (6 + 4 * h))
                    row_of(G["ps_as"], G["asb"]).then_inc(looked, 1)
                return
            if gat:
                pe.wait_ge(step, STEPS * n + 5)
                for k in range(CH):
                    mm = pe.matmul(B["ps_near"][0][:, 8 * k:8 * k + 8], G["hot_t"][:, k * P:(k + 1) * P],
                                   at1(K["near_tab"], w), start=True, stop=True)
                mm.then_inc(looked, 1)
            pe.wait_ge(step, STEPS * n + (STEPS - 1))
            pe.wait_ge(rows_in, 64 * n + 64)
            for k in range(CH):
                rhs = B["msg"][:, 0, k, :] if gat else B["rows"][:, 0, k, :]
                mm = pe.matmul(B["ps_sum"][0][:, 0:width], B["hot"][:, 0, k, :], rhs, start=(k == 0),
                               stop=(k == CH - 1))
            mm.then_inc(summed, 1)
        pairs(pe, pair)

    def dve_program(dve):
        count = K["count"][:, :].unsqueeze(1).to_broadcast([P, CH, P])
        relc = rel[:, :].unsqueeze(2).to_broadcast([P, CH, P])

        def largest(link, w, n):
            link(dve.tensor_scalar(G["hot_t"][:, :], G["ps_rel"][:, :], K["part"][:, 0:1], None, ALU.is_equal))
            link(dve.tensor_scalar(G["hot_t"][:, :], G["hot_t"][:, :], 1.0, 1.0e30, ALU.subtract, ALU.mult))
            dve.wait_ge(rows_in, 64 * n + 64)
            for h in range(HEADS):
                a_s = B["rows"][:, 0, :, FEAT + h:FEAT + h + 1].to_broadcast([P, CH, P])
                link(dve.tensor_copy(G["asb"][:, :, :], a_s))
                dve.wait_ge(looked, HEADS * n + (h + 1))
                link(dve.tensor_tensor(G["masked"][:, :], G["ps_as"][:, :], G["hot_t"][:, :], ALU.add))
                link(dve.tensor_reduce(G["top"][:, :], G["masked"][:, :], AX, ALU.max))
                to = K["shift_src"][:, one(w), h:h + 1].squeeze(1)
                link(dve.tensor_tensor(to, to, G["top"][:, :], ALU.max))

        def sums(link, w, n):
            link(dve.tensor_tensor(B["hot"][:, 0, :, :], count, relc, ALU.is_equal))
            if gat:
                near = B["ps_near"][0][:, 0:8 * CH].rearrange("p (c v) -> p c v", c=CH)
                logit = B["logit"][:, 0, :, :]
                dve.wait_ge(spread, n + 1)
                link(dve.tensor_scalar(G["hot_t"][:, :], G["ps_rel"][:, :], K["part"][:, 0:1], None,
                                       ALU.is_equal))
                dve.wait_ge(looked, n + 1)
                dve.wait_ge(rows_in, 64 * n + 64)
                link(dve.tensor_tensor(logit, B["rows"][:, 0, :, FEAT:ROW], near[:, :, 0:HEADS], ALU.add))
                link(dve.scalar_tensor_tensor(out=logit, in0=logit, scalar=SLOPE, in1=logit, op0=ALU.mult,
                                              op1=ALU.max))
                link(dve.tensor_tensor(logit, logit, near[:, :, HEADS:2 * HEADS], ALU.subtract))
                link(dve.tensor_scalar(logit, logit, 0.0, None, ALU.min))
                dve.wait_ge(weighed, n + 1)
                out = B["msg"][:, 0, :, 0:FEAT].rearrange("p c (h f) -> p c h f", h=HEADS)
                rows = B["rows"][:, 0, :, 0:FEAT].rearrange("p c (h f) -> p c h f", h=HEADS)
                link(dve.tensor_tensor(out, rows, B["msg"][:, 0, :, FEAT:ROW].unsqueeze(3).to_broadcast(
                    [P, CH, HEADS, HID]), ALU.mult))
            dve.wait_ge(summed, n + 1)
            to = feat[:, one(w), 0:width].squeeze(1)
            link(dve.tensor_tensor(to, to, B["ps_sum"][0][:, 0:width], ALU.add))

        dve.memset(win[:, :], -1.0).then_inc(window, 1)
        with dve.Fori(0, NW) as w:
            dve.wait_ge(window, w + 1)
            dve.tensor_scalar(win[:, :], win[:, :], 1.0, None, ALU.add).then_inc(window, 1)
            with dve.Fori(0, NG) as g:
                n = w * NG + g
                link = Chain(dve, step, STEPS * n)
                dve.wait_ge(window, w + 2)
                dve.tensor_copy(B["idx"][:, 0, :], at1(K["src_t"], g))
                link(dve.tensor_scalar(rel[:, :], at1(K["win_t"], g), win[:, 0:1], float(P), ALU.subtract,
                                       ALU.mult))
                link(dve.tensor_tensor(rel[:, :], rel[:, :], at1(K["mod_t"], g), ALU.add))
                if gat:
                    link(dve.tensor_copy(G["relb"][:, :, :], relc))
                if maxima:
                    dve.wait_ge(spread, n + 1)
                    largest(link, w, n)
                else:
                    sums(link, w, n)

    return dict(gather=gather, act=act_program, pe=pe_program, dve=dve_program)


def build_edges(nc, L, M, K, S, table, mod_rows, width, gat, flag):
    with ExitStack() as scope:
        T = Mem(nc, scope, L)
        B = edge_buffers(T, width, gat)
        G = general_buffers(T, gat)
        fast = fast_edges(L, M, K, S, B, table, mod_rows, width, gat)
        slow = any_edges(L, M, K, S, B, G, table, width, gat)

        def either(eng, one_way, other_way):
            ok = eng.value_load(flag[0:1, 0:1], min_val=0, max_val=1)
            with eng.If(ok != 0):
                one_way(eng)
            if other_way:
                with eng.Else():
                    other_way(eng)

        with nc.Block() as block:
            @block.gpsimd
            def _(pool):
                either(pool, fast["gather"], slow["gather"])

            @block.scalar
            def _(act):
                either(act, fast["act"], slow["act"] if gat else None)

            @block.tensor
            def _(pe):
                either(pe, fast["pe"], slow["pe"])

            @block.vector
            def _(dve):
                either(dve, fast["dve"], slow["dve"])

            if gat:
                @block.sync
                def _(sp):
                    either(sp, fast["send_mods"], None)


def build_attention(nc, L, M, K, S, table):
    NW, NWP, NG = S.NW, S.NWP, S.NG
    feat = K["feat"]
    step, ranged, all_max, selfed = M.sem(L + "att_step"), M.sem(L + "att_ranged"), M.sem(L + "att_max"), M.sem(L + "att_self")
    shift, near = K["shift_src"], K["near_tab"]
    flag = M.sb(L + "flag", [1, 1], I32)
    a_s = feat[:, :, FEAT:ROW]
    a_d = feat[:, :, ROW:WIDE]
    with ExitStack() as scope:
        T = Mem(nc, scope, L + "att_")
        own = T.sb("own_range", [P, 2 * HEADS])
        all_ = T.sb("all_range", [P, 2 * HEADS])
        least = T.sb("least_as", [P, HEADS])
        span = T.sb("span", [P, HEADS])
        widest = T.sb("widest_span", [P, 1])
        okf = T.sb("ok_f", [1, 2])

        with nc.Block() as block:
            @block.gpsimd
            def _(pool):
                pool.wait_ge(ranged, 1)
                pool.partition_all_reduce(all_[:, :], own[:, :], P, MAX).then_inc(all_max, 1)

            @block.vector
            def _(dve):
                link = Chain(dve, step)
                by_head = feat[:, 0:NW, FEAT:ROW].rearrange("p w h -> p h w")
                dve.tensor_reduce(own[:, 0:HEADS], by_head, AX, ALU.max)
                link(dve.tensor_reduce(least[:, :], by_head, AX, ALU.min))
                dve.tensor_scalar(own[:, HEADS:2 * HEADS], least[:, :], -1.0, None, ALU.mult).then_inc(ranged, 1)
                dve.wait_ge(all_max, 1)
                dve.tensor_copy(shift[:, :, :], all_[:, 0:HEADS].unsqueeze(1).to_broadcast([P, NWP, HEADS]))
                link(dve.tensor_tensor(span[:, :], all_[:, 0:HEADS], all_[:, HEADS:2 * HEADS], ALU.add))
                dve.tensor_copy(okf[:, 1:2], K["spread_ok"][:, :])
                link(dve.tensor_reduce(widest[:, :], span[:, :], AX, ALU.max))
                link(dve.tensor_scalar(okf[:, 0:1], widest[0:1, :], SAFE, None, ALU.is_le))
                dve.tensor_tensor(flag[:, :], okf[:, 0:1], okf[:, 1:2], ALU.mult)

    with ExitStack() as scope:
        T = Mem(nc, scope, L + "att_")
        B = dict(idx=T.sb("idx", [P, 1, CH], I32), rows=T.sb("rows", [P, 1, CH, ROW]))
        G = general_buffers(T, True)
        own_max = any_edges(L + "max_", M, K, S, B, G, table, ROW, True, maxima=True)
        begun = M.sem(L + "att_begun")

        def unless_flag(eng, program):
            ok = eng.value_load(flag[0:1, 0:1], min_val=0, max_val=1)
            with eng.If(ok == 0):
                program(eng)

        with nc.Block() as block:
            @block.gpsimd
            def _(pool):
                unless_flag(pool, own_max["gather"])

            @block.tensor
            def _(pe):
                unless_flag(pe, own_max["pe"])

            @block.vector
            def _(dve):
                def program(dve):
                    dve.tensor_copy(shift[:, 0:NW, :], feat[:, 0:NW, FEAT:ROW]).then_inc(begun, 1)
                    dve.wait_ge(begun, 1)
                    own_max["dve"](dve)
                unless_flag(dve, program)

    with ExitStack() as scope:
        T = Mem(nc, scope, L + "att_")
        own_l = T.sb("own_logit", [P, NWP, HEADS])
        own_w = T.sb("own_weight", [P, NWP, HEADS])
        rest = T.sb("tab_rest", [P, NWP, 2 * HEADS])
        part = K["tab24"][:, :, :].rearrange("p w (v s) -> p w v s", s=3)
        with nc.Block() as block:
            @block.scalar
            def _(act):
                act.wait_ge(step, 9)
                act.activation(own_w[:, :, :], own_l[:, :, :], ACT.Exp).then_inc(selfed, 1)

            @block.vector
            def _(dve):
                link = Chain(dve, step, 4)
                hi = near[:, :, HEADS:2 * HEADS]
                dve.tensor_copy(near[:, :, 0:HEADS], a_d)
                dve.tensor_tensor(hi, a_d, shift[:, :, :], ALU.add)
                link(dve.tensor_tensor(own_l[:, :, :], a_s, a_d, ALU.add))
                link(dve.scalar_tensor_tensor(out=hi, in0=hi, scalar=SLOPE, in1=hi, op0=ALU.mult, op1=ALU.max))
                link(dve.scalar_tensor_tensor(out=own_l[:, :, :], in0=own_l[:, :, :], scalar=SLOPE,
                                              in1=own_l[:, :, :], op0=ALU.mult, op1=ALU.max))
                link(dve.tensor_tensor(own_l[:, :, :], own_l[:, :, :], hi, ALU.subtract))
                link(dve.tensor_scalar(own_l[:, :, :], own_l[:, :, :], 0.0, None, ALU.min))
                link(dve.tensor_copy(part[:, :, :, 0], near[:, :, :]))
                link(dve.tensor_tensor(rest[:, :, :], near[:, :, :], part[:, :, :, 0], ALU.subtract))
                link(dve.tensor_copy(part[:, :, :, 1], rest[:, :, :]))
                link(dve.tensor_tensor(rest[:, :, :], rest[:, :, :], part[:, :, :, 1], ALU.subtract))
                link(dve.tensor_copy(part[:, :, :, 2], rest[:, :, :]))
                dve.wait_ge(selfed, 1)
                body = feat[:, 0:NW, 0:FEAT].rearrange("p w (h f) -> p w h f", h=HEADS)
                dve.tensor_tensor(body, body, own_w[:, 0:NW, :].unsqueeze(3).to_broadcast([P, NW, HEADS, HID]),
                                  ALU.mult)
                dve.tensor_copy(a_s, own_w[:, :, :])
    return flag


def build_batch_norm(nc, L, M, K, S, F, bias, gamma, beta, gat):
    N, NW, WB, NB, TAIL = S.N, S.NW, S.WB, S.NB, S.TAIL
    feat = K["feat"]
    params, rec_made, step = M.sem(L + "bn_params"), M.sem(L + "bn_rec"), M.sem(L + "bn_step")
    shaped, meaned, centred = M.sem(L + "bn_shaped"), M.sem(L + "bn_meaned"), M.sem(L + "bn_centred")
    squared, used, varied, rooted = (M.sem(L + "bn_squared"), M.sem(L + "bn_used"), M.sem(L + "bn_varied"),
                                     M.sem(L + "bn_rooted"))
    scale, offset = K["bn_scale"], K["bn_offset"]
    with ExitStack() as scope:
        T = Mem(nc, scope, L)
        bias_b = T.sb("bias_b", [P, F])
        mean = T.sb("mean", [P, F])
        std = T.sb("std", [P, F])
        rec = T.sb("rec", [P, NW, HEADS])
        square = T.sb("square", [P, 2, WB, F])
        ps_m, ps_v = T.ps("ps_mean"), T.ps("ps_var")

        def batch(b, lo=0, hi=F):
            return feat[:, bass.ds(b * WB, WB), lo:hi]

        def nodes_sum(pe, ps, source, ready, done):
            pe.matmul(ps[:, 0:F], K["zeros"][:, 0:P], K["zeros"][:, 0:F], start=True, stop=False)

            def windows(b, upto, static):
                pe.wait_ge(ready, b + 1)
                for j in range(upto):
                    mm = pe.matmul(ps[:, 0:F], K["ones"][:, :], source(b, j), start=False, stop=False)
                return mm
            with pe.Fori(0, NB - 1) as b:
                mm = windows(b, WB, False)
                if done is not None:
                    mm.then_inc(done, 1)
            windows(NB - 1, WB - 1, True)
            return pe.matmul(ps[:, 0:F], K["ones"][0:TAIL, :], source(NB - 1, WB - 1)[0:TAIL], start=False, stop=True)

        with nc.Block() as block:
            @block.sync
            def _(sp):
                for to, x in ((bias_b, bias), (scale, gamma), (offset, beta)):
                    sp.dma_start(to[:, 0:F], x.rearrange("(a f) -> a f", a=1).to_broadcast([P, F])
                                 ).then_inc(params, 16)

            @block.vector
            def _(dve):
                link = Chain(dve, step)
                dve.wait_ge(params, 48)
                if gat:
                    link(dve.reciprocal(rec[:, :, :], feat[:, 0:NW, FEAT:ROW]))
                else:
                    link(dve.memset(rec[:, 0, :], 0.0))
                K_ = 2 if gat else 3
                with dve.Fori(0, NB) as b:
                    chain = Chain(dve, step, 1 + K_ * b)
                    if gat:
                        v = batch(b).rearrange("p w (h f) -> p w h f", h=HEADS)
                        chain(dve.tensor_tensor(v, v, rec[:, bass.ds(b * WB, WB), :].unsqueeze(3).to_broadcast(
                            [P, WB, HEADS, HID]), ALU.mult))
                    else:
                        chain(dve.tensor_tensor(batch(b), batch(b), K["dinv"][:, bass.ds(b * WB, WB)].unsqueeze(
                            2).to_broadcast([P, WB, F]), ALU.mult))
                    chain(dve.tensor_tensor(batch(b), batch(b), bias_b[:, :].unsqueeze(1).to_broadcast([P, WB, F]),
                                            ALU.add))
                    if not gat:
                        chain(dve.tensor_scalar(batch(b), batch(b), 0.0, None, ALU.max))
                    dve.sem_inc(shaped, 1)
                base = 1 + K_ * NB
                link = Chain(dve, step, base)
                dve.wait_ge(meaned, 1)
                link(dve.tensor_scalar(mean[:, :], ps_m[:, 0:F], 1.0 / N, None, ALU.mult))
                with dve.Fori(0, NB) as b:
                    dve.tensor_tensor(batch(b), batch(b), mean[:, :].unsqueeze(1).to_broadcast([P, WB, F]),
                                      ALU.subtract).then_inc(centred, 1)
                dve.wait_ge(rooted, 1)
                link(dve.reciprocal(std[:, :], std[:, :]))
                dve.tensor_tensor(scale[:, 0:F], scale[:, 0:F], std[:, :], ALU.mult)

            @block.scalar
            def _(act):
                def squares(i, c):
                    b = 2 * i + c
                    act.wait_ge(centred, b + 1)
                    wait(act, used, b - 1)
                    act.activation(square[:, c % 2, :, :], batch(b), ACT.Square).then_inc(squared, 1)
                pace(act, NB, [(squares, 0)])
                act.wait_ge(varied, 1)
                act.activation(std[:, :], ps_v[:, 0:F], ACT.Sqrt, scale=1.0 / N, bias=K["eps"][:, 0:1]
                               ).then_inc(rooted, 1)

            @block.tensor
            def _(pe):
                nodes_sum(pe, ps_m, lambda b, j: feat[:, one(b * WB + j), 0:F].squeeze(1), shaped, None
                          ).then_inc(meaned, 1)
                pe.matmul(ps_v[:, 0:F], K["zeros"][:, 0:P], K["zeros"][:, 0:F], start=True, stop=False)

                def add_squares(i, c):
                    b = 2 * i + c
                    pe.wait_ge(squared, b + 1)
                    tail = isinstance(i, int) and b == NB - 1
                    for j in range(WB):
                        rows = TAIL if tail and j == WB - 1 else P
                        mm = pe.matmul(ps_v[:, 0:F], K["ones"][0:rows, :], square[0:rows, c % 2, j, :],
                                       start=False, stop=rows < P or (tail and j == WB - 1))
                    mm.then_inc(used, 1)
                pace(pe, NB, [(add_squares, 0)])
                pe.matmul(ps_m[:, 0:F], K["zeros"][:, 0:P], K["zeros"][:, 0:F], start=True,
                          stop=True).then_inc(varied, 1)


def build_gat_input(nc, L, M, K, S, F, elu, W, a_src, a_dst, table):
    NW, WB, NB = S.NW, S.WB, S.NB
    feat, scale, offset = K["feat"], K["bn_scale"], K["bn_offset"]
    KP = 1 if F <= P else 2
    KF = F // KP
    sems = ("w_in", "cleared", "wt", "wt_got", "wa", "wa_got", "scaled", "shifted", "clipped", "exped", "staged",
            "turned", "copied", "product", "placed", "stored")
    (w_in, cleared, wt_made, wt_got, wa_made, wa_got, scaled, shifted, clipped, exped, staged, turned, copied,
     product, placed, stored) = [M.sem(f"{L}gat_{n}") for n in sems]
    with ExitStack() as scope:
        T = Mem(nc, scope, L)
        w = T.sb("w_gat", [P, KP, WIDE])
        wt = T.sb("w_turned", [P, 2, F])
        heads = T.sb("heads", [P, 2, 2 * HEADS])
        scl = T.sb("scl", [P, 2, F])
        shf = T.sb("shf", [P, 2, F])
        clp = T.sb("clp", [P, 2, F])
        ex = T.sb("ex", [P, 2, F])
        stage = T.sb("stage", [P, 2, KP * P])
        xt = T.sb("xt", [P, 2, KP * P])
        ps_t = [T.ps(f"pt{i}") for i in range(2)]
        ps_o = [T.ps(f"po{i}") for i in range(2)]
        ps_w, ps_a = T.ps("pw"), T.ps("pa")

        with nc.Block() as block:
            @block.sync
            def _(sp):
                sp.dma_start(w[0:KF, :, 0:FEAT], W.rearrange("(k p) f -> p k f", p=KF)).then_inc(w_in, 16)
                sp.wait_ge(cleared, 1)
                with nc.allow_non_contiguous_dma(reason="a head's 64 values down the partitions"):
                    for h in range(HEADS):
                        rows = slice(HID * (h % 2), HID * (h % 2) + HID)
                        for q, a in enumerate((a_src, a_dst)):
                            col = q * HEADS + h
                            sp.dma_start(heads[rows, h // 2, col:col + 1],
                                         a[h:h + 1, :].rearrange("a f -> f a")).then_inc(w_in, 16)
                for b in range(NB):
                    sp.wait_ge(placed, (b + 1) * WB)
                    rows = table[b * WB * P:(b + 1) * WB * P, :].rearrange("(w p) f -> p w f", p=P)
                    sp.dma_start(rows, feat[:, b * WB:(b + 1) * WB, 0:ROW]).then_inc(stored, 16)
                sp.wait_ge(stored, 16 * NB)

            @block.gpsimd
            def _(pool):
                pool.memset(heads[:, :, :], 0.0).then_inc(cleared, 1)

                def scaling(i, c):
                    n, slot = 2 * i + c, c % 2
                    wait(pool, shifted, n - 1)
                    pool.tensor_tensor(scl[:, slot, :], feat[:, one(n), 0:F].squeeze(1), scale[:, 0:F],
                                       ALU.mult).then_inc(scaled, 1)
                pace(pool, NW, [(scaling, 0)])

            @block.vector
            def _(dve):
                if F < P:
                    dve.memset(stage[:, :, F:P], 0.0)

                def widen(n, src, out, made, got):
                    dve.wait_ge(made, n)
                    dve.tensor_copy(out, src).then_inc(got, 1)
                for j in range(2):
                    for k in range(KP):
                        n = j * KP + k
                        widen(n + 1, ps_w[:, 0:KF], wt[:, j, k * KF:(k + 1) * KF], wt_made, wt_got)
                for k in range(KP):
                    widen(k + 1, ps_a[0:KF, 0:2 * HEADS], w[0:KF, k, FEAT:WIDE], wa_made, wa_got)

                def shift(i, c):
                    n, slot = 2 * i + c, c % 2
                    dve.wait_ge(scaled, n + 1)
                    to = shf if elu else stage
                    wait(dve, staged if elu else turned, n - 1)
                    dve.tensor_tensor(to[:, slot, 0:F], scl[:, slot, :], offset[:, 0:F], ALU.add
                                      ).then_inc(shifted, 1)
                    if elu:
                        dve.wait_ge(shifted, n + 1)
                        wait(dve, exped, n - 1)
                        dve.tensor_scalar(clp[:, slot, :], shf[:, slot, :], 0.0, None, ALU.min
                                          ).then_inc(clipped, 1)

                def unite(i, c):
                    n, slot = 2 * i + c, c % 2
                    dve.wait_ge(exped, n + 1)
                    wait(dve, turned, n - 1)
                    dve.scalar_tensor_tensor(out=stage[:, slot, :], in0=ex[:, slot, :], scalar=-1.0,
                                             in1=shf[:, slot, :], op0=ALU.add, op1=ALU.max).then_inc(staged, 1)
                pace(dve, NW, [(shift, 1), (unite, 0)] if elu else [(shift, 0)])

            @block.scalar
            def _(act):
                def expo(i, c):
                    n, slot = 2 * i + c, c % 2
                    act.wait_ge(clipped, n + 1)
                    wait(act, staged, n - 1)
                    act.activation(ex[:, slot, :], clp[:, slot, :], ACT.Exp).then_inc(exped, 1)

                def copy(i, c):
                    n, slot = 2 * i + c, c % 2
                    act.wait_ge(turned, n + 1)
                    wait(act, product, n - 1)
                    act.copy(xt[0:KF, slot, :], ps_t[slot][0:KF, 0:KP * P]).then_inc(copied, 1)

                def place(i, c):
                    n, slot = 2 * i + c, c % 2
                    act.wait_ge(product, n + 1)
                    act.copy(feat[:, one(n), 0:WIDE].squeeze(1), ps_o[slot][:, 0:WIDE]).then_inc(placed, 1)
                pace(act, NW, ([(expo, 2)] if elu else []) + [(copy, 1), (place, 0)])

            @block.tensor
            def _(pe):
                pe.wait_ge(w_in, 16 * (1 + 2 * HEADS))
                for j in range(2):
                    for k in range(KP):
                        n = j * KP + k
                        wait(pe, wt_got, n)
                        pe.transpose(ps_w[:, 0:KF], w[0:KF, k, j * P:(j + 1) * P], K["ident"][0:KF, 0:KF]
                                     ).then_inc(wt_made, 1)
                pe.wait_ge(wt_got, 2 * KP)
                for k in range(KP):
                    wait(pe, wa_got, k)
                    for j in range(2):
                        mm = pe.matmul(ps_a[0:KF, 0:2 * HEADS], wt[:, j, k * KF:(k + 1) * KF], heads[:, j, :],
                                       start=(j == 0), stop=(j == 1))
                    mm.then_inc(wa_made, 1)
                pe.wait_ge(wa_got, KP)
                linear(pe, K, S, (KP, KF), stage, ps_t, xt, ps_o, w, WIDE, staged if elu else shifted, turned,
                       copied, product, placed)


def build_gnn(nc, M, K, S, x, src, dst, W_gcn, gcn, gats):
    mod_rows = nc.dram_tensor("mod_rows", (S.NG, GE), BF16).ap()
    table0 = nc.dram_tensor("gcn_table", (S.NW * P, HID), F32).ap()
    K["bn_scale"], K["bn_offset"] = M.sb("bn_scale", [P, FEAT]), M.sb("bn_offset", [P, FEAT])
    build_constants(nc, M, K)
    K["feat"] = M.sb("feat", [P, S.NWP, WIDE])
    with ExitStack() as scope:
        T = Mem(nc, scope)
        K["shift_src"] = T.sb("shift_src", [P, S.NWP, HEADS])
        K["near_tab"] = T.sb("near_tab", [P, S.NWP, 2 * HEADS])
        K["tab24"] = T.sb("tab24", [P, S.NWP, 24], BF16)
        build_edge_tables(nc, T, K, S, src, dst, mod_rows)
        build_degrees(nc, T, K, S)
        build_gcn_input(nc, T, K, S, x, W_gcn, table0)
        build_edges(nc, "gcn_", T, K, S, table0, mod_rows, HID, False, K["spread_ok"])
        build_batch_norm(nc, "gcn_", T, K, S, HID, *gcn, gat=False)
        Mem.clear_signals(nc)
        for n, (W, a_src, a_dst, bias, gamma, beta) in enumerate(gats):
            L = f"gat{n}_"
            table = nc.dram_tensor(L + "table", (S.NW * P, ROW), F32).ap()
            build_gat_input(nc, L, T, K, S, W.shape[0], n > 0, W, a_src, a_dst, table)
            flag = build_attention(nc, L, T, K, S, table)
            build_edges(nc, L, T, K, S, table, mod_rows, ROW, True, flag)
            build_batch_norm(nc, L, T, K, S, FEAT, bias, gamma, beta, gat=True)
            Mem.clear_signals(nc)


def build_ffn_input(nc, M, K, S, x, gamma, beta, Wr, br, xn_rows):
    N, NW, WB, NB, TAIL, EX = S.N, S.NW, S.WB, S.NB, S.TAIL, S.EX
    feat, scale, offset = K["feat"], K["bn_scale"], K["bn_offset"]
    names = ("params x_in cleared scaled offset_in clipped exped elued joined step varied rooted staged turned "
             "copied product routed apart weighed stored").split()
    (params, x_in, cleared, scaled, offset_in, clipped, exped, elued, joined, step, varied, rooted, staged, turned,
     copied, product, routed, apart, weighed, stored) = [M.sem("ffi_" + n) for n in names]
    with ExitStack() as scope:
        T = Mem(nc, scope, "ffi_")
        xr = T.sb("xr", [P, WB, FEAT])
        z = T.sb("z", [P, 2, WB, FEAT])
        zt = T.sb("zt", [P, 2, 2, P])
        st = T.sb("st", [P, WB, 6])
        mean, var, std, rstd = [T.sb(n, [P, WB]) for n in ("mean", "var", "std", "rstd")]
        std2, rstd2 = T.sb("std2", [P, WB]), T.sb("rstd2", [P, WB])
        gm, bt = T.sb("gm", [P, FEAT]), T.sb("bt", [P, FEAT])
        wr = T.sb("wr", [P, 2, EX])
        brb = T.sb("brb", [P, EX])
        lg, eq, score = T.sb("lg", [P, WB, EX]), T.sb("eq", [P, WB, EX]), T.sb("score", [P, WB, EX])
        largest, first = T.sb("largest", [P, 2, WB]), T.sb("first", [P, WB])
        diff, ge, gs = T.sb("diff", [P, WB]), T.sb("ge", [P, WB]), T.sb("gs", [P, WB])
        ps_t = [T.ps(f"pt{i}") for i in range(2)]
        ps_l = T.ps("pl")

        def body(b):
            return feat[:, b * WB:(b + 1) * WB, 0:FEAT]

        def every(v):
            return v[:, :].unsqueeze(1).to_broadcast([P, WB, v.shape[1]])

        def by_expert(v):
            return v.unsqueeze(2).to_broadcast([P, WB, EX])

        with nc.Block() as block:
            @block.sync
            def _(sp):
                for to, v in ((gm, gamma), (bt, beta), (brb, br)):
                    sp.dma_start(to[:, :], v.rearrange("(a f) -> a f", a=1).to_broadcast(
                        [P, v.shape[0]])).then_inc(params, 16)
                sp.dma_start(wr[:, :, :], Wr.rearrange("(k p) e -> p k e", p=P)).then_inc(params, 16)
                sp.wait_ge(cleared, 1)
                for b in range(NB + 1):
                    if b < NB:
                        wait(sp, joined, b)
                        w0, w1 = b * WB, min((b + 1) * WB, NW - 1)
                        sp.dma_start(xr[:, 0:w1 - w0, :],
                                     x[w0 * P:w1 * P, :].rearrange("(w p) f -> p w f", p=P)).then_inc(x_in, 16)
                        if b == NB - 1:
                            sp.dma_start(xr[0:TAIL, WB - 1, :], x[(NW - 1) * P:N, :]).then_inc(x_in, 16)
                    if b:
                        sp.wait_ge(staged, b)
                        rows = xn_rows[(b - 1) * WB * P:b * WB * P, :].rearrange("(w p) f -> p w f", p=P)
                        sp.dma_start(rows, z[:, (b - 1) % 2, :, :]).then_inc(stored, 16)
                sp.wait_ge(stored, 16 * NB)

            @block.gpsimd
            def _(pool):
                pool.memset(xr[:, :, :], 0.0).then_inc(cleared, 1)

                def scaling(b):
                    pool.tensor_tensor(body(b), body(b), every(scale), ALU.mult).then_inc(scaled, 1)
                scaling(0)
                for b in range(NB):
                    if b + 1 < NB:
                        scaling(b + 1)
                    pool.wait_ge(elued, b + 1)
                    pool.wait_ge(x_in, 16 * (b + 1 + (b == NB - 1)))
                    pool.tensor_tensor(body(b), body(b), xr[:, :, :], ALU.add).then_inc(joined, 1)

            @block.vector
            def _(dve):
                dve.wait_ge(params, 64)
                link = Chain(dve, step)

                def add_offset(b):
                    dve.wait_ge(scaled, b + 1)
                    dve.tensor_tensor(body(b), body(b), every(offset), ALU.add).then_inc(offset_in, 1)

                def elu(b):
                    dve.wait_ge(exped, b + 1)
                    dve.wait_ge(offset_in, b + 1)
                    dve.scalar_tensor_tensor(out=body(b), in0=z[:, b % 2, :, :], scalar=-1.0, in1=body(b),
                                             op0=ALU.add, op1=ALU.max).then_inc(elued, 1)

                def norm(b):
                    zb = z[:, b % 2, :, :]
                    dve.wait_ge(joined, b + 1)
                    for w in range(WB):
                        ins = dve.bn_stats(st[:, w, :], body(b)[:, w, :])
                    link(ins)
                    spread_of(dve, link, st, mean[:, :], var[:, :])
                    dve.sem_inc(varied, 1)
                    dve.wait_ge(rooted, 2 * b + 1)
                    link(dve.reciprocal(rstd[:, :], std[:, :]))
                    link(dve.tensor_tensor(var[:, :], var[:, :], rstd[:, :], ALU.mult))
                    link(dve.tensor_tensor(var[:, :], var[:, :], rstd[:, :], ALU.mult))
                    dve.sem_inc(varied, 1)
                    dve.wait_ge(rooted, 2 * b + 2)
                    link(dve.reciprocal(rstd2[:, :], std2[:, :]))
                    link(dve.tensor_tensor(rstd[:, :], rstd[:, :], rstd2[:, :], ALU.mult))
                    for w in range(WB):
                        ins = dve.tensor_scalar(zb[:, w, :], body(b)[:, w, :], mean[:, w:w + 1], rstd[:, w:w + 1],
                                                ALU.subtract, ALU.mult)
                    link(ins)
                    link(dve.tensor_tensor(zb, zb, every(gm), ALU.mult))
                    dve.tensor_tensor(zb, zb, every(bt), ALU.add).then_inc(staged, 1)

                def choose(b):
                    at = slice(b * WB, (b + 1) * WB)
                    count8 = K["count"][:, 0:EX].unsqueeze(1).to_broadcast([P, WB, EX])
                    dve.wait_ge(routed, b + 1)
                    link(dve.tensor_tensor(lg[:, :, :], ps_l[:, 0:WB * EX].rearrange("p (w e) -> p w e", e=EX),
                                           every(brb), ALU.add))
                    for n, hot in enumerate((K["hot1"], K["hot2"])):
                        link(dve.tensor_reduce(largest[:, n, :], lg[:, :, :], AX, ALU.max))
                        link(dve.tensor_tensor(eq[:, :, :], lg[:, :, :], by_expert(largest[:, n, :]), ALU.is_equal))
                        link(dve.scalar_tensor_tensor(out=score[:, :, :], in0=eq[:, :, :], scalar=-float(EX),
                                                      in1=count8, op0=ALU.mult, op1=ALU.add))
                        link(dve.tensor_reduce(first[:, :], score[:, :, :], AX, ALU.min))
                        link(dve.tensor_tensor(hot[:, at, :], score[:, :, :], by_expert(first[:, :]), ALU.is_equal))
                        if n == 0:
                            link(dve.scalar_tensor_tensor(out=lg[:, :, :], in0=hot[:, at, :], scalar=-1.0e30,
                                                          in1=lg[:, :, :], op0=ALU.mult, op1=ALU.add))
                    dve.tensor_tensor(diff[:, :], largest[:, 1, :], largest[:, 0, :], ALU.subtract
                                      ).then_inc(apart, 1)
                    dve.wait_ge(weighed, b + 1)
                    link(dve.tensor_scalar(gs[:, :], ge[:, :], 1.0, None, ALU.add))
                    link(dve.reciprocal(K["weight1"][:, at], gs[:, :]))
                    link(dve.tensor_tensor(K["weight2"][:, at], ge[:, :], K["weight1"][:, at], ALU.mult))

                add_offset(0)
                elu(0)
                for b in range(NB):
                    if b + 1 < NB:
                        add_offset(b + 1)
                    norm(b)
                    if b + 1 < NB:
                        elu(b + 1)
                    choose(b)

            @block.scalar
            def _(act):
                def expo(b):
                    zb = z[:, b % 2, :, :]
                    act.wait_ge(offset_in, b + 1)
                    wait(act, turned, (b - 1) * WB)
                    wait(act, stored, 16 * (b - 1))
                    act.activation(zb, body(b), ACT.Relu, scale=-1.0).then_inc(clipped, 1)
                    act.wait_ge(clipped, b + 1)
                    act.activation(zb, zb, ACT.Exp, scale=-1.0).then_inc(exped, 1)
                expo(0)
                for b in range(NB):
                    if b + 1 < NB:
                        expo(b + 1)
                    for n, to in enumerate((std, std2)):
                        act.wait_ge(varied, 2 * b + n + 1)
                        act.activation(to[:, :], var[:, :], ACT.Sqrt, bias=K["eps"][:, 0:1]).then_inc(rooted, 1)
                    for w in range(WB):
                        n = b * WB + w
                        act.wait_ge(turned, n + 1)
                        wait(act, product, n - 1)
                        act.copy(zt[:, n % 2, :, :], ps_t[n % 2][:, 0:2 * P].rearrange(
                            "p (k t) -> p k t", k=2)).then_inc(copied, 1)
                    act.wait_ge(apart, b + 1)
                    act.activation(ge[:, :], diff[:, :], ACT.Exp).then_inc(weighed, 1)

            @block.tensor
            def _(pe):
                pe.wait_ge(params, 64)
                for b in range(NB):
                    pe.wait_ge(staged, b + 1)
                    for w in range(WB + 1):
                        n = b * WB + w
                        if w < WB:
                            wait(pe, copied, n - 1)
                            for k in range(2):
                                mm = pe.transpose(ps_t[n % 2][:, k * P:(k + 1) * P],
                                                  z[:, b % 2, w, k * P:(k + 1) * P], K["ident"][:, :])
                            mm.then_inc(turned, 1)
                        if w:
                            pe.wait_ge(copied, n)
                            for k in range(2):
                                mm = pe.matmul(ps_l[:, (w - 1) * EX:w * EX], zt[:, (n - 1) % 2, k, :],
                                               wr[:, k, :], start=(k == 0), stop=(k == 1))
                            mm.then_inc(product, 1)
                    pe.matmul(ps_l[:, WB * EX:WB * EX + 8], K["zeros"][:, 0:P], K["zeros"][:, 0:8], start=True,
                              stop=True).then_inc(routed, 1)


def build_routing(nc, M, K, S):
    NW, EX, NS = S.NW, S.EX, S.NS
    HALF = NW // 2
    hots = (K["hot1"], K["hot2"])
    names = "counted step tri_in both_in sums_in built used token_in".split()
    counted, step, tri_in, both_in, sums_in, built, used, token_in = [M.sem("route_" + n) for n in names]
    with ExitStack() as scope:
        T = Mem(nc, scope, "route_")
        NUM = max(NS, P)
        num_i, num, num_b = T.sb("num_i", [P, NUM], I32), T.sb("num", [P, NUM]), T.sb("num_b", [P, NUM], BF16)
        tri = T.sb("tri", [P, P])
        both = T.sb("both", [P, NW, EX])
        own = T.sb("own", [P, NW, EX])
        upto = [T.sb(f"upto{i}", [P, NW, EX]) for i in range(2)]
        slot = T.sb("slot", [P, NW, EX])
        picked = T.sb("picked", [P, NW, EX])
        tokens, chunks, ends = T.sb("tokens", [P, EX]), T.sb("chunks", [P, EX]), [T.sb(f"ends{i}", [P, EX])
                                                                               for i in range(2)]
        tok_i, base = T.sb("tok_i", [P, EX], I32), T.sb("base", [P, EX])
        past, which = T.sb("past", [1, NS, EX - 1]), T.sb("which", [1, NS])
        slot_f = T.sb("slot_f", [P, NW, 2])
        chunk_i, place_i = T.sb("chunk_i", [P, NW, 2], I32), T.sb("place_i", [P, NW, 2], I32)
        chunk, place = T.sb("chunk", [P, NW, 2]), T.sb("place", [P, NW, 2])
        hot_p = T.sb("hot_p", [P, 2, 2, P], BF16)
        hot_w = T.sb("hot_w", [P, 2, 2, P], BF16)
        hot_c = T.sb("hot_c", [P, 2, 2, NS], BF16)
        token_f = T.sb("token_f", [P, NS])
        ps_own = [T.ps(f"own{i}") for i in range(2)]
        ps_pre = [T.ps(f"pre{i}") for i in range(2)]
        ps_p, ps_w = T.ps("p"), T.ps("w")

        def half(v, i):
            return v[:, i * HALF:(i + 1) * HALF, :]

        def halves(ps, i):
            return ps[i][:, 0:HALF * EX].rearrange("p (w e) -> p w e", e=EX)

        with nc.Block() as block:
            @block.gpsimd
            def _(pool):
                pool.iota(num_i[:, :], pattern=[[1, NUM]], base=0, channel_multiplier=0).then_inc(counted, 1)

            @block.tensor
            def _(pe):
                pe.wait_ge(both_in, 1)
                pe.wait_ge(tri_in, 1)
                for i in range(2):
                    pe.matmul(ps_own[i][:, 0:HALF * EX], K["ones"][:, :], half(both, i), start=True, stop=True)
                for i in range(2):
                    mm = pe.matmul(ps_pre[i][:, 0:HALF * EX], tri[:, :], half(both, i), start=True, stop=True)
                mm.then_inc(sums_in, 1)
                for ps in (ps_p, ps_w):
                    pe.matmul(ps[:, 0:NS], K["zeros"][:, 0:P], K["zeros"][:, 0:NS], start=True, stop=False)

                def places(i, b):
                    pe.wait_ge(built, 2 * i + b + 1)
                    for n in range(2):
                        pe.matmul(ps_p[:, 0:NS], hot_p[:, b, n, :], hot_c[:, b, n, :], start=False, stop=False)
                        mm = pe.matmul(ps_w[:, 0:NS], hot_w[:, b, n, :], hot_c[:, b, n, :], start=False, stop=False)
                    mm.then_inc(used, 1)
                pace(pe, NW, [(places, 0)])
                for ps in (ps_p, ps_w):
                    mm = pe.matmul(ps[:, 0:NS], K["zeros"][:, 0:P], K["zeros"][:, 0:NS], start=False, stop=True)
                mm.then_inc(token_in, 1)

            @block.vector
            def _(dve):
                link = Chain(dve, step)
                dve.tensor_scalar(tri[:, :], K["count"][:, :], K["part"][:, 0:1], None, ALU.is_gt).then_inc(tri_in, 1)
                dve.tensor_tensor(both[:, :, :], hots[0][:, :, :], hots[1][:, :, :], ALU.add).then_inc(both_in, 1)
                dve.wait_ge(counted, 1)
                dve.tensor_copy(num[:, :], num_i[:, :])
                dve.tensor_copy(num_b[:, :], num_i[:, :])
                dve.wait_ge(sums_in, 1)
                for i in range(2):
                    dve.tensor_copy(half(own, i), halves(ps_own, i))
                    ins = dve.tensor_copy(half(upto[0], i), halves(ps_own, i))
                link(ins)
                n, d = 0, 1
                while d < NW:
                    a, b = upto[n % 2], upto[(n + 1) % 2]
                    dve.tensor_copy(b[:, 0:d, :], a[:, 0:d, :])
                    link(dve.tensor_tensor(b[:, d:NW, :], a[:, d:NW, :], a[:, 0:NW - d, :], ALU.add))
                    n, d = n + 1, 2 * d
                total = upto[n % 2]
                link(dve.tensor_scalar(tokens[:, :], total[:, NW - 1, :], float(P - 1), None, ALU.add))
                link(dve.tensor_copy(tok_i[:, :], tokens[:, :]))
                link(dve.tensor_scalar(tok_i[:, :], tok_i[:, :], 7, None, ALU.logical_shift_right))
                dve.tensor_copy(ends[0][:, :], tok_i[:, :])
                link(dve.tensor_copy(chunks[:, :], tok_i[:, :]))
                m, d = 0, 1
                while d < EX:
                    a, b = ends[m % 2], ends[(m + 1) % 2]
                    dve.tensor_copy(b[:, 0:d], a[:, 0:d])
                    link(dve.tensor_tensor(b[:, d:EX], a[:, d:EX], a[:, 0:EX - d], ALU.add))
                    m, d = m + 1, 2 * d
                end = ends[m % 2]
                dve.tensor_tensor(past[:, :, :], num[0:1, 0:NS].unsqueeze(2).to_broadcast([1, NS, EX - 1]),
                                  end[0:1, 0:EX - 1].unsqueeze(1).to_broadcast([1, NS, EX - 1]), ALU.is_ge)
                link(dve.tensor_tensor(base[:, :], end[:, :], chunks[:, :], ALU.subtract))
                dve.tensor_reduce(which[:, :], past[:, :, :], AX, ALU.add)
                link(dve.tensor_scalar(base[:, :], base[:, :], float(P), None, ALU.mult))
                dve.tensor_copy(K["expert_of"][:, :], which[:, :])
                link(dve.tensor_tensor(slot[:, :, :], total[:, :, :], own[:, :, :], ALU.subtract))
                for i in range(2):
                    ins = dve.tensor_tensor(half(slot, i), half(slot, i), halves(ps_pre, i), ALU.add)
                link(ins)
                link(dve.tensor_tensor(slot[:, :, :], slot[:, :, :],
                                       base[:, :].unsqueeze(1).to_broadcast([P, NW, EX]), ALU.add))
                for i in range(2):
                    link(dve.tensor_tensor(picked[:, :, :], slot[:, :, :], hots[i][:, :, :], ALU.mult))
                    link(dve.tensor_reduce(slot_f[:, :, i], picked[:, :, :], AX, ALU.add))
                link(dve.tensor_copy(K["slot_of"][:, :, :], slot_f[:, :, :]))
                dve.tensor_scalar(chunk_i[:, :, :], K["slot_of"][:, :, :], 7, None, ALU.logical_shift_right)
                link(dve.tensor_scalar(place_i[:, :, :], K["slot_of"][:, :, :], P - 1, None, ALU.bitwise_and))
                dve.tensor_copy(chunk[:, :, :], chunk_i[:, :, :])
                link(dve.tensor_copy(place[:, :, :], place_i[:, :, :]))

                def marks(i, b):
                    w = 2 * i + b
                    wait(dve, used, w - 1)
                    for n in range(2):
                        at = at1(place, w)[:, n:n + 1]
                        dve.tensor_scalar(hot_p[:, b, n, :], num_b[:, 0:P], at, K["part"][:, 0:1], ALU.is_equal,
                                          ALU.mult)
                        dve.tensor_scalar(hot_w[:, b, n, :], num_b[:, 0:P], at, num[:, one(w)], ALU.is_equal,
                                          ALU.mult)
                        ins = dve.tensor_scalar(hot_c[:, b, n, :], num_b[:, 0:NS], at1(chunk, w)[:, n:n + 1], None,
                                                ALU.is_equal)
                    ins.then_inc(built, 1)
                pace(dve, NW, [(marks, 0)])
                dve.wait_ge(token_in, 1)
                link(dve.tensor_copy(token_f[:, :], ps_p[:, 0:NS]))
                dve.scalar_tensor_tensor(out=K["token_of"][:, :], in0=ps_w[:, 0:NS], scalar=float(P),
                                         in1=token_f[:, :], op0=ALU.mult, op1=ALU.add)


def build_experts(nc, M, K, S, W1, b1, W2, b2, xn_rows, y_rows):
    EX, HD, NS = S.EX, S.HD, S.NS
    HB = HD // P
    with ExitStack() as scope:
        T = Mem(nc, scope, "ffn_")
        up_all = T.sb("up_all", [P, EX, 2 * HD + HB])
        up_now = T.sb("up_now", [P, 2, 2 * HD + HB])
        w2 = T.sb("w2", [P, EX, HB, FEAT])
        b2b = T.sb("b2b", [P, EX, FEAT])
        b1r = T.sb("b1r", [EX * HB, P])
        idx = T.sb("idx", [P, RING], I32)
        xg = T.sb("xg", [P, RING, FEAT])
        xt = T.sb("xt", [P, 2, 2, P])
        h = T.sb("h", [P, 2, HB, P])
        y = T.sb("y", [P, 2, FEAT])
        ps_t = [T.ps(f"pt{i}") for i in range(2)]
        ps_h = [T.ps(f"ph{i}") for i in range(2)]
        ps_y = [T.ps(f"py{i}") for i in range(2)]
        names = "w1_in w2_in b1_in b1_turned b1_got staged begun turned fed up acted down placed".split()
        (w1_in, w2_in, b1_in, b1_turned, b1_got, staged, begun, turned, fed, up, acted, down,
         placed) = [M.sem("ffn_" + n) for n in names]
        gathered = [M.sem(f"ffn_gathered{j}") for j in range(RING)]
        stored = [M.sem(f"ffn_stored{j}") for j in range(2)]

        with nc.Block() as block:
            @block.sync
            def _(sp):
                sp.dma_start(b1r[:, :], b1.rearrange("e (k p) -> (e k) p", p=P)).then_inc(b1_in, 16)
                for e in range(EX):
                    sp.dma_start(up_all[:, e, 0:2 * HD].rearrange("p (k h) -> p k h", k=2),
                                 W1[e].rearrange("(k p) h -> p k h", p=P)).then_inc(w1_in, 16)
                for e in range(EX):
                    sp.dma_start(w2[:, e, :, :], W2[e].rearrange("(k p) f -> p k f", p=P)).then_inc(w2_in, 16)
                    sp.dma_start(b2b[:, e, :], b2[e:e + 1, :].to_broadcast([P, FEAT])).then_inc(w2_in, 16)

                def store(i, c):
                    s = RING * i + c
                    sp.wait_ge(placed, s + 1)
                    sp.dma_start(y_rows[bass.ds(s * P, P), :], y[:, c % 2, :]).then_inc(stored[c % 2], 16)
                pace(sp, NS, [(store, 0)], RING)
                for j in range(2):
                    sp.wait_ge(stored[j], 16 * (NS // 2))

            @block.gpsimd
            def _(pool):
                def gather(i, c):
                    s = RING * i + c
                    pool.wait_ge(staged, s + 1)
                    wait(pool, turned, s - (RING - 1))
                    pool.sem_inc(begun, 1)
                    pool.indirect_dma_start(xg[:, c, :], None, xn_rows,
                                            bass.IndirectOffsetOnAxis(ap=idx[:, c:c + 1], axis=0)
                                            ).then_inc(gathered[c], 16)
                pace(pool, NS, [(gather, 0)], RING)

            @block.tensor
            def _(pe):
                regs = [pe.alloc_register(f"ffn_pe_e{j}") for j in range(RING)]
                pe.wait_ge(b1_in, 16)
                pe.transpose(ps_y[0][:, 0:EX * HB], b1r[:, :], K["ident"][0:EX * HB, 0:EX * HB]
                             ).then_inc(b1_turned, 1)

                def turn(i, c):
                    j, s, b = c % RING, RING * i + c, c % 2
                    pe.wait_ge(gathered[j], 16 * (i + c // RING + 1))
                    wait(pe, fed, s - 1)
                    for k in range(2):
                        mm = pe.transpose(ps_t[b][:, k * P:(k + 1) * P], xg[:, j, k * P:(k + 1) * P],
                                          K["ident"][:, :])
                    mm.then_inc(turned, 1)

                def upward(i, c):
                    s, b = RING * i + c, c % 2
                    pe.wait_ge(fed, s + 1)
                    wait(pe, acted, s - 1)
                    for k in range(HB):
                        for d in range(2):
                            mm = pe.matmul(ps_h[b][:, k * P:(k + 1) * P],
                                           up_now[:, b, d * HD + k * P:d * HD + (k + 1) * P], xt[:, b, d, :],
                                           start=(d == 0), stop=(d == 1))
                    mm.then_inc(up, 1)

                def downward(i, c):
                    s, b = RING * i + c, c % 2
                    if c % RING == 0:
                        pe.load(regs, K["expert_of"][0:1, bass.ds(s, RING)])
                    e = pe.snap(regs[c % RING], min_val=0, max_val=EX - 1)
                    if isinstance(s, int) and s == 0:
                        pe.wait_ge(w2_in, 32 * EX)
                    pe.wait_ge(acted, s + 1)
                    wait(pe, placed, s - 1)
                    for k in range(HB):
                        mm = pe.matmul(ps_y[b][:, 0:FEAT], h[:, b, k, :],
                                       w2[:, bass.ds(e, 1), k, :].squeeze(1), start=(k == 0), stop=(k == HB - 1))
                    mm.then_inc(down, 1)
                pace(pe, NS, [(turn, 2), (upward, 1), (downward, 0)], RING)

            @block.scalar
            def _(act):
                def stage(i, c):
                    j, s = c % RING, RING * i + c
                    wait(act, gathered[j], 16 * (i + c // RING))
                    act.copy(idx[:, j:j + 1], K["token_of"][:, one(s)]).then_inc(staged, 1)

                def gelus(i, c):
                    s, b = RING * i + c, c % 2
                    wait(act, down, s - 1)
                    act.wait_ge(up, s + 1)
                    for k in range(HB):
                        ins = act.activation(h[:, b, k, :], ps_h[b][:, k * P:(k + 1) * P], ACT.Gelu,
                                             bias=up_now[:, b, 2 * HD + k:2 * HD + k + 1])
                    ins.then_inc(acted, 1)
                pace(act, NS, [(gelus, 0), (stage, RING + 1)], RING)

            @block.vector
            def _(dve):
                up_regs = [dve.alloc_register(f"ffn_up_e{j}") for j in range(RING)]
                down_regs = [dve.alloc_register(f"ffn_down_e{j}") for j in range(RING)]
                dve.wait_ge(b1_turned, 1)
                dve.wait_ge(w1_in, 16 * EX)
                dve.tensor_copy(up_all[:, :, 2 * HD:], ps_y[0][:, 0:EX * HB].rearrange("p (e k) -> p e k", k=HB)
                                ).then_inc(b1_got, 1)
                dve.wait_ge(b1_got, 1)
                dve.wait_ge(w2_in, 32 * EX)

                def feed(i, c):
                    s, b = RING * i + c, c % 2
                    if c % RING == 0:
                        dve.load(up_regs, K["expert_of"][0:1, bass.ds(s, RING)])
                    e = dve.snap(up_regs[c % RING], min_val=0, max_val=EX - 1)
                    wait(dve, acted, s - 1)
                    dve.tensor_copy(up_now[:, b, :], up_all[:, bass.ds(e, 1), :].squeeze(1))
                    dve.wait_ge(turned, s + 1)
                    dve.tensor_copy(xt[:, b, :, :], ps_t[b][:, 0:2 * P].rearrange("p (k t) -> p k t", k=2)
                                    ).then_inc(fed, 1)

                def take(i, c):
                    s, b = RING * i + c, c % 2
                    if c % RING == 0:
                        dve.load(down_regs, K["expert_of"][0:1, bass.ds(s, RING)])
                    e = dve.snap(down_regs[c % RING], min_val=0, max_val=EX - 1)
                    dve.wait_ge(down, s + 1)
                    wait(dve, stored[b], 16 * (RING // 2 * i + c // 2))
                    dve.tensor_tensor(y[:, b, :], ps_y[b][:, 0:FEAT], b2b[:, bass.ds(e, 1), :].squeeze(1),
                                      ALU.add).then_inc(placed, 1)
                pace(dve, NS, [(take, -1), (feed, 2)], RING)


def build_combine(nc, M, K, S, y_rows, out):
    N, NW, TAIL = S.N, S.NW, S.TAIL
    feat = K["feat"]
    names = "staged begun joined added stored".split()
    staged, begun, joined, added, stored = [M.sem("mix_" + n) for n in names]
    gathered = [M.sem(f"mix_gathered{j}") for j in range(RING)]
    with ExitStack() as scope:
        T = Mem(nc, scope, "mix_")
        idx = T.sb("idx", [P, RING, 2], I32)
        rows = T.sb("rows", [P, RING, 2, FEAT])

        with nc.Block() as block:
            @block.scalar
            def _(act):
                def stage(i, c):
                    j, w = c % RING, RING * i + c
                    wait(act, gathered[j], 32 * (i + c // RING))
                    act.copy(idx[:, j, :], at1(K["slot_of"], w)).then_inc(staged, 1)
                pace(act, NW, [(stage, 0)], RING)

            @block.gpsimd
            def _(pool):
                def gather(i, c):
                    w = RING * i + c
                    pool.wait_ge(staged, w + 1)
                    wait(pool, added, w - (RING - 1))
                    pool.sem_inc(begun, 1)
                    for n in range(2):
                        pool.indirect_dma_start(rows[:, c, n, :], None, y_rows,
                                                bass.IndirectOffsetOnAxis(ap=idx[:, c, n:n + 1], axis=0)
                                                ).then_inc(gathered[c], 16)
                pace(pool, NW, [(gather, 0)], RING)

            @block.vector
            def _(dve):
                def mix(i, c):
                    w = RING * i + c
                    v = feat[:, one(w), 0:FEAT].squeeze(1)
                    dve.wait_ge(gathered[c], 32 * (i + 1))
                    dve.scalar_tensor_tensor(out=v, in0=rows[:, c, 0, :], scalar=K["weight1"][:, one(w)], in1=v,
                                             op0=ALU.mult, op1=ALU.add).then_inc(joined, 1)
                    dve.wait_ge(joined, w + 1)
                    dve.scalar_tensor_tensor(out=v, in0=rows[:, c, 1, :], scalar=K["weight2"][:, one(w)], in1=v,
                                             op0=ALU.mult, op1=ALU.add).then_inc(added, 1)
                pace(dve, NW, [(mix, 0)], RING)

            @block.sync
            def _(sp):
                with sp.Fori(0, NW // 2 - 1) as t:
                    sp.wait_ge(added, 2 * t + 2)
                    sp.dma_start(out[bass.ds(t * 2 * P, 2 * P), :].rearrange("(w p) f -> p w f", p=P),
                                 feat[:, bass.ds(t * 2, 2), 0:FEAT]).then_inc(stored, 16)
                sp.wait_ge(added, NW)
                sp.dma_start(out[(NW - 2) * P:(NW - 1) * P, :], feat[:, NW - 2, 0:FEAT]).then_inc(stored, 16)
                sp.dma_start(out[(NW - 1) * P:N, :], feat[0:TAIL, NW - 1, 0:FEAT]).then_inc(stored, 16)
                sp.wait_ge(stored, 16 * (NW // 2 + 1))


def build(nc, x, src, dst, gnn, ffn, out):
    W_gcn, b_gcn, g0, beta0, W1, a_src1, a_dst1, b1, g1, beta1, W2, a_src2, a_dst2, b2, g2, beta2 = gnn
    gamma, beta, Wr, br, F1, c1, F2, c2 = ffn
    S = Shapes(x.shape[0], src.shape[0], Wr.shape[1], F1.shape[2])
    xn_rows = nc.dram_tensor("xn_rows", (S.NW * P, FEAT), F32).ap()
    y_rows = nc.dram_tensor("y_rows", (S.NS * P, FEAT), F32).ap()
    with ExitStack() as ctx:
        M, K = Mem(nc, ctx), {}
        build_gnn(nc, M, K, S, x, src, dst, W_gcn, (b_gcn, g0, beta0),
                  [(W1, a_src1, a_dst1, b1, g1, beta1), (W2, a_src2, a_dst2, b2, g2, beta2)])
        K["slot_of"] = M.sb("slot_of", [P, S.NW, 2], I32)
        K["token_of"] = M.sb("token_of", [P, S.NS], I32)
        K["expert_of"] = M.sb("expert_of", [1, S.NS], I32)
        for n in (1, 2):
            K[f"weight{n}"] = M.sb(f"weight{n}", [P, S.NW])
        with ExitStack() as scope:
            T = Mem(nc, scope)
            for n in (1, 2):
                K[f"hot{n}"] = T.sb(f"hot{n}", [P, S.NW, S.EX])
            build_ffn_input(nc, T, K, S, x, gamma, beta, Wr, br, xn_rows)
            build_routing(nc, T, K, S)
        build_experts(nc, M, K, S, F1, c1, F2, c2, xn_rows, y_rows)
        build_combine(nc, M, K, S, y_rows, out)


_GNN = ["W_gcn", "b_gcn", "g0", "beta0", "W1", "a_src1", "a_dst1", "b1", "g1", "beta1", "W2", "a_src2", "a_dst2",
        "b2", "g2", "beta2"]
_FFN = ["gamma", "beta", "Wr", "br", "W1", "b1", "W2", "b2"]
_INS = ["x", "src", "dst"] + ["L0_gnn_" + n for n in _GNN] + ["L0_ffn_" + n for n in _FFN]


def kernel(**inputs):
    import numpy as _np
    import concourse.bacc as _bacc
    from concourse import mybir as _mybir
    from concourse.bass_utils import run_bass_kernel_spmd as _run

    nc = _bacc.Bacc("TRN2", target_bir_lowering=False, num_devices=1)
    arrays, args = {}, []
    for name in _INS:
        a = _np.ascontiguousarray(inputs[name])
        arrays[f"in_{name}_dram"] = a
        args.append(nc.dram_tensor(f"in_{name}_dram", a.shape, _mybir.dt.from_np(a.dtype),
                                   kind="ExternalInput").ap())
    shape = inputs["x"].shape
    out = nc.dram_tensor("out_0_dram", tuple(shape), _mybir.dt.float32, kind="ExternalOutput").ap()
    n = 3 + len(_GNN)
    build(nc, *args[:3], args[3:n], args[n:], out)
    r = _run(nc, [arrays], core_ids=[0])
    return r.results[0]["out_0_dram"]
```

```python
from contextlib import ExitStack

import concourse.bass as bass
from concourse import mybir

P = 128
F32 = mybir.dt.float32
BF16 = mybir.dt.bfloat16
I32 = mybir.dt.int32
ALU = mybir.AluOpType
ACT = mybir.ActivationFunctionType
AX = mybir.AxisListType.X
MAX = bass.bass_isa.ReduceOp.max

HEADS, HID = 4, 64
FEAT = HEADS * HID
ROW = FEAT + HEADS
WIDE = FEAT + 2 * HEADS
CH = 4
GE = CH * P
RING = 4
SLOPE = 0.2
EPS = 1e-5
SAFE = 60.0
NOWHERE = -1.0e6


class Chain:

    def __init__(self, eng, sem, start=0):
        self.eng, self.sem, self.start, self.n = eng, sem, start, 0

    def __call__(self, ins):
        ins.then_inc(self.sem, 1)
        self.n += 1
        self.eng.wait_ge(self.sem, self.start + self.n)


def pace(eng, n, steps, ring=2):
    leads = [lead for _, lead in steps]
    low, high = -max(leads), n - min(leads)
    first = -(-(ring + max(0, -min(leads))) // ring)
    last = (n - max(leads)) // ring

    def turn(i, c, known):
        for fn, lead in steps:
            if not known or 0 <= ring * i + c + lead < n:
                fn(i, c + lead)

    first, last = (first, last) if last - first >= 2 else (n, n)
    for t in range(low, min(first * ring, high)):
        turn(t // ring, t % ring, True)
    if first < n:
        with eng.Fori(first, last) as i:
            for c in range(ring):
                turn(i, c, False)
        for t in range(last * ring, high):
            turn(t // ring, t % ring, True)


class Mem:

    taken = []

    def __init__(self, nc, ctx, stage=""):
        self.nc, self.ctx, self.stage = nc, ctx, stage

    def sb(self, name, shape, dt=F32):
        return self.ctx.enter_context(self.nc.sbuf_tensor(self.stage + name, shape, dt))

    def ps(self, name, shape=(P, 512), dt=F32):
        return self.ctx.enter_context(self.nc.psum_tensor(self.stage + name, list(shape), dt))

    def sem(self, name):
        handle = self.nc.alloc_semaphore(name=name)
        Mem.taken.append(handle)
        return handle

    @staticmethod
    def clear_signals(nc):
        nc.clear_and_free_semaphores(Mem.taken)
        nc.all_engine_barrier()
        Mem.taken = []


class Shapes:
    def __init__(self, n, e, experts, hidden):
        self.N, self.E = n, e
        self.NW = -(-n // P)
        self.TAIL = n - (self.NW - 1) * P
        self.NWP = -(-(self.NW + 1) // 4) * 4
        self.NG = -(-e // GE)
        self.LAST = e - (self.NG - 1) * GE
        self.NT = -(-self.NG // P)
        self.GT = self.NG // self.NT
        self.WB = next(b for b in (14, 7, 4, 2) if self.NW % b == 0)
        self.NB = self.NW // self.WB
        self.EX, self.HD = experts, hidden
        self.NS = -(-(2 * self.NW + experts - 1) // 4) * 4
        assert self.NS <= 256 and 2 * self.NW <= 256
        assert self.NB % 2 or self.NB < 4
        assert self.NG % 8 == 0 and self.NG // 8 >= self.NW // 2
        assert self.NG % 4 == 0 and self.GT * self.NT == self.NG and self.NW % 2 == 0


def wait(eng, sem, count):
    if not isinstance(count, int) or count > 0:
        eng.wait_ge(sem, count)


def spread_of(dve, link, st, mean, var):
    link(dve.tensor_tensor(var, st[:, :, 1], st[:, :, 4], ALU.subtract))
    link(dve.tensor_tensor(mean, st[:, :, 1], st[:, :, 4], ALU.add))
    link(dve.tensor_scalar(mean, mean, 0.5, None, ALU.mult))
    link(dve.scalar_tensor_tensor(out=var, in0=var, scalar=0.25, in1=var, op0=ALU.mult, op1=ALU.mult))
    link(dve.scalar_tensor_tensor(out=var, in0=st[:, :, 2], scalar=1.0 / FEAT, in1=var, op0=ALU.mult,
                                  op1=ALU.add))
    link(dve.scalar_tensor_tensor(out=var, in0=st[:, :, 5], scalar=1.0 / FEAT, in1=var, op0=ALU.mult,
                                  op1=ALU.add))


def one(n):
    return bass.ds(n, 1)


def at1(t, n):
    return t[:, bass.ds(n, 1), :].squeeze(1)


def build_constants(nc, M, K, S):
    ident = M.sb("ident", [P, P])
    ones = M.sb("ones", [P, P])
    zeros = M.sb("zeros", [P, 512])
    count_i = M.sb("count_i", [P, P], I32)
    count = M.sb("count", [P, P])
    part_i = M.sb("part_i", [P, 1], I32)
    part = M.sb("part", [P, 1])
    eps = M.sb("eps", [P, 1])
    real = M.sb("real", [P, 1])
    K.update(ident=ident, ones=ones, zeros=zeros, count=count, part=part, eps=eps, real=real)
    filled, counted = M.sem("const_filled"), M.sem("const_counted")
    with nc.Block() as block:
        @block.gpsimd
        def _(pool):
            pool.memset(ident[:, :], 0.0).then_inc(filled, 1)
            pool.wait_ge(filled, 1)
            pool.affine_select(out=ident[:, :], in_=ident[:, :], compare_op=ALU.not_equal, fill=1.0, base=0,
                               pattern=[[-1, P]], channel_multiplier=1)
            pool.iota(count_i[:, :], pattern=[[1, P]], base=0, channel_multiplier=0)
            pool.iota(part_i[:, :], pattern=[[1, 1]], base=0, channel_multiplier=1).then_inc(counted, 1)

        @block.vector
        def _(dve):
            dve.memset(ones[:, :], 1.0)
            dve.memset(zeros[:, :], 0.0)
            dve.memset(eps[:, :], EPS)
            dve.wait_ge(counted, 1)
            dve.tensor_copy(count[:, :], count_i[:, :])
            dve.tensor_copy(part[:, :], part_i[:, :]).then_inc(counted, 1)
            dve.wait_ge(counted, 2)
            dve.tensor_scalar(real[:, :], part[:, :], float(S.TAIL), None, ALU.is_lt)


def build_edge_tables(nc, M, K, S, src, dst, mod_rows):
    E, NG, NT, GT, LAST = S.E, S.NG, S.NT, S.GT, S.LAST
    src_t = M.sb("src_t", [P, NG, CH], I32)
    mod_t = M.sb("mod_t", [P, NG, CH])
    win_t = M.sb("win_t", [P, NG, CH])
    first_w = M.sb("first_w", [P, NG], I32)
    in_first = M.sb("in_first", [P, NG])
    in_next = M.sb("in_next", [P, NG])
    spread_ok = M.sb("spread_ok", [1, 1], I32)
    lw = M.sb("lead_w", [GT, NT])
    K.update(src_t=src_t, mod_t=mod_t, win_t=win_t, first_w=first_w, in_first=in_first, in_next=in_next,
             spread_ok=spread_ok, lead_w=lw)
    loaded_d, loaded_s, filled = M.sem("edge_dst_loaded"), M.sem("edge_src_loaded"), M.sem("edge_filled")
    step, rows_ready, padded = M.sem("edge_step"), M.sem("edge_rows_ready"), M.sem("edge_padded")
    stored, turned, taken = M.sem("edge_mod_stored"), M.sem("edge_turned"), M.sem("edge_taken")
    spread_max, spread_in = M.sem("edge_spread_max"), M.sem("edge_spread_in")
    with ExitStack() as scope:
        T = Mem(nc, scope)
        raw_d = T.sb("raw_d", [GT, NT, GE], I32)
        raw_s = T.sb("raw_s", [GT, NT, GE], I32)
        win_i = T.sb("win_i", [GT, NT, GE], I32)
        mod_i = T.sb("mod_i", [GT, NT, GE], I32)
        flat = K["feat"][0:GT, :, :].rearrange("p w f -> p (w f)")
        f_dst, f_src, f_win = [flat[:, n * NT * GE:(n + 1) * NT * GE].rearrange("p (t e) -> p t e", t=NT)
                               for n in range(3)]
        f_mod = T.sb("f_mod", [GT, NT, GE])
        b_mod = T.sb("b_mod", [GT, NT, GE], BF16)
        least = T.sb("least", [GT, NT])
        most = T.sb("most", [GT, NT])
        least_i = T.sb("least_i", [GT, NT], I32)
        lw_i = T.sb("lw_i", [GT, NT], I32)
        lm_i = T.sb("lm_i", [GT, NT], I32)
        lm = T.sb("lm", [GT, NT])
        wide = T.sb("wide", [GT, 1])
        widest = T.sb("widest", [GT, 1])
        spread1 = T.sb("spread1", [1, 1])
        lwb = T.sb("lwb", [GT, NT, P])
        lmb = T.sb("lmb", [GT, NT, P])
        nowhere = T.sb("nowhere", [1, GE])
        turn = [T.ps(f"turn{i}") for i in range(2)]

        def rows(x, t, full):
            return x[t * GT * GE:(t * GT + full) * GE].rearrange("(g e) -> g e", e=GE)

        @nc_block(nc)
        def _(block):
            @block.sync
            def _(sp):
                for raw, x, got in ((raw_d, dst, loaded_d), (raw_s, src, loaded_s)):
                    if raw is raw_s:
                        sp.wait_ge(filled, 1)
                    for t in range(NT):
                        full = GT if t < NT - 1 else GT - 1
                        if full:
                            sp.dma_start(raw[0:full, t, :], rows(x, t, full)).then_inc(got, 16)
                    tail = x[(NG - 1) * GE:E].rearrange("(a e) -> a e", a=1)
                    sp.dma_start(raw[GT - 1:GT, NT - 1, 0:LAST], tail).then_inc(got, 16)
                if LAST < GE:
                    before = dst[(NG - 1) * GE - (GE - LAST):(NG - 1) * GE].rearrange("(a e) -> a e", a=1)
                    sp.dma_start(raw_d[GT - 1:GT, NT - 1, LAST:GE], before).then_inc(loaded_d, 16)
                sp.wait_ge(rows_ready, 1)
                for t in range(NT):
                    sp.dma_start(mod_rows[t * GT:(t + 1) * GT, :], b_mod[:, t, :]).then_inc(stored, 16)
                if LAST < GE:
                    sp.dma_start(f_mod[GT - 1:GT, NT - 1, LAST:GE], nowhere[0:1, LAST:GE]).then_inc(padded, 16)
                sp.wait_ge(stored, 16 * NT)

            @block.gpsimd
            def _(pool):
                pool.memset(raw_s[:, NT - 1, :], 0).then_inc(filled, 1)
                pool.wait_ge(spread_in, 1)
                pool.partition_all_reduce(widest[:, :], wide[:, :], GT, MAX).then_inc(spread_max, 1)

            @block.vector
            def _(dve):
                link = Chain(dve, step)
                dve.memset(nowhere[:, :], NOWHERE)
                dve.wait_ge(loaded_d, 16 * (NT - (GT == 1) + 1 + (LAST < GE)))
                dve.tensor_scalar(win_i[:, :, :], raw_d[:, :, :], 7, None, ALU.logical_shift_right)
                dve.tensor_scalar(mod_i[:, :, :], raw_d[:, :, :], P - 1, None, ALU.bitwise_and)
                link(dve.tensor_copy(f_dst[:, :, :], raw_d[:, :, :]))
                dve.tensor_copy(f_win[:, :, :], win_i[:, :, :])
                dve.tensor_copy(f_mod[:, :, :], mod_i[:, :, :])
                dve.tensor_copy(b_mod[:, :, :], mod_i[:, :, :]).then_inc(rows_ready, 1)
                dve.tensor_reduce(least[:, :], f_dst[:, :, :], AX, ALU.min)
                link(dve.tensor_reduce(most[:, :], f_dst[:, :, :], AX, ALU.max))
                dve.tensor_copy(least_i[:, :], least[:, :])
                link(dve.tensor_tensor(most[:, :], most[:, :], least[:, :], ALU.subtract))
                dve.tensor_reduce(wide[:, :], most[:, :], AX, ALU.max).then_inc(spread_in, 1)
                dve.tensor_scalar(lw_i[:, :], least_i[:, :], 7, None, ALU.logical_shift_right)
                link(dve.tensor_scalar(lm_i[:, :], least_i[:, :], P - 1, None, ALU.bitwise_and))
                dve.tensor_copy(lw[:, :], lw_i[:, :])
                link(dve.tensor_copy(lm[:, :], lm_i[:, :]))
                dve.tensor_copy(lwb[:, :, :], lw[:, :].unsqueeze(2).to_broadcast([GT, NT, P]))
                dve.tensor_copy(lmb[:, :, :], lm[:, :].unsqueeze(2).to_broadcast([GT, NT, P]))
                dve.wait_ge(loaded_s, 16 * (NT - (GT == 1) + 1))
                dve.tensor_copy(f_src[:, :, :], raw_s[:, :, :]).then_inc(rows_ready, 1)
                dve.wait_ge(spread_max, 1)
                dve.tensor_scalar(spread1[:, :], widest[0:1, :], float(P - 1), None, ALU.is_le).then_inc(rows_ready, 1)
                dve.wait_ge(rows_ready, 3)
                dve.tensor_copy(spread_ok[:, :], spread1[:, :])
                n = 0
                for t in range(NT):
                    g = slice(t * GT, (t + 1) * GT)
                    for f, out in ((f_src, src_t), (f_win, win_t), (f_mod, mod_t)):
                        dve.wait_ge(turned, n + 1)
                        v = turn[n % 2][:, 0:CH * GT].rearrange("p (c g) -> p g c", c=CH)
                        dve.tensor_copy(out[:, g, :], v).then_inc(taken, 1)
                        n += 1
                    dve.wait_ge(turned, n + 1)
                    lo, hi = turn[n % 2][:, 0:GT], turn[n % 2][:, P:P + GT]
                    dve.tensor_copy(first_w[:, g], lo)
                    dve.tensor_scalar(in_first[:, g], hi, K["part"][:, 0:1], None, ALU.is_le)
                    dve.tensor_scalar(in_next[:, g], hi, K["part"][:, 0:1], None, ALU.is_gt).then_inc(taken, 1)
                    n += 1

            @block.tensor
            def _(pe):
                n = 0
                pe.wait_ge(rows_ready, 3)
                if LAST < GE:
                    pe.wait_ge(padded, 16)
                for t in range(NT):
                    for f in (f_src, f_win, f_mod):
                        if n >= 2:
                            pe.wait_ge(taken, n - 1)
                        for c in range(CH):
                            mm = pe.transpose(turn[n % 2][:, c * GT:(c + 1) * GT], f[:, t, c * P:(c + 1) * P],
                                              K["ident"][0:GT, 0:GT])
                        mm.then_inc(turned, 1)
                        n += 1
                    if n >= 2:
                        pe.wait_ge(taken, n - 1)
                    pe.matmul(turn[n % 2][:, 0:GT], lwb[:, t, :], K["ident"][0:GT, 0:GT], start=True, stop=True)
                    pe.matmul(turn[n % 2][:, P:P + GT], lmb[:, t, :], K["ident"][0:GT, 0:GT],
                              start=True, stop=True).then_inc(turned, 1)
                    n += 1


def nc_block(nc):
    def run(body):
        with nc.Block() as block:
            body(block)
    return run


def when(eng, flag, wanted, program):
    value = eng.value_load(flag[0:1, 0:1], min_val=0, max_val=1)
    with eng.If(value != 0 if wanted else value == 0):
        program(eng)


def build_any_degrees(nc, M, K, S):
    NG, NW = S.NG, S.NW
    ok = K["spread_ok"]
    built, used, done, step = M.sem("deg_built"), M.sem("deg_used"), M.sem("deg_done"), M.sem("deg_step")
    Q = 4 * CH
    with ExitStack() as scope:
        T = Mem(nc, scope)
        cb = T.sb("deg_count", [P, P], BF16)
        mb = T.sb("deg_mod", [P, NG * CH], BF16)
        wb = T.sb("deg_win", [P, NG * CH], BF16)
        hot_m = T.sb("hot_m", [P, 2, Q, P], BF16)
        hot_w = T.sb("hot_w", [P, 2, Q, NW], BF16)
        zb = T.sb("deg_zero", [P, P], BF16)
        acc = T.ps("deg_ps")

        @nc_block(nc)
        def _(block):
            @block.vector
            def _(dve):
                def program(dve):
                    link = Chain(dve, step)
                    dve.memset(zb[:, :], 0.0).then_inc(built, 1)
                    dve.tensor_copy(cb[:, :], K["count"][:, :])
                    dve.tensor_copy(mb[:, :], K["mod_t"][:, :, :].rearrange("p g c -> p (g c)"))
                    link(dve.tensor_copy(wb[:, :], K["win_t"][:, :, :].rearrange("p g c -> p (g c)")))

                    def hots(i, b):
                        t = 2 * i + b
                        at = bass.ds(t * Q, Q)
                        wait(dve, used, t - 1)
                        dve.tensor_tensor(hot_m[:, b, :, :], cb[:, :].unsqueeze(1).to_broadcast([P, Q, P]),
                                          mb[:, at].unsqueeze(2).to_broadcast([P, Q, P]), ALU.is_equal)
                        dve.tensor_tensor(hot_w[:, b, :, :], cb[:, 0:NW].unsqueeze(1).to_broadcast([P, Q, NW]),
                                          wb[:, at].unsqueeze(2).to_broadcast([P, Q, NW]),
                                          ALU.is_equal).then_inc(built, 1)

                    hots(0, 0)
                    hots(0, 1)
                    with dve.Fori(1, NG // 8) as i:
                        hots(i, 0)
                        hots(i, 1)
                    dve.wait_ge(done, 1)
                    dve.tensor_copy(K["deg"][:, :], acc[:, 0:NW])
                when(dve, ok, False, program)

            @block.tensor
            def _(pe):
                def program(pe):
                    pe.wait_ge(built, 1)
                    pe.matmul(acc[:, 0:NW], zb[:, :], zb[:, 0:NW], start=True, stop=False)
                    with pe.Fori(0, NG // 8) as i:
                        for b in range(2):
                            pe.wait_ge(built, 2 * i + b + 2)
                            for q in range(Q):
                                mm = pe.matmul(acc[:, 0:NW], hot_m[:, b, q, :], hot_w[:, b, q, :], start=False,
                                               stop=False)
                            mm.then_inc(used, 1)
                    pe.matmul(acc[:, 0:NW], zb[:, :], zb[:, 0:NW], start=False,
                              stop=True).then_inc(done, 1)
                when(pe, ok, False, program)


def build_gcn_input(nc, M, K, S, x, W_gcn, mod_rows):
    N, NW, NWP, TAIL, WB, NB, NG = S.N, S.NW, S.NWP, S.TAIL, S.WB, S.NB, S.NG
    EIGHT = 8
    MINE = 6
    NO = NG // EIGHT
    feat = K["feat"]
    cleared, w_in, step = M.sem("gi_cleared"), M.sem("gi_weights"), M.sem("gi_step")
    x_in = [M.sem(f"gi_x{b}") for b in range(NB)]
    mods_in = [M.sem(f"gi_mods{b}") for b in range(RING)]
    counted, apart, act_counted = M.sem("gi_counted"), M.sem("gi_apart"), M.sem("gi_act_counted")
    rooted, scaled = M.sem("gi_rooted"), M.sem("gi_scaled")
    staged, turned, copied = M.sem("gi_staged"), M.sem("gi_turned"), M.sem("gi_copied")
    product, placed = M.sem("gi_product"), M.sem("gi_placed")
    with ExitStack() as scope:
        T = Mem(nc, scope)
        wg = T.sb("w_gcn", [P, 2, HID])
        st = T.sb("gi_st", [P, NW, 6])
        mean, var = T.sb("gi_mean", [P, NW]), T.sb("gi_var", [P, NW])
        std = T.sb("gi_std", [P, NW])
        rstd = T.sb("gi_rstd", [P, NW])
        stage = T.sb("gi_stage", [P, 2, FEAT])
        xt = T.sb("gi_xt", [P, 2, FEAT])
        mods = T.sb("gi_mods", [P, RING, EIGHT, GE], BF16)
        equal = T.sb("gi_equal", [P, MINE, GE], BF16)
        away = T.sb("gi_away", [P, EIGHT - MINE, GE], BF16)
        same = T.sb("gi_same", [P, EIGHT - MINE, GE], BF16)
        less_p = T.sb("gi_less_p", [P, 1])
        ps_t = [T.ps(f"gi_pt{i}") for i in range(2)]
        ps_o = [T.ps(f"gi_po{i}") for i in range(2)]

        @nc_block(nc)
        def _(block):
            @block.sync
            def _(sp):
                sp.wait_ge(cleared, 1)
                for b in range(NB):
                    w0, w1 = b * WB, min((b + 1) * WB, NW - 1)
                    sp.dma_start(feat[:, w0:w1, 0:FEAT],
                                 x[w0 * P:w1 * P, :].rearrange("(w p) f -> p w f", p=P)).then_inc(x_in[b], 16)
                sp.dma_start(feat[0:TAIL, NW - 1, 0:FEAT], x[(NW - 1) * P:N, :]).then_inc(x_in[NB - 1], 16)
                sp.dma_start(wg[:, :, :], W_gcn.rearrange("(k p) f -> p k f", p=P)).then_inc(w_in, 16)

                def spread(i, c):
                    o = RING * i + c
                    wait(sp, counted, MINE * (o - (RING - 1)))
                    wait(sp, act_counted, o - (RING - 1))
                    rows = mod_rows[bass.ds(o * EIGHT, EIGHT), :].rearrange("(a g) e -> a (g e)", a=1)
                    sp.dma_start(mods[:, c, :, :].rearrange("p g e -> p (g e)"),
                                 rows.to_broadcast([P, EIGHT * GE])).then_inc(mods_in[c], 16)
                pace(sp, NO, [(spread, 0)], RING)

            @block.vector
            def _(dve):
                dve.memset(feat[:, NW - 1:NWP, :], 0.0).then_inc(cleared, 1)
                dve.tensor_scalar(less_p[:, :], K["part"][:, :], -1.0, None, ALU.mult)
                link = Chain(dve, step)
                for b in range(NB):
                    dve.wait_ge(x_in[b], 16 * (1 + (b == NB - 1)))
                    for w in range(b * WB, (b + 1) * WB):
                        ins = dve.bn_stats(st[:, w, :], feat[:, w, 0:FEAT])
                ins.then_inc(scaled, 1)
                dve.wait_ge(scaled, 1)
                spread_of(dve, link, st, mean[:, :], var[:, :])
                dve.wait_ge(rooted, 1)
                link(dve.reciprocal(rstd[:, :], std[:, :]))

                def puts(i, c):
                    for slot in range(2):
                        w = 2 * RING * i + 2 * c + slot
                        wait(dve, turned, w - 1)
                        dve.tensor_scalar(stage[:, slot, :], feat[:, bass.ds(w, 1), 0:FEAT].squeeze(1),
                                          mean[:, one(w)], rstd[:, bass.ds(w, 1)],
                                          ALU.subtract, ALU.mult).then_inc(staged, 1)

                def takes(i, c):
                    for slot in range(2):
                        w = 2 * RING * i + 2 * c + slot
                        dve.wait_ge(product, w + 1)
                        dve.wait_ge(staged, w + 1)
                        dve.tensor_scalar(feat[:, bass.ds(w, 1), 0:HID].squeeze(1), ps_o[slot][:, 0:HID],
                                          1.0, None, ALU.mult).then_inc(placed, 1)

                def counts(i, c):
                    o = RING * i + c
                    dve.wait_ge(mods_in[c % RING], 16 * (i + c // RING + 1))
                    wait(dve, counted, MINE * o)
                    for q in range(MINE):
                        dve.tensor_scalar(equal[:, q, :], mods[:, c % RING, q, :], K["part"][:, 0:1], 0.0,
                                          ALU.is_equal, ALU.add,
                                          accum_out=K["tally"][:, one(EIGHT * o + q)]).then_inc(counted, 1)

                pace(dve, NW // 2, [(puts, 1), (counts, 0), (takes, 0)], RING)
                for o in range(NW // 2, NO):
                    counts(o // RING, o % RING)
                if S.LAST < GE:
                    dve.wait_ge(counted, MINE * NO)
                    dve.wait_ge(act_counted, NO)
                    dve.tensor_scalar(equal[:, 0, 0:S.LAST], mods[:, (NO - 1) % RING, EIGHT - 1, 0:S.LAST],
                                      K["part"][:, 0:1], 0.0, ALU.is_equal, ALU.add,
                                      accum_out=K["tally"][:, NG - 1:NG])

            @block.scalar
            def _(act):
                act.wait_ge(step, 6)
                act.activation(std[:, :], var[:, :], ACT.Sqrt, bias=K["eps"][:, 0:1]).then_inc(rooted, 1)

                def copies(i, c):
                    for slot in range(2):
                        w = 2 * RING * i + 2 * c + slot
                        act.wait_ge(turned, w + 1)
                        wait(act, product, w - 1)
                        act.copy(xt[:, slot, :], ps_t[slot][:, 0:FEAT]).then_inc(copied, 1)

                def counts(i, c):
                    o = RING * i + c
                    act.wait_ge(mods_in[c % RING], 16 * (i + c // RING + 1))
                    wait(act, act_counted, o)
                    act.activation(away[:, :, :], mods[:, c % RING, MINE:EIGHT, :], ACT.Abs, bias=less_p[:, 0:1]
                                   ).then_inc(apart, 1)
                    act.wait_ge(apart, o + 1)
                    for q in range(MINE, EIGHT):
                        ins = act.activation(same[:, q - MINE, :], away[:, q - MINE, :], ACT.Relu, scale=-1.0,
                                             bias=K["ones"][:, 0:1], accum_out=K["tally"][:, one(EIGHT * o + q)])
                    ins.then_inc(act_counted, 1)

                pace(act, NW // 2, [(copies, 0), (counts, 0)], RING)
                for o in range(NW // 2, NO):
                    counts(o // RING, o % RING)

            @block.tensor
            def _(pe):
                pe.wait_ge(w_in, 16)
                linear(pe, K, S, 2, stage, ps_t, xt, ps_o, wg, HID, staged, turned, copied, product, placed)


def build_fast_degrees(nc, M, K, S):
    NG, NW, NT, GT = S.NG, S.NW, S.NT, S.GT
    ok, tally = K["spread_ok"], K["tally"]
    names = "masked window_known turned taken done".split()
    masked, windows, turned, taken, done = [M.sem("fd_" + n) for n in names]
    with ExitStack() as scope:
        T = Mem(nc, scope, "fd_")
        share = T.sb("share", [P, 2, NG])
        at = T.sb("at", [GT, NT, 2, NW])
        next_w = T.sb("next_w", [GT, NT])
        rows = T.sb("rows", [GT, NT, 2, P])
        ps_t = [T.ps(f"pt{i}") for i in range(2)]
        acc = T.ps("acc")

        @nc_block(nc)
        def _(block):
            @block.vector
            def _(dve):
                def program(dve):
                    dve.tensor_tensor(share[:, 0, :], tally[:, :], K["in_first"][:, :], ALU.mult)
                    dve.tensor_tensor(share[:, 1, :], tally[:, :], K["in_next"][:, :], ALU.mult).then_inc(masked, 1)
                    dve.tensor_scalar(next_w[:, :], K["lead_w"][:, :], 1.0, None, ALU.add).then_inc(windows, 1)
                    dve.wait_ge(windows, 1)
                    for side, w in enumerate((K["lead_w"], next_w)):
                        dve.tensor_tensor(at[:, :, side, :],
                                          K["count"][0:GT, 0:NW].unsqueeze(1).to_broadcast([GT, NT, NW]),
                                          w[:, :].unsqueeze(2).to_broadcast([GT, NT, NW]), ALU.is_equal)
                    for t in range(NT):
                        dve.wait_ge(turned, t + 1)
                        dve.tensor_copy(rows[:, t, :, :], ps_t[t % 2][0:GT, 0:2 * P].rearrange(
                            "g (s p) -> g s p", s=2)).then_inc(taken, 1)
                    dve.wait_ge(done, 1)
                    dve.tensor_copy(K["deg"][:, :], acc[:, 0:NW])
                when(dve, ok, True, program)

            @block.tensor
            def _(pe):
                def program(pe):
                    pe.wait_ge(masked, 1)
                    for t in range(NT):
                        wait(pe, taken, t - 1)
                        for side in range(2):
                            mm = pe.transpose(ps_t[t % 2][0:GT, side * P:(side + 1) * P],
                                              share[:, side, t * GT:(t + 1) * GT], K["ident"][:, :])
                        mm.then_inc(turned, 1)
                    pe.wait_ge(taken, NT)
                    for t in range(NT):
                        for side in range(2):
                            mm = pe.matmul(acc[:, 0:NW], rows[:, t, side, :], at[:, t, side, :],
                                           start=(t + side == 0), stop=(t == NT - 1 and side == 1))
                    mm.then_inc(done, 1)
                when(pe, ok, True, program)


def build_gcn_table(nc, M, K, S, table):
    WB, NB = S.WB, S.NB
    feat = K["feat"]
    dinv = K["dinv"]
    step, rooted, placed, stored = [M.sem("gt_" + n) for n in "step rooted placed stored".split()]
    with nc.Block() as block:
        @block.vector
        def _(dve):
            link = Chain(dve, step)
            link(dve.tensor_scalar(K["deg"][:, :], K["deg"][:, :], 1.0, 1.0, ALU.add, ALU.max))
            dve.wait_ge(rooted, 1)
            link(dve.reciprocal(dinv[:, :], K["deg"][:, :]))
            for b in range(NB):
                v = feat[:, b * WB:(b + 1) * WB, 0:HID]
                dve.tensor_tensor(v, v, dinv[:, b * WB:(b + 1) * WB].unsqueeze(2).to_broadcast([P, WB, HID]),
                                  ALU.mult).then_inc(placed, 1)

        @block.scalar
        def _(act):
            act.wait_ge(step, 1)
            act.activation(K["deg"][:, :], K["deg"][:, :], ACT.Sqrt).then_inc(rooted, 1)

        @block.sync
        def _(sp):
            for b in range(NB):
                sp.wait_ge(placed, b + 1)
                rows = table[b * WB * P:(b + 1) * WB * P, :].rearrange("(w p) f -> p w f", p=P)
                sp.dma_start(rows, feat[:, b * WB:(b + 1) * WB, 0:HID]).then_inc(stored, 16)
            sp.wait_ge(stored, 16 * NB)


def linear(pe, K, S, parts, stage, ps_t, xt, ps_o, weights, width, staged, turned, copied, product, placed):
    def turn(i, c):
        w, slot = 2 * i + c, c % 2
        pe.wait_ge(staged, w + 1)
        wait(pe, copied, w - 1)
        for k in range(parts):
            mm = pe.transpose(ps_t[slot][:, k * P:k * P + P], stage[:, slot, k * P:k * P + P], K["ident"][:, :])
        mm.then_inc(turned, 1)

    def multiply(i, c):
        w, slot = 2 * i + c, c % 2
        pe.wait_ge(copied, w + 1)
        wait(pe, placed, w - 1)
        for k in range(parts):
            mm = pe.matmul(ps_o[slot][:, 0:width], xt[:, slot, k * P:k * P + P], weights[:, k, 0:width],
                           start=(k == 0), stop=(k == parts - 1))
        mm.then_inc(product, 1)

    pace(pe, S.NW, [(turn, 1), (multiply, 0)])


def edge_buffers(T, width, gat):
    B = dict(idx=T.sb("idx", [P, RING, CH], I32), rows=T.sb("rows", [P, RING, CH, width]),
             hot=T.sb("hot", [P, RING, CH, P]), ps_sum=[T.ps(f"ps_sum{i}") for i in range(2)])
    if gat:
        B.update(mod=T.sb("mod", [P, RING, GE], BF16), hot_t=T.sb("hot_t", [P, RING, GE], BF16),
                 tab=T.sb("tab", [P, RING, 2, 24], BF16), near=T.sb("near", [P, 2, CH, 2 * HEADS]),
                 logit=T.sb("logit", [P, 2, CH, HEADS]), msg=T.sb("msg", [P, 2, CH, ROW]),
                 ps_near=[T.ps(f"ps_near{i}") for i in range(2)])
    return B


def fast_edges(L, M, K, S, B, table, mod_rows, width, gat):
    NG = S.NG
    feat = K["feat"]
    idx_staged, begun = M.sem(L + "idx_staged"), M.sem(L + "begun")
    rows_in = [M.sem(f"{L}rows_in{j}") for j in range(RING)]
    hot_built, summed, added = M.sem(L + "hot_built"), M.sem(L + "summed"), M.sem(L + "added")
    if gat:
        mod_in = [M.sem(f"{L}mod_in{j}") for j in range(RING)]
        tab_staged, near_made = M.sem(L + "tab_staged"), M.sem(L + "near_made")
        logit_step, weighed, msg_made = M.sem(L + "logit_step"), M.sem(L + "weighed"), M.sem(L + "msg_made")
    rows_used = msg_made if gat else summed

    def gather(pool):
        def group(i, c):
            g = RING * i + c
            pool.wait_ge(idx_staged, g + 1)
            wait(pool, rows_used, g - 3)
            pool.sem_inc(begun, 1)
            for k in range(CH):
                pool.indirect_dma_start(B["rows"][:, c, k, :], None, table,
                                        bass.IndirectOffsetOnAxis(ap=B["idx"][:, c, k:k + 1], axis=0)
                                        ).then_inc(rows_in[c], 16)
        pace(pool, NG, [(group, 0)], RING)

    def send_mods(sp):
        def group(i, c):
            g = RING * i + c
            wait(sp, hot_built, g - 3)
            sp.dma_start(B["mod"][:, c, :], mod_rows[one(g), :].to_broadcast([P, GE])).then_inc(mod_in[c], 16)
        pace(sp, NG, [(group, 0)], RING)

    def act_program(act):
        regs = [act.alloc_register(f"{L}act_w{j}") for j in range(RING)]

        def stage(i, c):
            j, g = c % RING, RING * i + c
            wait(act, rows_in[j], 64 * (i + c // RING))
            act.copy(B["idx"][:, j, :], at1(K["src_t"], g)).then_inc(idx_staged, 1)
            if not gat:
                return
            wait(act, near_made, g - 3)
            if j == 0:
                act.load(regs, K["first_w"][0:1, bass.ds(g, RING)])
            w = act.snap(regs[j], min_val=0, max_val=S.NW - 1)
            for side, mask in enumerate(("in_first", "in_next")):
                ins = act.activation(B["tab"][:, j, side, :], K["tab24"][:, bass.ds(w + side, 1), :].squeeze(1),
                                     ACT.Copy, scale=K[mask][:, one(g)])
            ins.then_inc(tab_staged, 1)

        def weigh(i, c):
            g = RING * i + c
            act.wait_ge(logit_step, 4 * g + 4)
            wait(act, summed, g - 1)
            act.activation(B["msg"][:, c % 2, :, FEAT:ROW], B["logit"][:, c % 2, :, :], ACT.Exp).then_inc(weighed, 1)

        pace(act, NG, [(weigh, 2), (stage, RING + 2)] if gat else [(stage, RING)], RING)

    def pe_program(pe):
        def look(i, c):
            j, g, b = c % RING, RING * i + c, c % 2
            pe.wait_ge(hot_built, g + 1)
            pe.wait_ge(tab_staged, g + 1)
            wait(pe, logit_step, 4 * (g - 2) + 1)
            for k in range(CH):
                for side in range(2):
                    mm = pe.matmul(B["ps_near"][b][:, 24 * k:24 * k + 24], B["hot_t"][:, j, k * P:(k + 1) * P],
                                   B["tab"][:, j, side, :], start=(side == 0), stop=(side == 1))
            mm.then_inc(near_made, 1)

        def total(i, c):
            j, g, b = c % RING, RING * i + c, c % 2
            if gat:
                pe.wait_ge(msg_made, g + 1)
            else:
                pe.wait_ge(hot_built, g + 1)
                pe.wait_ge(rows_in[j], 64 * (i + c // RING + 1))
            wait(pe, added, g - 1)
            for k in range(CH):
                rhs = B["msg"][:, b, k, :] if gat else B["rows"][:, j, k, :]
                mm = pe.matmul(B["ps_sum"][b][:, 0:width], B["hot"][:, j, k, :], rhs, start=(k == 0),
                               stop=(k == CH - 1))
            mm.then_inc(summed, 1)

        pace(pe, NG, [(total, 1), (look, 3)] if gat else [(total, 0)], RING)

    def dve_program(dve):
        regs = [dve.alloc_register(f"{L}dve_w{j}") for j in range(RING)]

        def add(i, c):
            g, b = RING * i + c, c % 2
            if c % RING == 0:
                dve.load(regs, K["first_w"][0:1, bass.ds(g, RING)])
            w = dve.snap(regs[c % RING], min_val=0, max_val=S.NW - 1)
            dve.wait_ge(summed, g + 1)
            wait(dve, added, g)
            for side, mask in enumerate(("in_first", "in_next")):
                to = feat[:, bass.ds(w + side, 1), 0:width].squeeze(1)
                ins = dve.scalar_tensor_tensor(out=to, in0=B["ps_sum"][b][:, 0:width],
                                               scalar=K[mask][:, one(g)], in1=to, op0=ALU.mult,
                                               op1=ALU.add)
            ins.then_inc(added, 1)

        def hots(i, c):
            j, g = c % RING, RING * i + c
            wait(dve, summed, g - 3)
            if gat:
                wait(dve, near_made, g - 3)
                dve.wait_ge(mod_in[j], 16 * (i + c // RING + 1))
                dve.tensor_scalar(B["hot_t"][:, j, :], B["mod"][:, j, :], K["part"][:, 0:1], None, ALU.is_equal)
            dve.tensor_tensor(B["hot"][:, j, :, :], K["count"][:, :].unsqueeze(1).to_broadcast([P, CH, P]),
                              at1(K["mod_t"], g).unsqueeze(2).to_broadcast([P, CH, P]),
                              ALU.is_equal).then_inc(hot_built, 1)

        def logits(i, c):
            j, g, b = c % RING, RING * i + c, c % 2
            near, logit = B["near"][:, b, :, :], B["logit"][:, b, :, :]
            dve.wait_ge(near_made, g + 1)
            link = Chain(dve, logit_step, 4 * g)
            link(dve.tensor_reduce(near, B["ps_near"][b][:, 0:24 * CH].rearrange("p (c v s) -> p c v s", c=CH, s=3),
                                   AX, ALU.add))
            dve.wait_ge(rows_in[j], 64 * (i + c // RING + 1))
            link(dve.tensor_tensor(logit, B["rows"][:, j, :, FEAT:ROW], near[:, :, 0:HEADS], ALU.add))
            link(dve.scalar_tensor_tensor(out=logit, in0=logit, scalar=SLOPE, in1=logit, op0=ALU.mult, op1=ALU.max))
            dve.tensor_tensor(logit, logit, near[:, :, HEADS:2 * HEADS], ALU.subtract).then_inc(logit_step, 1)

        def messages(i, c):
            j, g, b = c % RING, RING * i + c, c % 2
            dve.wait_ge(weighed, g + 1)
            rows = B["rows"][:, j, :, 0:FEAT].rearrange("p c (h f) -> p c h f", h=HEADS)
            out = B["msg"][:, b, :, 0:FEAT].rearrange("p c (h f) -> p c h f", h=HEADS)
            w = B["msg"][:, b, :, FEAT:ROW].unsqueeze(3).to_broadcast([P, CH, HEADS, HID])
            dve.tensor_tensor(out, rows, w, ALU.mult).then_inc(msg_made, 1)

        steps = [(messages, 1), (add, -1), (logits, 2), (hots, 3)] if gat else [(add, 0), (hots, 3)]
        pace(dve, NG, steps, RING)

    return dict(gather=gather, send_mods=send_mods, act=act_program, pe=pe_program, dve=dve_program)


def general_buffers(T, gat):
    G = dict(rel=T.sb("rel", [P, CH]), win=T.sb("win_now", [P, 1]))
    if gat:
        G.update(relb=T.sb("relb", [P, CH, P]), hot_t=T.sb("hot_tf", [P, GE]), ps_rel=T.ps("ps_rel"),
                 ps_as=T.ps("ps_as"), asb=T.sb("asb", [P, CH, P]), top=T.sb("top", [P, 1]),
                 masked=T.sb("masked", [P, GE]))
    return G


def any_edges(L, M, K, S, B, G, table, width, gat, maxima=False):
    NG, NW = S.NG, S.NW
    feat = K["feat"]
    names = ("step", "rows_in", "spread", "looked", "weighed", "summed", "window", "begun")
    step, rows_in, spread, looked, weighed, summed, window, begun = [M.sem(L + "any_" + n) for n in names]
    STEPS = 5 + 4 * HEADS if maxima else 11 if gat else 4
    rel, win = G["rel"], G["win"]

    def pairs(eng, body):
        with eng.Fori(0, NW) as w:
            with eng.Fori(0, NG) as g:
                body(w, g, w * NG + g)

    def gather(pool):
        def pair(w, g, n):
            pool.wait_ge(step, STEPS * n + 2)
            pool.sem_inc(begun, 1)
            for k in range(CH):
                pool.indirect_dma_start(B["rows"][:, 0, k, :], None, table,
                                        bass.IndirectOffsetOnAxis(ap=B["idx"][:, 0, k:k + 1], axis=0)
                                        ).then_inc(rows_in, 16)
        pairs(pool, pair)

    def act_program(act):
        def pair(w, g, n):
            act.wait_ge(step, STEPS * n + 9)
            act.activation(B["msg"][:, 0, :, FEAT:ROW], B["logit"][:, 0, :, :], ACT.Exp).then_inc(weighed, 1)
        if gat and not maxima:
            pairs(act, pair)

    def pe_program(pe):
        def row_of(ps, cols):
            for k in range(CH):
                mm = pe.matmul(ps[:, k * P:(k + 1) * P], cols[:, k, :], K["ident"][:, :], start=True, stop=True)
            return mm

        def pair(w, g, n):
            if gat:
                pe.wait_ge(step, STEPS * n + 3)
                row_of(G["ps_rel"], G["relb"]).then_inc(spread, 1)
            if maxima:
                for h in range(HEADS):
                    pe.wait_ge(step, STEPS * n + (6 + 4 * h))
                    row_of(G["ps_as"], G["asb"]).then_inc(looked, 1)
                return
            if gat:
                pe.wait_ge(step, STEPS * n + 5)
                for k in range(CH):
                    mm = pe.matmul(B["ps_near"][0][:, 8 * k:8 * k + 8], G["hot_t"][:, k * P:(k + 1) * P],
                                   at1(K["near_tab"], w), start=True, stop=True)
                mm.then_inc(looked, 1)
            pe.wait_ge(step, STEPS * n + (STEPS - 1))
            pe.wait_ge(rows_in, 64 * n + 64)
            for k in range(CH):
                rhs = B["msg"][:, 0, k, :] if gat else B["rows"][:, 0, k, :]
                mm = pe.matmul(B["ps_sum"][0][:, 0:width], B["hot"][:, 0, k, :], rhs, start=(k == 0),
                               stop=(k == CH - 1))
            mm.then_inc(summed, 1)
        pairs(pe, pair)

    def dve_program(dve):
        count = K["count"][:, :].unsqueeze(1).to_broadcast([P, CH, P])
        relc = rel[:, :].unsqueeze(2).to_broadcast([P, CH, P])

        def largest(link, w, n):
            link(dve.tensor_scalar(G["hot_t"][:, :], G["ps_rel"][:, :], K["part"][:, 0:1], None, ALU.is_equal))
            link(dve.tensor_scalar(G["hot_t"][:, :], G["hot_t"][:, :], 1.0, 1.0e30, ALU.subtract, ALU.mult))
            dve.wait_ge(rows_in, 64 * n + 64)
            for h in range(HEADS):
                a_s = B["rows"][:, 0, :, FEAT + h:FEAT + h + 1].to_broadcast([P, CH, P])
                link(dve.tensor_copy(G["asb"][:, :, :], a_s))
                dve.wait_ge(looked, HEADS * n + (h + 1))
                link(dve.tensor_tensor(G["masked"][:, :], G["ps_as"][:, :], G["hot_t"][:, :], ALU.add))
                link(dve.tensor_reduce(G["top"][:, :], G["masked"][:, :], AX, ALU.max))
                to = K["shift_src"][:, one(w), h:h + 1].squeeze(1)
                link(dve.tensor_tensor(to, to, G["top"][:, :], ALU.max))

        def sums(link, w, n):
            link(dve.tensor_tensor(B["hot"][:, 0, :, :], count, relc, ALU.is_equal))
            if gat:
                near = B["ps_near"][0][:, 0:8 * CH].rearrange("p (c v) -> p c v", c=CH)
                logit = B["logit"][:, 0, :, :]
                dve.wait_ge(spread, n + 1)
                link(dve.tensor_scalar(G["hot_t"][:, :], G["ps_rel"][:, :], K["part"][:, 0:1], None,
                                       ALU.is_equal))
                dve.wait_ge(looked, n + 1)
                dve.wait_ge(rows_in, 64 * n + 64)
                link(dve.tensor_tensor(logit, B["rows"][:, 0, :, FEAT:ROW], near[:, :, 0:HEADS], ALU.add))
                link(dve.scalar_tensor_tensor(out=logit, in0=logit, scalar=SLOPE, in1=logit, op0=ALU.mult,
                                              op1=ALU.max))
                link(dve.tensor_tensor(logit, logit, near[:, :, HEADS:2 * HEADS], ALU.subtract))
                link(dve.tensor_scalar(logit, logit, 0.0, None, ALU.min))
                dve.wait_ge(weighed, n + 1)
                out = B["msg"][:, 0, :, 0:FEAT].rearrange("p c (h f) -> p c h f", h=HEADS)
                rows = B["rows"][:, 0, :, 0:FEAT].rearrange("p c (h f) -> p c h f", h=HEADS)
                link(dve.tensor_tensor(out, rows, B["msg"][:, 0, :, FEAT:ROW].unsqueeze(3).to_broadcast(
                    [P, CH, HEADS, HID]), ALU.mult))
            dve.wait_ge(summed, n + 1)
            to = feat[:, one(w), 0:width].squeeze(1)
            link(dve.tensor_tensor(to, to, B["ps_sum"][0][:, 0:width], ALU.add))

        dve.memset(win[:, :], -1.0).then_inc(window, 1)
        with dve.Fori(0, NW) as w:
            dve.wait_ge(window, w + 1)
            dve.tensor_scalar(win[:, :], win[:, :], 1.0, None, ALU.add).then_inc(window, 1)
            with dve.Fori(0, NG) as g:
                n = w * NG + g
                link = Chain(dve, step, STEPS * n)
                dve.wait_ge(window, w + 2)
                dve.tensor_copy(B["idx"][:, 0, :], at1(K["src_t"], g))
                link(dve.tensor_scalar(rel[:, :], at1(K["win_t"], g), win[:, 0:1], float(P), ALU.subtract,
                                       ALU.mult))
                link(dve.tensor_tensor(rel[:, :], rel[:, :], at1(K["mod_t"], g), ALU.add))
                if gat:
                    link(dve.tensor_copy(G["relb"][:, :, :], relc))
                if maxima:
                    dve.wait_ge(spread, n + 1)
                    largest(link, w, n)
                else:
                    sums(link, w, n)

    return dict(gather=gather, act=act_program, pe=pe_program, dve=dve_program)


def build_edges(nc, L, M, K, S, table, mod_rows, width, gat, flag):
    with ExitStack() as scope:
        T = Mem(nc, scope, L)
        B = edge_buffers(T, width, gat)
        G = general_buffers(T, gat)
        fast = fast_edges(L, M, K, S, B, table, mod_rows, width, gat)
        slow = any_edges(L, M, K, S, B, G, table, width, gat)
        begun = M.sem(L + "self_messages")

        def either(eng, one_way, other_way):
            ok = eng.value_load(flag[0:1, 0:1], min_val=0, max_val=1)
            with eng.If(ok != 0):
                one_way(eng)
            if other_way:
                with eng.Else():
                    other_way(eng)

        with nc.Block() as block:
            @block.gpsimd
            def _(pool):
                either(pool, fast["gather"], slow["gather"])

            @block.scalar
            def _(act):
                either(act, fast["act"], slow["act"] if gat else None)

            @block.tensor
            def _(pe):
                either(pe, fast["pe"], slow["pe"])

            @block.vector
            def _(dve):
                if gat:
                    body = K["feat"][:, 0:S.NW, 0:FEAT].rearrange("p w (h f) -> p w h f", h=HEADS)
                    dve.tensor_tensor(body, body, K["feat"][:, 0:S.NW, FEAT:ROW].unsqueeze(3).to_broadcast(
                        [P, S.NW, HEADS, HID]), ALU.mult).then_inc(begun, 1)
                    dve.wait_ge(begun, 1)
                either(dve, fast["dve"], slow["dve"])

            if gat:
                @block.sync
                def _(sp):
                    either(sp, fast["send_mods"], None)


def build_attention(nc, L, M, K, S, table):
    NW, NWP = S.NW, S.NWP
    feat = K["feat"]
    step, ranged, all_max, selfed = M.sem(L + "att_step"), M.sem(L + "att_ranged"), M.sem(L + "att_max"), M.sem(L + "att_self")
    shift, near = K["shift_src"], K["near_tab"]
    flag = M.sb(L + "flag", [1, 1], I32)
    a_s = feat[:, :, FEAT:ROW]
    a_d = feat[:, :, ROW:WIDE]
    with ExitStack() as scope:
        T = Mem(nc, scope, L + "att_")
        own = T.sb("own_range", [P, 2 * HEADS])
        all_ = T.sb("all_range", [P, 2 * HEADS])
        least = T.sb("least_as", [P, HEADS])
        span = T.sb("span", [P, HEADS])
        widest = T.sb("widest_span", [P, 1])
        okf = T.sb("ok_f", [1, 2])

        with nc.Block() as block:
            @block.gpsimd
            def _(pool):
                pool.wait_ge(ranged, 1)
                pool.partition_all_reduce(all_[:, :], own[:, :], P, MAX).then_inc(all_max, 1)

            @block.vector
            def _(dve):
                link = Chain(dve, step)
                by_head = feat[:, 0:NW, FEAT:ROW].rearrange("p w h -> p h w")
                dve.tensor_reduce(own[:, 0:HEADS], by_head, AX, ALU.max)
                link(dve.tensor_reduce(least[:, :], by_head, AX, ALU.min))
                dve.tensor_scalar(own[:, HEADS:2 * HEADS], least[:, :], -1.0, None, ALU.mult).then_inc(ranged, 1)
                dve.wait_ge(all_max, 1)
                dve.tensor_copy(shift[:, :, :], all_[:, 0:HEADS].unsqueeze(1).to_broadcast([P, NWP, HEADS]))
                link(dve.tensor_tensor(span[:, :], all_[:, 0:HEADS], all_[:, HEADS:2 * HEADS], ALU.add))
                dve.tensor_copy(okf[:, 1:2], K["spread_ok"][:, :])
                link(dve.tensor_reduce(widest[:, :], span[:, :], AX, ALU.max))
                link(dve.tensor_scalar(okf[:, 0:1], widest[0:1, :], SAFE, None, ALU.is_le))
                dve.tensor_tensor(flag[:, :], okf[:, 0:1], okf[:, 1:2], ALU.mult)

    with ExitStack() as scope:
        T = Mem(nc, scope, L + "att_")
        B = dict(idx=T.sb("idx", [P, 1, CH], I32), rows=T.sb("rows", [P, 1, CH, ROW]))
        G = general_buffers(T, True)
        own_max = any_edges(L + "max_", M, K, S, B, G, table, ROW, True, maxima=True)
        begun = M.sem(L + "att_begun")

        with nc.Block() as block:
            @block.gpsimd
            def _(pool):
                when(pool, flag, False, own_max["gather"])

            @block.tensor
            def _(pe):
                when(pe, flag, False, own_max["pe"])

            @block.vector
            def _(dve):
                def program(dve):
                    dve.tensor_copy(shift[:, 0:NW, :], feat[:, 0:NW, FEAT:ROW]).then_inc(begun, 1)
                    dve.wait_ge(begun, 1)
                    own_max["dve"](dve)
                when(dve, flag, False, program)

    with ExitStack() as scope:
        T = Mem(nc, scope, L + "att_")
        own_l = T.sb("own_logit", [P, NWP, HEADS])
        own_w = T.sb("own_weight", [P, NWP, HEADS])
        rest = T.sb("tab_rest", [P, NWP, 2 * HEADS])
        part = K["tab24"][:, :, :].rearrange("p w (v s) -> p w v s", s=3)
        with nc.Block() as block:
            @block.scalar
            def _(act):
                act.wait_ge(step, 9)
                act.activation(own_w[:, :, :], own_l[:, :, :], ACT.Exp).then_inc(selfed, 1)

            @block.vector
            def _(dve):
                link = Chain(dve, step, 4)
                hi = near[:, :, HEADS:2 * HEADS]
                dve.tensor_copy(near[:, :, 0:HEADS], a_d)
                dve.tensor_tensor(hi, a_d, shift[:, :, :], ALU.add)
                link(dve.tensor_tensor(own_l[:, :, :], a_s, a_d, ALU.add))
                link(dve.scalar_tensor_tensor(out=hi, in0=hi, scalar=SLOPE, in1=hi, op0=ALU.mult, op1=ALU.max))
                link(dve.scalar_tensor_tensor(out=own_l[:, :, :], in0=own_l[:, :, :], scalar=SLOPE,
                                              in1=own_l[:, :, :], op0=ALU.mult, op1=ALU.max))
                link(dve.tensor_tensor(own_l[:, :, :], own_l[:, :, :], hi, ALU.subtract))
                link(dve.tensor_scalar(own_l[:, :, :], own_l[:, :, :], 0.0, None, ALU.min))
                link(dve.tensor_copy(part[:, :, :, 0], near[:, :, :]))
                link(dve.tensor_tensor(rest[:, :, :], near[:, :, :], part[:, :, :, 0], ALU.subtract))
                link(dve.tensor_copy(part[:, :, :, 1], rest[:, :, :]))
                link(dve.tensor_tensor(rest[:, :, :], rest[:, :, :], part[:, :, :, 1], ALU.subtract))
                link(dve.tensor_copy(part[:, :, :, 2], rest[:, :, :]))
                dve.wait_ge(selfed, 1)
                dve.tensor_copy(a_s, own_w[:, :, :])
    return flag


def build_batch_norm(nc, L, M, K, S, F, bias, gamma, beta, gat):
    N, NW, WB, NB = S.N, S.NW, S.WB, S.NB
    feat = K["feat"]
    params, rec_made, step = M.sem(L + "bn_params"), M.sem(L + "bn_rec"), M.sem(L + "bn_step")
    shaped, meaned, centred = M.sem(L + "bn_shaped"), M.sem(L + "bn_meaned"), M.sem(L + "bn_centred")
    paired, squared, used = M.sem(L + "bn_paired"), M.sem(L + "bn_squared"), M.sem(L + "bn_used")
    varied, rooted = M.sem(L + "bn_varied"), M.sem(L + "bn_rooted")
    scale, offset = K["bn_scale"], K["bn_offset"]
    HALF = WB // 2
    Q = max(q for q in range(1, HALF + 1) if HALF % q == 0 and q * F <= 512)
    with ExitStack() as scope:
        T = Mem(nc, scope, L)
        bias_b = T.sb("bias_b", [P, F])
        mean = T.sb("mean", [P, F])
        var = T.sb("var", [P, F])
        std = T.sb("std", [P, F])
        rec = T.sb("rec", [P, NW, HEADS])
        square = T.sb("square", [P, 2, WB, F])
        pair = T.sb("pair", [P, 2, HALF, F])
        ps_m, ps_v = T.ps("ps_mean"), T.ps("ps_var")

        def batch(b):
            return feat[:, bass.ds(b * WB, WB), 0:F]

        def every(v):
            return v[:, :].unsqueeze(1).to_broadcast([P, WB, F])

        def last_window(dve, sem):
            v = feat[:, NW - 1, 0:F]
            return dve.tensor_scalar(v, v, K["real"][:, 0:1], None, ALU.mult).then_inc(sem, 1)

        def total(dve, out, ps):
            return dve.tensor_reduce(out, ps[:, 0:Q * F].rearrange("p (q f) -> p f q", q=Q), AX, ALU.add)

        with nc.Block() as block:
            @block.sync
            def _(sp):
                for to, x in ((bias_b, bias), (scale, gamma), (offset, beta)):
                    sp.dma_start(to[:, 0:F], x.rearrange("(a f) -> a f", a=1).to_broadcast([P, F])
                                 ).then_inc(params, 16)

            @block.vector
            def _(dve):
                dve.wait_ge(params, 48)
                if gat:
                    dve.reciprocal(rec[:, :, :], feat[:, 0:NW, FEAT:ROW]).then_inc(rec_made, 1)
                    dve.wait_ge(rec_made, 1)
                STEPS = 0 if gat else 2
                with dve.Fori(0, NB) as b:
                    if gat:
                        v = batch(b).rearrange("p w (h f) -> p w h f", h=HEADS)
                        dve.tensor_tensor(v, v, rec[:, bass.ds(b * WB, WB), :].unsqueeze(3).to_broadcast(
                            [P, WB, HEADS, HID]), ALU.mult).then_inc(shaped, 1)
                    else:
                        chain = Chain(dve, step, STEPS * b)
                        chain(dve.tensor_tensor(batch(b), batch(b), K["dinv"][:, bass.ds(b * WB, WB)].unsqueeze(
                            2).to_broadcast([P, WB, F]), ALU.mult))
                        chain(dve.tensor_tensor(batch(b), batch(b), every(bias_b), ALU.add))
                        dve.tensor_scalar(batch(b), batch(b), 0.0, None, ALU.max).then_inc(shaped, 1)
                dve.wait_ge(shaped, NB)
                last_window(dve, shaped)
                link = Chain(dve, step, STEPS * NB)
                dve.wait_ge(meaned, 1)
                link(total(dve, mean[:, :], ps_m))
                if gat:
                    link(dve.scalar_tensor_tensor(out=mean[:, :], in0=mean[:, :], scalar=1.0 / N, in1=bias_b[:, :],
                                                  op0=ALU.mult, op1=ALU.add))
                    link(dve.tensor_tensor(mean[:, :], mean[:, :], bias_b[:, :], ALU.subtract))
                else:
                    link(dve.tensor_scalar(mean[:, :], mean[:, :], 1.0 / N, None, ALU.mult))
                with dve.Fori(0, NB) as b:
                    dve.tensor_tensor(batch(b), batch(b), every(mean), ALU.subtract).then_inc(centred, 1)
                dve.wait_ge(centred, NB)
                last_window(dve, centred)
                dve.wait_ge(varied, 1)
                total(dve, var[:, :], ps_v).then_inc(varied, 1)
                dve.wait_ge(rooted, 1)
                link(dve.reciprocal(std[:, :], std[:, :]))
                dve.tensor_tensor(scale[:, 0:F], scale[:, 0:F], std[:, :], ALU.mult)

            @block.gpsimd
            def _(pool):
                def halves(i, c):
                    b = 2 * i + c
                    last = isinstance(i, int) and b == NB - 1
                    pool.wait_ge(shaped, b + 1 + last)
                    wait(pool, used, b - 1)
                    pool.tensor_tensor(pair[:, c % 2, :, :], feat[:, bass.ds(b * WB, HALF), 0:F],
                                       feat[:, bass.ds(b * WB + HALF, HALF), 0:F], ALU.add).then_inc(paired, 1)

                def square_halves(i, c):
                    b = 2 * i + c
                    pool.wait_ge(squared, b + 1)
                    pool.wait_ge(used, NB + b - 1)
                    pool.tensor_tensor(pair[:, c % 2, :, :], square[:, c % 2, 0:HALF, :], square[:, c % 2, HALF:WB, :],
                                       ALU.add).then_inc(paired, 1)
                pace(pool, NB, [(halves, 0)])
                pace(pool, NB, [(square_halves, 0)])

            @block.scalar
            def _(act):
                def squares(i, c):
                    b = 2 * i + c
                    last = isinstance(i, int) and b == NB - 1
                    act.wait_ge(centred, b + 1 + last)
                    act.wait_ge(paired, NB + b - 1)
                    act.activation(square[:, c % 2, :, :], batch(b), ACT.Square).then_inc(squared, 1)
                pace(act, NB, [(squares, 0)])
                act.wait_ge(varied, 2)
                act.activation(std[:, :], var[:, :], ACT.Sqrt, scale=1.0 / N, bias=K["eps"][:, 0:1]
                               ).then_inc(rooted, 1)

            @block.tensor
            def _(pe):
                for n, (ps, done) in enumerate(((ps_m, meaned), (ps_v, varied))):
                    pe.matmul(ps[:, 0:Q * F], K["zeros"][:, 0:P], K["zeros"][:, 0:Q * F], start=True, stop=False)

                    def add_pairs(i, c):
                        b = 2 * i + c
                        pe.wait_ge(paired, n * NB + b + 1)
                        for j in range(0, HALF, Q):
                            mm = pe.matmul(ps[:, 0:Q * F], K["ones"][:, :],
                                           pair[:, c % 2, j:j + Q, :].rearrange("p q f -> p (q f)"),
                                           start=False, stop=False)
                        mm.then_inc(used, 1)
                    pace(pe, NB, [(add_pairs, 0)])
                    pe.matmul(ps[:, 0:Q * F], K["zeros"][:, 0:P], K["zeros"][:, 0:Q * F], start=False, stop=True
                              ).then_inc(done, 1)


def build_gat_input(nc, L, M, K, S, F, elu, W, a_src, a_dst, table):
    NW, WB, NB = S.NW, S.WB, S.NB
    feat, scale, offset = K["feat"], K["bn_scale"], K["bn_offset"]
    KP = 1 if F <= P else 2
    KF = F // KP
    sems = ("w_in", "cleared", "wt", "wt_got", "wa", "wa_got", "scaled", "shifted", "clipped", "exped", "staged",
            "turned", "copied", "product", "placed", "stored")
    (w_in, cleared, wt_made, wt_got, wa_made, wa_got, scaled, shifted, clipped, exped, staged, turned, copied,
     product, placed, stored) = [M.sem(f"{L}gat_{n}") for n in sems]
    with ExitStack() as scope:
        T = Mem(nc, scope, L)
        w = T.sb("w_gat", [P, KP, WIDE])
        wt = T.sb("w_turned", [P, 2, F])
        heads = T.sb("heads", [P, 2, 2 * HEADS])
        scl = T.sb("scl", [P, 2, F])
        shf = T.sb("shf", [P, 2, F])
        clp = T.sb("clp", [P, 2, F])
        ex = T.sb("ex", [P, 2, F])
        stage = T.sb("stage", [P, 2, KP * P])
        xt = T.sb("xt", [P, 2, KP * P])
        ps_t = [T.ps(f"pt{i}") for i in range(2)]
        ps_o = [T.ps(f"po{i}") for i in range(2)]
        ps_w, ps_a = T.ps("pw"), T.ps("pa")

        with nc.Block() as block:
            @block.sync
            def _(sp):
                sp.dma_start(w[0:KF, :, 0:FEAT], W.rearrange("(k p) f -> p k f", p=KF)).then_inc(w_in, 16)
                sp.wait_ge(cleared, 1)
                with nc.allow_non_contiguous_dma(reason="a head's 64 values down the partitions"):
                    for h in range(HEADS):
                        rows = slice(HID * (h % 2), HID * (h % 2) + HID)
                        for q, a in enumerate((a_src, a_dst)):
                            col = q * HEADS + h
                            sp.dma_start(heads[rows, h // 2, col:col + 1],
                                         a[h:h + 1, :].rearrange("a f -> f a")).then_inc(w_in, 16)
                for b in range(NB):
                    sp.wait_ge(placed, (b + 1) * WB)
                    rows = table[b * WB * P:(b + 1) * WB * P, :].rearrange("(w p) f -> p w f", p=P)
                    sp.dma_start(rows, feat[:, b * WB:(b + 1) * WB, 0:ROW]).then_inc(stored, 16)
                sp.wait_ge(stored, 16 * NB)

            @block.gpsimd
            def _(pool):
                pool.memset(heads[:, :, :], 0.0).then_inc(cleared, 1)

                def scaling(i, c):
                    n, slot = 2 * i + c, c % 2
                    wait(pool, shifted, n - 1)
                    pool.tensor_tensor(scl[:, slot, :], feat[:, one(n), 0:F].squeeze(1), scale[:, 0:F],
                                       ALU.mult).then_inc(scaled, 1)
                pace(pool, NW, [(scaling, 0)])

            @block.vector
            def _(dve):
                if F < P:
                    dve.memset(stage[:, :, F:P], 0.0)
                    dve.memset(w[F:P, :, :], 0.0)

                def widen(n, src, out, made, got):
                    dve.wait_ge(made, n)
                    dve.tensor_copy(out, src).then_inc(got, 1)
                for j in range(2):
                    for k in range(KP):
                        n = j * KP + k
                        widen(n + 1, ps_w[:, 0:KF], wt[:, j, k * KF:(k + 1) * KF], wt_made, wt_got)
                for k in range(KP):
                    widen(k + 1, ps_a[0:KF, 0:2 * HEADS], w[0:KF, k, FEAT:WIDE], wa_made, wa_got)

                def shift(i, c):
                    n, slot = 2 * i + c, c % 2
                    dve.wait_ge(scaled, n + 1)
                    to = shf if elu else stage
                    wait(dve, staged if elu else turned, n - 1)
                    dve.tensor_tensor(to[:, slot, 0:F], scl[:, slot, :], offset[:, 0:F], ALU.add
                                      ).then_inc(shifted, 1)
                    if elu:
                        dve.wait_ge(shifted, n + 1)
                        wait(dve, exped, n - 1)
                        dve.tensor_scalar(clp[:, slot, :], shf[:, slot, :], 0.0, None, ALU.min
                                          ).then_inc(clipped, 1)

                def unite(i, c):
                    n, slot = 2 * i + c, c % 2
                    dve.wait_ge(exped, n + 1)
                    wait(dve, turned, n - 1)
                    dve.scalar_tensor_tensor(out=stage[:, slot, :], in0=ex[:, slot, :], scalar=-1.0,
                                             in1=shf[:, slot, :], op0=ALU.add, op1=ALU.max).then_inc(staged, 1)
                pace(dve, NW, [(shift, 1), (unite, 0)] if elu else [(shift, 0)])

            @block.scalar
            def _(act):
                def expo(i, c):
                    n, slot = 2 * i + c, c % 2
                    act.wait_ge(clipped, n + 1)
                    wait(act, staged, n - 1)
                    act.activation(ex[:, slot, :], clp[:, slot, :], ACT.Exp).then_inc(exped, 1)

                def copy(i, c):
                    n, slot = 2 * i + c, c % 2
                    act.wait_ge(turned, n + 1)
                    wait(act, product, n - 1)
                    act.copy(xt[:, slot, :], ps_t[slot][:, 0:KP * P]).then_inc(copied, 1)

                def place(i, c):
                    n, slot = 2 * i + c, c % 2
                    act.wait_ge(product, n + 1)
                    act.copy(feat[:, one(n), 0:WIDE].squeeze(1), ps_o[slot][:, 0:WIDE]).then_inc(placed, 1)
                pace(act, NW, ([(expo, 2)] if elu else []) + [(copy, 1), (place, 0)])

            @block.tensor
            def _(pe):
                pe.wait_ge(w_in, 16 * (1 + 2 * HEADS))
                for j in range(2):
                    for k in range(KP):
                        n = j * KP + k
                        wait(pe, wt_got, n)
                        pe.transpose(ps_w[:, 0:KF], w[0:KF, k, j * P:(j + 1) * P], K["ident"][0:KF, 0:KF]
                                     ).then_inc(wt_made, 1)
                pe.wait_ge(wt_got, 2 * KP)
                for k in range(KP):
                    wait(pe, wa_got, k)
                    for j in range(2):
                        mm = pe.matmul(ps_a[0:KF, 0:2 * HEADS], wt[:, j, k * KF:(k + 1) * KF], heads[:, j, :],
                                       start=(j == 0), stop=(j == 1))
                    mm.then_inc(wa_made, 1)
                pe.wait_ge(wa_got, KP)
                linear(pe, K, S, KP, stage, ps_t, xt, ps_o, w, WIDE, staged if elu else shifted, turned,
                       copied, product, placed)


def build_gnn(nc, M, K, S, x, src, dst, W_gcn, gcn, gats):
    mod_rows = nc.dram_tensor("mod_rows", (S.NG, GE), BF16).ap()
    table0 = nc.dram_tensor("gcn_table", (S.NW * P, HID), F32).ap()
    K["bn_scale"], K["bn_offset"] = M.sb("bn_scale", [P, FEAT]), M.sb("bn_offset", [P, FEAT])
    build_constants(nc, M, K, S)
    K["feat"] = M.sb("feat", [P, S.NWP, WIDE])
    with ExitStack() as scope:
        T = Mem(nc, scope)
        K["shift_src"] = T.sb("shift_src", [P, S.NWP, HEADS])
        K["near_tab"] = T.sb("near_tab", [P, S.NWP, 2 * HEADS])
        K["tab24"] = T.sb("tab24", [P, S.NWP, 24], BF16)
        build_edge_tables(nc, T, K, S, src, dst, mod_rows)
        K["dinv"] = T.sb("dinv", [P, S.NW])
        with ExitStack() as part:
            D = Mem(nc, part)
            K["deg"] = D.sb("deg", [P, S.NW])
            K["tally"] = D.sb("tally", [P, S.NG])
            build_any_degrees(nc, D, K, S)
            build_gcn_input(nc, D, K, S, x, W_gcn, mod_rows)
            build_fast_degrees(nc, D, K, S)
            build_gcn_table(nc, D, K, S, table0)
        build_edges(nc, "gcn_", T, K, S, table0, mod_rows, HID, False, K["spread_ok"])
        build_batch_norm(nc, "gcn_", T, K, S, HID, *gcn, gat=False)
        Mem.clear_signals(nc)
        for n, (W, a_src, a_dst, bias, gamma, beta) in enumerate(gats):
            L = f"gat{n}_"
            table = nc.dram_tensor(L + "table", (S.NW * P, ROW), F32).ap()
            build_gat_input(nc, L, T, K, S, W.shape[0], n > 0, W, a_src, a_dst, table)
            flag = build_attention(nc, L, T, K, S, table)
            build_edges(nc, L, T, K, S, table, mod_rows, ROW, True, flag)
            build_batch_norm(nc, L, T, K, S, FEAT, bias, gamma, beta, gat=True)
            Mem.clear_signals(nc)


def build_ffn_input(nc, M, K, S, x, gamma, beta, Wr, br, xn_rows):
    N, NW, WB, NB, TAIL, EX = S.N, S.NW, S.WB, S.NB, S.TAIL, S.EX
    Z = 4
    feat, scale, offset = K["feat"], K["bn_scale"], K["bn_offset"]
    names = ("params x_in cleared scaled offset_in clipped exped elued joined step varied rooted normed "
             "stretched staged turned copied product routed taken").split()
    (params, x_in, cleared, scaled, offset_in, clipped, exped, elued, joined, step, varied, rooted, normed,
     stretched, staged, turned, copied, product, routed, taken) = [M.sem("ffi_" + n) for n in names]
    stored = [M.sem(f"ffi_stored{j}") for j in range(Z)]
    with ExitStack() as scope:
        T = Mem(nc, scope, "ffi_")
        xr = T.sb("xr", [P, WB, FEAT])
        z = T.sb("z", [P, Z, WB, FEAT])
        zt = T.sb("zt", [P, 2, 2, P])
        st = T.sb("st", [P, WB, 6])
        mean, var, std, rstd = [T.sb(n, [P, WB]) for n in ("mean", "var", "std", "rstd")]
        std2, rstd2 = T.sb("std2", [P, WB]), T.sb("rstd2", [P, WB])
        gm, bt = T.sb("gm", [P, FEAT]), T.sb("bt", [P, FEAT])
        wr = T.sb("wr", [P, 2, EX])
        brb = T.sb("brb", [P, EX])
        ps_t = [T.ps(f"pt{i}") for i in range(2)]
        ps_l = [T.ps(f"pl{i}") for i in range(2)]

        def body(b):
            return feat[:, b * WB:(b + 1) * WB, 0:FEAT]

        def every(v):
            return v[:, :].unsqueeze(1).to_broadcast([P, WB, v.shape[1]])

        def turns(steps):
            for t in range(-max(lead for _, lead in steps), NB - min(lead for _, lead in steps)):
                for fn, lead in steps:
                    if 0 <= t + lead < NB:
                        fn(t + lead)

        with nc.Block() as block:
            @block.sync
            def _(sp):
                for to, v in ((gm, gamma), (bt, beta), (brb, br)):
                    sp.dma_start(to[:, :], v.rearrange("(a f) -> a f", a=1).to_broadcast(
                        [P, v.shape[0]])).then_inc(params, 16)
                sp.dma_start(wr[:, :, :], Wr.rearrange("(k p) e -> p k e", p=P)).then_inc(params, 16)
                sp.wait_ge(cleared, 1)

                def load(b):
                    wait(sp, joined, b)
                    w0, w1 = b * WB, min((b + 1) * WB, NW - 1)
                    sp.dma_start(xr[:, 0:w1 - w0, :],
                                 x[w0 * P:w1 * P, :].rearrange("(w p) f -> p w f", p=P)).then_inc(x_in, 16)
                    if b == NB - 1:
                        sp.dma_start(xr[0:TAIL, WB - 1, :], x[(NW - 1) * P:N, :]).then_inc(x_in, 16)

                def store(b):
                    sp.wait_ge(staged, b + 1)
                    rows = xn_rows[b * WB * P:(b + 1) * WB * P, :].rearrange("(w p) f -> p w f", p=P)
                    sp.dma_start(rows, z[:, b % Z, :, :]).then_inc(stored[b % Z], 16)
                turns([(load, 2), (store, -1)])
                for j in range(Z):
                    wait(sp, stored[j], 16 * len(range(j, NB, Z)))

            @block.gpsimd
            def _(pool):
                def scaling(b):
                    pool.tensor_tensor(body(b), body(b), every(scale), ALU.mult).then_inc(scaled, 1)

                def add_x(b):
                    pool.wait_ge(elued, b + 1)
                    pool.wait_ge(x_in, 16 * (b + 1 + (b == NB - 1)))
                    pool.tensor_tensor(body(b), body(b), xr[:, :, :], ALU.add).then_inc(joined, 1)

                def stretch(b):
                    zb = z[:, b % Z, :, :]
                    pool.wait_ge(normed, b + 1)
                    pool.tensor_tensor(zb, zb, every(gm), ALU.mult).then_inc(stretched, 1)
                pool.memset(xr[:, :, :], 0.0).then_inc(cleared, 1)
                pool.wait_ge(params, 64)
                turns([(scaling, 2), (add_x, 1), (stretch, 0)])

            @block.vector
            def _(dve):
                dve.wait_ge(params, 64)
                link = Chain(dve, step)

                def add_offset(b):
                    dve.wait_ge(scaled, b + 1)
                    dve.tensor_tensor(body(b), body(b), every(offset), ALU.add).then_inc(offset_in, 1)

                def elu(b):
                    dve.wait_ge(exped, b + 1)
                    dve.wait_ge(offset_in, b + 1)
                    dve.scalar_tensor_tensor(out=body(b), in0=z[:, b % Z, :, :], scalar=-1.0, in1=body(b),
                                             op0=ALU.add, op1=ALU.max).then_inc(elued, 1)

                def spread(b):
                    dve.wait_ge(joined, b + 1)
                    for w in range(WB):
                        ins = dve.bn_stats(st[:, w, :], body(b)[:, w, :])
                    link(ins)
                    spread_of(dve, link, st, mean[:, :], var[:, :])
                    dve.sem_inc(varied, 1)

                def norm(b):
                    dve.wait_ge(rooted, 2 * b + 1)
                    link(dve.reciprocal(rstd[:, :], std[:, :]))
                    link(dve.tensor_tensor(var[:, :], var[:, :], rstd[:, :], ALU.mult))
                    link(dve.tensor_tensor(var[:, :], var[:, :], rstd[:, :], ALU.mult))
                    dve.sem_inc(varied, 1)
                    dve.wait_ge(rooted, 2 * b + 2)
                    link(dve.reciprocal(rstd2[:, :], std2[:, :]))
                    link(dve.tensor_tensor(rstd[:, :], rstd[:, :], rstd2[:, :], ALU.mult))
                    for w in range(WB):
                        ins = dve.tensor_scalar(z[:, b % Z, w, :], body(b)[:, w, :], mean[:, w:w + 1],
                                                rstd[:, w:w + 1], ALU.subtract, ALU.mult)
                    ins.then_inc(normed, 1)
                    dve.wait_ge(normed, b + 1)

                def add_beta(b):
                    zb = z[:, b % Z, :, :]
                    dve.wait_ge(stretched, b + 1)
                    dve.tensor_tensor(zb, zb, every(bt), ALU.add).then_inc(staged, 1)

                def take(b):
                    dve.wait_ge(routed, b + 1)
                    dve.tensor_tensor(K["logits"][:, b * WB:(b + 1) * WB, :],
                                      ps_l[b % 2][:, 0:WB * EX].rearrange("p (w e) -> p w e", e=EX), every(brb),
                                      ALU.add).then_inc(taken, 1)
                turns([(spread, 0), (elu, 1), (norm, 0), (add_offset, 2), (add_beta, -1), (take, -2)])

            @block.scalar
            def _(act):
                def expo(b):
                    zb = z[:, b % Z, :, :]
                    act.wait_ge(offset_in, b + 1)
                    wait(act, turned, (b - Z + 1) * WB)
                    wait(act, stored[b % Z], 16 * (b // Z))
                    act.activation(zb, body(b), ACT.Relu, scale=-1.0).then_inc(clipped, 1)
                    act.wait_ge(clipped, b + 1)
                    act.activation(zb, zb, ACT.Exp, scale=-1.0).then_inc(exped, 1)

                def roots(b):
                    for n, to in enumerate((std, std2)):
                        act.wait_ge(varied, 2 * b + n + 1)
                        act.activation(to[:, :], var[:, :], ACT.Sqrt, bias=K["eps"][:, 0:1]).then_inc(rooted, 1)

                def copies(b):
                    for w in range(WB):
                        n = b * WB + w
                        act.wait_ge(turned, n + 1)
                        wait(act, product, n - 1)
                        act.copy(zt[:, n % 2, :, :], ps_t[n % 2][:, 0:2 * P].rearrange(
                            "p (k t) -> p k t", k=2)).then_inc(copied, 1)
                turns([(roots, 0), (copies, -2), (expo, 2)])

            @block.tensor
            def _(pe):
                pe.wait_ge(params, 64)
                for b in range(NB):
                    pe.wait_ge(staged, b + 1)
                    wait(pe, taken, b - 1)
                    for w in range(WB + 1):
                        n = b * WB + w
                        if w < WB:
                            wait(pe, copied, n - 1)
                            for k in range(2):
                                mm = pe.transpose(ps_t[n % 2][:, k * P:(k + 1) * P],
                                                  z[:, b % Z, w, k * P:(k + 1) * P], K["ident"][:, :])
                            mm.then_inc(turned, 1)
                        if w:
                            pe.wait_ge(copied, n)
                            for k in range(2):
                                mm = pe.matmul(ps_l[b % 2][:, (w - 1) * EX:w * EX], zt[:, (n - 1) % 2, k, :],
                                               wr[:, k, :], start=(k == 0), stop=(k == 1))
                            mm.then_inc(product, 1)
                    pe.matmul(ps_l[b % 2][:, WB * EX:WB * EX + 8], K["zeros"][:, 0:P], K["zeros"][:, 0:8],
                              start=True, stop=True).then_inc(routed, 1)


def build_routing(nc, M, K, S, W1):
    NW, EX, NS = S.NW, S.EX, S.NS
    HALF = NW // 2
    HD, up_all = S.HD, K["up_all"]
    names = "counted step tri_in both_in sums_in matched built used token_in apart weighed w1_in".split()
    counted, step, tri_in, both_in, sums_in, matched, built, used, token_in, apart, weighed, w1_in = [
        M.sem("route_" + n) for n in names]
    with ExitStack() as scope:
        T = Mem(nc, scope, "route_")
        hots = [T.sb(f"hot{n}", [P, NW, EX]) for n in range(2)]
        largest, first = T.sb("largest", [P, 2, NW]), T.sb("first", [P, NW])
        diff, ge, gs = T.sb("diff", [P, NW]), T.sb("ge", [P, NW]), T.sb("gs", [P, NW])
        NUM = max(NS, P, 2 * NW + 1)
        num_i, num, num_b = T.sb("num_i", [P, NUM], I32), T.sb("num", [P, NUM]), T.sb("num_b", [P, NUM], BF16)
        tri = T.sb("tri", [P, P])
        both = T.sb("both", [P, NW, EX])
        own = T.sb("own", [P, NW, EX])
        upto = [T.sb(f"upto{i}", [P, NW, EX]) for i in range(2)]
        slot = T.sb("slot", [P, NW, EX])
        picked = T.sb("picked", [P, NW, EX])
        tokens, chunks, ends = T.sb("tokens", [P, EX]), T.sb("chunks", [P, EX]), [T.sb(f"ends{i}", [P, EX])
                                                                               for i in range(2)]
        tok_i, base = T.sb("tok_i", [P, EX], I32), T.sb("base", [P, EX])
        past, which = T.sb("past", [1, NS, EX - 1]), T.sb("which", [1, NS])
        slot_f, slot_i = T.sb("slot_f", [P, NW, 2]), T.sb("slot_i", [P, NW, 2], I32)
        chunk_i, place_i = T.sb("chunk_i", [P, NW, 2], I32), T.sb("place_i", [P, NW, 2], I32)
        chunk, place = T.sb("chunk", [P, NW, 2]), T.sb("place", [P, NW, 2])
        hot = T.sb("hot", [P, RING, 2, P], BF16)
        hot_p = T.sb("hot_p", [P, RING, 2, P], BF16)
        hot_w = T.sb("hot_w", [P, RING, 2, P], BF16)
        hot_c = T.sb("hot_c", [P, RING, 2, NS], BF16)
        block_f, row_f, gap, gap_row, second, token_f = [
            T.sb(n, [P, NS]) for n in "block_f row_f gap gap_row second token_f".split()]
        ps_own = [T.ps(f"own{i}") for i in range(2)]
        ps_pre = [T.ps(f"pre{i}") for i in range(2)]
        ps_p, ps_w = T.ps("p"), T.ps("w")

        def half(v, i):
            return v[:, i * HALF:(i + 1) * HALF, :]

        def halves(ps, i):
            return ps[i][:, 0:HALF * EX].rearrange("p (w e) -> p w e", e=EX)

        def choose(dve, link):
            lg, eq, score = K["logits"], slot, picked

            def by_expert(v):
                return v.unsqueeze(2).to_broadcast([P, NW, EX])
            count8 = K["count"][:, 0:EX].unsqueeze(1).to_broadcast([P, NW, EX])
            for n, hot in enumerate(hots):
                link(dve.tensor_reduce(largest[:, n, :], lg[:, :, :], AX, ALU.max))
                link(dve.tensor_tensor(eq[:, :, :], lg[:, :, :], by_expert(largest[:, n, :]), ALU.is_equal))
                link(dve.scalar_tensor_tensor(out=score[:, :, :], in0=eq[:, :, :], scalar=-float(EX), in1=count8,
                                              op0=ALU.mult, op1=ALU.add))
                link(dve.tensor_reduce(first[:, :], score[:, :, :], AX, ALU.min))
                link(dve.tensor_tensor(hot[:, :, :], score[:, :, :], by_expert(first[:, :]), ALU.is_equal))
                if n == 0:
                    link(dve.scalar_tensor_tensor(out=lg[:, :, :], in0=hot[:, :, :], scalar=-1.0e30,
                                                  in1=lg[:, :, :], op0=ALU.mult, op1=ALU.add))
            dve.tensor_tensor(diff[:, :], largest[:, 1, :], largest[:, 0, :], ALU.subtract).then_inc(apart, 1)
            dve.wait_ge(weighed, 1)
            link(dve.tensor_scalar(gs[:, :], ge[:, :], 1.0, None, ALU.add))
            link(dve.reciprocal(K["weight1"][:, :], gs[:, :]))
            link(dve.tensor_tensor(K["weight2"][:, :], ge[:, :], K["weight1"][:, :], ALU.mult))

        with nc.Block() as block:
            @block.scalar
            def _(act):
                act.wait_ge(apart, 1)
                act.activation(ge[:, :], diff[:, :], ACT.Exp).then_inc(weighed, 1)

                def scales(i, b):
                    w = RING * i + b
                    act.wait_ge(matched, w + 1)
                    act.activation(hot_p[:, b, :, :], hot[:, b, :, :], ACT.Copy, scale=K["part"][:, 0:1])
                    for n in range(2):
                        ins = act.activation(hot_w[:, b, n, :], hot[:, b, n, :], ACT.Copy,
                                             scale=num[:, one(w + (NW * n + 1))])
                    ins.then_inc(built, 1)
                pace(act, NW, [(scales, 0)], RING)

            @block.sync
            def _(sp):
                for e in range(EX):
                    sp.dma_start(up_all[:, e, 0:2 * HD].rearrange("p (k h) -> p k h", k=2),
                                 W1[e].rearrange("(k p) h -> p k h", p=P)).then_inc(w1_in, 16)
                sp.wait_ge(w1_in, 16 * EX)

            @block.gpsimd
            def _(pool):
                pool.iota(num_i[:, :], pattern=[[1, NUM]], base=0, channel_multiplier=0).then_inc(counted, 1)

            @block.tensor
            def _(pe):
                pe.wait_ge(both_in, 1)
                pe.wait_ge(tri_in, 1)
                for i in range(2):
                    pe.matmul(ps_own[i][:, 0:HALF * EX], K["ones"][:, :], half(both, i), start=True, stop=True)
                for i in range(2):
                    mm = pe.matmul(ps_pre[i][:, 0:HALF * EX], tri[:, :], half(both, i), start=True, stop=True)
                mm.then_inc(sums_in, 1)
                for ps in (ps_p, ps_w):
                    pe.matmul(ps[:, 0:NS], K["zeros"][:, 0:P], K["zeros"][:, 0:NS], start=True, stop=False)

                def places(i, b):
                    pe.wait_ge(built, RING * i + b + 1)
                    for n in range(2):
                        pe.matmul(ps_p[:, 0:NS], hot_p[:, b, n, :], hot_c[:, b, n, :], start=False, stop=False)
                        mm = pe.matmul(ps_w[:, 0:NS], hot_w[:, b, n, :], hot_c[:, b, n, :], start=False, stop=False)
                    mm.then_inc(used, 1)
                pace(pe, NW, [(places, 0)], RING)
                for ps in (ps_p, ps_w):
                    mm = pe.matmul(ps[:, 0:NS], K["zeros"][:, 0:P], K["zeros"][:, 0:NS], start=False, stop=True)
                mm.then_inc(token_in, 1)

            @block.vector
            def _(dve):
                link = Chain(dve, step)
                choose(dve, link)
                dve.tensor_scalar(tri[:, :], K["count"][:, :], K["part"][:, 0:1], None, ALU.is_gt).then_inc(tri_in, 1)
                dve.tensor_tensor(both[:, :, :], hots[0][:, :, :], hots[1][:, :, :], ALU.add).then_inc(both_in, 1)
                dve.wait_ge(counted, 1)
                dve.tensor_copy(num[:, :], num_i[:, :])
                dve.tensor_copy(num_b[:, :], num_i[:, :])
                dve.wait_ge(sums_in, 1)
                for i in range(2):
                    dve.tensor_copy(half(own, i), halves(ps_own, i))
                    ins = dve.tensor_copy(half(upto[0], i), halves(ps_own, i))
                link(ins)
                n, d = 0, 1
                while d < NW:
                    a, b = upto[n % 2], upto[(n + 1) % 2]
                    dve.tensor_copy(b[:, 0:d, :], a[:, 0:d, :])
                    link(dve.tensor_tensor(b[:, d:NW, :], a[:, d:NW, :], a[:, 0:NW - d, :], ALU.add))
                    n, d = n + 1, 2 * d
                total = upto[n % 2]
                link(dve.tensor_scalar(tokens[:, :], total[:, NW - 1, :], float(P - 1), None, ALU.add))
                link(dve.tensor_copy(tok_i[:, :], tokens[:, :]))
                link(dve.tensor_scalar(tok_i[:, :], tok_i[:, :], 7, None, ALU.logical_shift_right))
                dve.tensor_copy(ends[0][:, :], tok_i[:, :])
                link(dve.tensor_copy(chunks[:, :], tok_i[:, :]))
                m, d = 0, 1
                while d < EX:
                    a, b = ends[m % 2], ends[(m + 1) % 2]
                    dve.tensor_copy(b[:, 0:d], a[:, 0:d])
                    link(dve.tensor_tensor(b[:, d:EX], a[:, d:EX], a[:, 0:EX - d], ALU.add))
                    m, d = m + 1, 2 * d
                end = ends[m % 2]
                dve.tensor_tensor(past[:, :, :], num[0:1, 0:NS].unsqueeze(2).to_broadcast([1, NS, EX - 1]),
                                  end[0:1, 0:EX - 1].unsqueeze(1).to_broadcast([1, NS, EX - 1]), ALU.is_ge)
                link(dve.tensor_tensor(base[:, :], end[:, :], chunks[:, :], ALU.subtract))
                dve.tensor_reduce(which[:, :], past[:, :, :], AX, ALU.add)
                link(dve.tensor_scalar(base[:, :], base[:, :], float(P), None, ALU.mult))
                dve.tensor_copy(K["expert_of"][:, :], which[:, :])
                link(dve.tensor_tensor(slot[:, :, :], total[:, :, :], own[:, :, :], ALU.subtract))
                for i in range(2):
                    ins = dve.tensor_tensor(half(slot, i), half(slot, i), halves(ps_pre, i), ALU.add)
                link(ins)
                link(dve.tensor_tensor(slot[:, :, :], slot[:, :, :],
                                       base[:, :].unsqueeze(1).to_broadcast([P, NW, EX]), ALU.add))
                for i in range(2):
                    link(dve.tensor_tensor(picked[:, :, :], slot[:, :, :], hots[i][:, :, :], ALU.mult))
                    link(dve.tensor_reduce(slot_f[:, :, i], picked[:, :, :], AX, ALU.add))
                link(dve.tensor_copy(slot_i[:, :, :], slot_f[:, :, :]))
                dve.tensor_scalar(chunk_i[:, :, :], slot_i[:, :, :], 7, None, ALU.logical_shift_right)
                link(dve.tensor_scalar(place_i[:, :, :], slot_i[:, :, :], P - 1, None, ALU.bitwise_and))
                dve.tensor_copy(chunk[:, :, :], chunk_i[:, :, :])
                link(dve.tensor_copy(place[:, :, :], place_i[:, :, :]))

                def marks(i, b):
                    w = RING * i + b
                    wait(dve, used, w - (RING - 1))
                    for n in range(2):
                        at = at1(place, w)[:, n:n + 1]
                        dve.tensor_scalar(hot[:, b, n, :], num_b[:, 0:P], at, None, ALU.is_equal)
                        ins = dve.tensor_scalar(hot_c[:, b, n, :], num_b[:, 0:NS], at1(chunk, w)[:, n:n + 1], None,
                                                ALU.is_equal)
                    ins.then_inc(matched, 1)
                pace(dve, NW, [(marks, 0)], RING)
                dve.wait_ge(token_in, 1)
                link(dve.tensor_copy(block_f[:, :], ps_w[:, 0:NS]))
                dve.tensor_scalar(gap[:, :], block_f[:, :], 0.0, None, ALU.is_equal)
                dve.tensor_scalar(second[:, :], block_f[:, :], float(NW), float(NW * P), ALU.is_gt, ALU.mult)
                dve.tensor_scalar(row_f[:, :], block_f[:, :], 1.0, float(P), ALU.subtract, ALU.mult)
                link(dve.tensor_scalar(gap_row[:, :], num[:, 0:NS], float(P), K["part"][:, 0:1], ALU.mult, ALU.add))
                dve.scalar_tensor_tensor(out=gap_row[:, :], in0=gap_row[:, :], scalar=float((2 * NW + 1) * P),
                                         in1=gap[:, :], op0=ALU.add, op1=ALU.mult)
                link(dve.tensor_tensor(row_f[:, :], row_f[:, :], ps_p[:, 0:NS], ALU.add))
                dve.tensor_tensor(token_f[:, :], row_f[:, :], second[:, :], ALU.subtract)
                link(dve.tensor_tensor(row_f[:, :], row_f[:, :], gap_row[:, :], ALU.add))
                link(dve.tensor_scalar(token_f[:, :], token_f[:, :], 0.0, float(NW * P - 1), ALU.max, ALU.min))
                dve.tensor_copy(K["token_of"][:, :], token_f[:, :])
                link(dve.tensor_scalar(row_f[:, :], row_f[:, :], 0.0, float((2 * NW + NS) * P - 1), ALU.max, ALU.min))
                dve.tensor_copy(K["row_of"][:, :], row_f[:, :])


def build_experts(nc, M, K, S, b1, W2, b2, xn_rows, y_rows):
    EX, HD, NS = S.EX, S.HD, S.NS
    HB = HD // P
    with ExitStack() as scope:
        T = Mem(nc, scope, "ffn_")
        up_all = K["up_all"]
        up_now = T.sb("up_now", [P, 2, 2 * HD + HB])
        w2 = T.sb("w2", [P, EX, HB, FEAT])
        b2b = T.sb("b2b", [P, EX, FEAT])
        b1r = T.sb("b1r", [EX * HB, P])
        idx = T.sb("idx", [P, RING], I32)
        row = T.sb("row", [P, RING], I32)
        xg = T.sb("xg", [P, RING, FEAT])
        xt = T.sb("xt", [P, 2, 2, P])
        h = T.sb("h", [P, 2, HB, P])
        y = T.sb("y", [P, RING, FEAT])
        ps_t = [T.ps(f"pt{i}") for i in range(2)]
        ps_h = [T.ps(f"ph{i}") for i in range(2)]
        ps_y = [T.ps(f"py{i}") for i in range(2)]
        names = "w2_in b1_in b1_turned b1_got staged begun turned fed up acted down rowed placed".split()
        (w2_in, b1_in, b1_turned, b1_got, staged, begun, turned, fed, up, acted, down,
         rowed, placed) = [M.sem("ffn_" + n) for n in names]
        gathered = [M.sem(f"ffn_gathered{j}") for j in range(RING)]
        stored = [M.sem(f"ffn_stored{j}") for j in range(RING)]

        with nc.Block() as block:
            @block.sync
            def _(sp):
                sp.dma_start(b1r[:, :], b1.rearrange("e (k p) -> (e k) p", p=P)).then_inc(b1_in, 16)
                for e in range(EX):
                    sp.dma_start(w2[:, e, :, :], W2[e].rearrange("(k p) f -> p k f", p=P)).then_inc(w2_in, 16)
                    sp.dma_start(b2b[:, e, :], b2[e:e + 1, :].to_broadcast([P, FEAT])).then_inc(w2_in, 16)

            @block.gpsimd
            def _(pool):
                def gather(i, c):
                    j, s = c % RING, RING * i + c
                    pool.wait_ge(staged, s + 1)
                    wait(pool, turned, s - (RING - 1))
                    pool.sem_inc(begun, 1)
                    pool.indirect_dma_start(xg[:, j, :], None, xn_rows,
                                            bass.IndirectOffsetOnAxis(ap=idx[:, j:j + 1], axis=0)
                                            ).then_inc(gathered[j], 16)

                def scatter(i, c):
                    j, s = c % RING, RING * i + c
                    pool.wait_ge(placed, s + 1)
                    pool.wait_ge(rowed, s + 1)
                    pool.sem_inc(begun, 1)
                    pool.indirect_dma_start(y_rows, bass.IndirectOffsetOnAxis(ap=row[:, j:j + 1], axis=0),
                                            y[:, j, :], None).then_inc(stored[j], 16)
                pace(pool, NS, [(gather, 3), (scatter, -1)], RING)
                for j in range(RING):
                    pool.wait_ge(stored[j], 16 * (NS // RING))

            @block.tensor
            def _(pe):
                regs = [pe.alloc_register(f"ffn_pe_e{j}") for j in range(RING)]
                pe.wait_ge(b1_in, 16)
                pe.transpose(ps_y[0][:, 0:EX * HB], b1r[:, :], K["ident"][0:EX * HB, 0:EX * HB]
                             ).then_inc(b1_turned, 1)

                def turn(i, c):
                    j, s, b = c % RING, RING * i + c, c % 2
                    pe.wait_ge(gathered[j], 16 * (i + c // RING + 1))
                    wait(pe, fed, s - 1)
                    for k in range(2):
                        mm = pe.transpose(ps_t[b][:, k * P:(k + 1) * P], xg[:, j, k * P:(k + 1) * P],
                                          K["ident"][:, :])
                    mm.then_inc(turned, 1)

                def upward(i, c):
                    s, b = RING * i + c, c % 2
                    pe.wait_ge(fed, s + 1)
                    wait(pe, acted, s - 1)
                    for k in range(HB):
                        for d in range(2):
                            mm = pe.matmul(ps_h[b][:, k * P:(k + 1) * P],
                                           up_now[:, b, d * HD + k * P:d * HD + (k + 1) * P], xt[:, b, d, :],
                                           start=(d == 0), stop=(d == 1))
                    mm.then_inc(up, 1)

                def downward(i, c):
                    s, b = RING * i + c, c % 2
                    if c % RING == 0:
                        pe.load(regs, K["expert_of"][0:1, bass.ds(s, RING)])
                    e = pe.snap(regs[c % RING], min_val=0, max_val=EX - 1)
                    if isinstance(s, int) and s == 0:
                        pe.wait_ge(w2_in, 32 * EX)
                    pe.wait_ge(acted, s + 1)
                    wait(pe, placed, s - 1)
                    for k in range(HB):
                        mm = pe.matmul(ps_y[b][:, 0:FEAT], h[:, b, k, :],
                                       w2[:, bass.ds(e, 1), k, :].squeeze(1), start=(k == 0), stop=(k == HB - 1))
                    mm.then_inc(down, 1)
                pace(pe, NS, [(turn, 2), (upward, 1), (downward, 0)], RING)

            @block.scalar
            def _(act):
                def stage(i, c):
                    j, s = c % RING, RING * i + c
                    wait(act, gathered[j], 16 * (i + c // RING))
                    act.copy(idx[:, j:j + 1], K["token_of"][:, one(s)]).then_inc(staged, 1)

                def gelus(i, c):
                    s, b = RING * i + c, c % 2
                    wait(act, down, s - 1)
                    act.wait_ge(up, s + 1)
                    for k in range(HB):
                        ins = act.activation(h[:, b, k, :], ps_h[b][:, k * P:(k + 1) * P], ACT.Gelu,
                                             bias=up_now[:, b, 2 * HD + k:2 * HD + k + 1])
                    ins.then_inc(acted, 1)
                def stage_row(i, c):
                    j, s = c % RING, RING * i + c
                    wait(act, stored[j], 16 * (i + c // RING))
                    act.copy(row[:, j:j + 1], K["row_of"][:, one(s)]).then_inc(rowed, 1)
                pace(act, NS, [(gelus, 0), (stage_row, 1), (stage, RING + 1)], RING)

            @block.vector
            def _(dve):
                up_regs = [dve.alloc_register(f"ffn_up_e{j}") for j in range(RING)]
                down_regs = [dve.alloc_register(f"ffn_down_e{j}") for j in range(RING)]
                dve.wait_ge(b1_turned, 1)
                dve.tensor_copy(up_all[:, :, 2 * HD:], ps_y[0][:, 0:EX * HB].rearrange("p (e k) -> p e k", k=HB)
                                ).then_inc(b1_got, 1)
                dve.wait_ge(b1_got, 1)

                def feed(i, c):
                    s, b = RING * i + c, c % 2
                    if c % RING == 0:
                        dve.load(up_regs, K["expert_of"][0:1, bass.ds(s, RING)])
                    e = dve.snap(up_regs[c % RING], min_val=0, max_val=EX - 1)
                    wait(dve, acted, s - 1)
                    dve.tensor_copy(up_now[:, b, :], up_all[:, bass.ds(e, 1), :].squeeze(1))
                    dve.wait_ge(turned, s + 1)
                    dve.tensor_copy(xt[:, b, :, :], ps_t[b][:, 0:2 * P].rearrange("p (k t) -> p k t", k=2)
                                    ).then_inc(fed, 1)

                def take(i, c):
                    j, s, b = c % RING, RING * i + c, c % 2
                    if c % RING == 0:
                        dve.load(down_regs, K["expert_of"][0:1, bass.ds(s, RING)])
                    e = dve.snap(down_regs[c % RING], min_val=0, max_val=EX - 1)
                    if isinstance(s, int) and s == 0:
                        dve.wait_ge(w2_in, 32 * EX)
                    dve.wait_ge(down, s + 1)
                    wait(dve, stored[j], 16 * (i + c // RING))
                    dve.tensor_tensor(y[:, j, :], ps_y[b][:, 0:FEAT], b2b[:, bass.ds(e, 1), :].squeeze(1),
                                      ALU.add).then_inc(placed, 1)
                pace(dve, NS, [(take, -1), (feed, 2)], RING)


def build_combine(nc, M, K, S, y_rows, out):
    N, NW, TAIL = S.N, S.NW, S.TAIL
    feat = K["feat"]
    names = "joined added stored".split()
    joined, added, stored = [M.sem("mix_" + n) for n in names]
    loaded = [M.sem(f"mix_loaded{j}") for j in range(RING)]
    with ExitStack() as scope:
        T = Mem(nc, scope, "mix_")
        rows = T.sb("rows", [P, RING, 2, 2, FEAT])

        with nc.Block() as block:
            @block.sync
            def _(sp):
                def load(i, c):
                    t = RING * i + c
                    wait(sp, added, 2 * (t - (RING - 1)))
                    for n in range(2):
                        sp.dma_start(rows[:, c, n, :, :], y_rows[bass.ds(n * NW * P + t * 2 * P, 2 * P), :].rearrange(
                            "(w p) f -> p w f", p=P)).then_inc(loaded[c], 16)
                pace(sp, NW // 2, [(load, 0)], RING)

            @block.vector
            def _(dve):
                def mix(i, c):
                    t = RING * i + c
                    dve.wait_ge(loaded[c], 32 * (i + 1))
                    for n, done in enumerate((joined, added)):
                        for j in range(2):
                            w = 2 * t + j
                            v = feat[:, one(w), 0:FEAT].squeeze(1)
                            if n:
                                dve.wait_ge(joined, w + 1)
                            dve.scalar_tensor_tensor(out=v, in0=rows[:, c, n, j, :],
                                                     scalar=K[f"weight{n + 1}"][:, one(w)], in1=v,
                                                     op0=ALU.mult, op1=ALU.add).then_inc(done, 1)
                pace(dve, NW // 2, [(mix, 0)], RING)

            @block.scalar
            def _(act):
                with act.Fori(0, NW // 2 - 1) as t:
                    act.wait_ge(added, 2 * t + 2)
                    act.dma_start(out[bass.ds(t * 2 * P, 2 * P), :].rearrange("(w p) f -> p w f", p=P),
                                  feat[:, bass.ds(t * 2, 2), 0:FEAT]).then_inc(stored, 16)
                act.wait_ge(added, NW)
                act.dma_start(out[(NW - 2) * P:(NW - 1) * P, :], feat[:, NW - 2, 0:FEAT]).then_inc(stored, 16)
                act.dma_start(out[(NW - 1) * P:N, :], feat[0:TAIL, NW - 1, 0:FEAT]).then_inc(stored, 16)
                act.wait_ge(stored, 16 * (NW // 2 + 1))


def build(nc, x, src, dst, gnn, ffn, out):
    W_gcn, b_gcn, g0, beta0, W1, a_src1, a_dst1, b1, g1, beta1, W2, a_src2, a_dst2, b2, g2, beta2 = gnn
    gamma, beta, Wr, br, F1, c1, F2, c2 = ffn
    S = Shapes(x.shape[0], src.shape[0], Wr.shape[1], F1.shape[2])
    xn_rows = nc.dram_tensor("xn_rows", (S.NW * P, FEAT), F32).ap()
    y_rows = nc.dram_tensor("y_rows", ((2 * S.NW + S.NS) * P, FEAT), F32).ap()
    with ExitStack() as ctx:
        M, K = Mem(nc, ctx), {}
        build_gnn(nc, M, K, S, x, src, dst, W_gcn, (b_gcn, g0, beta0),
                  [(W1, a_src1, a_dst1, b1, g1, beta1), (W2, a_src2, a_dst2, b2, g2, beta2)])
        K["token_of"] = M.sb("token_of", [P, S.NS], I32)
        K["row_of"] = M.sb("row_of", [P, S.NS], I32)
        K["expert_of"] = M.sb("expert_of", [1, S.NS], I32)
        for n in (1, 2):
            K[f"weight{n}"] = M.sb(f"weight{n}", [P, S.NW])
        assert S.EX <= WIDE - FEAT
        K["logits"] = K["feat"][:, 0:S.NW, FEAT:FEAT + S.EX]
        build_ffn_input(nc, M, K, S, x, gamma, beta, Wr, br, xn_rows)
        K["up_all"] = M.sb("up_all", [P, S.EX, 2 * S.HD + S.HD // P])
        build_routing(nc, M, K, S, F1)
        build_experts(nc, M, K, S, c1, F2, c2, xn_rows, y_rows)
        build_combine(nc, M, K, S, y_rows, out)


_GNN = ["W_gcn", "b_gcn", "g0", "beta0", "W1", "a_src1", "a_dst1", "b1", "g1", "beta1", "W2", "a_src2", "a_dst2",
        "b2", "g2", "beta2"]
_FFN = ["gamma", "beta", "Wr", "br", "W1", "b1", "W2", "b2"]
_INS = ["x", "src", "dst"] + ["L0_gnn_" + n for n in _GNN] + ["L0_ffn_" + n for n in _FFN]


def kernel(**inputs):
    import numpy as _np
    import concourse.bacc as _bacc
    from concourse import mybir as _mybir
    from concourse.bass_utils import run_bass_kernel_spmd as _run

    nc = _bacc.Bacc("TRN2", target_bir_lowering=False, num_devices=1)
    arrays, args = {}, []
    for name in _INS:
        a = _np.ascontiguousarray(inputs[name])
        arrays[f"in_{name}_dram"] = a
        args.append(nc.dram_tensor(f"in_{name}_dram", a.shape, _mybir.dt.from_np(a.dtype),
                                   kind="ExternalInput").ap())
    shape = inputs["x"].shape
    out = nc.dram_tensor("out_0_dram", tuple(shape), _mybir.dt.float32, kind="ExternalOutput").ap()
    n = 3 + len(_GNN)
    build(nc, *args[:3], args[3:n], args[n:], out)
    r = _run(nc, [arrays], core_ids=[0])
    return r.results[0]["out_0_dram"]
```
